# Optimizing a Trainium2 kernel written in Bass

```python
import numpy as np
import jax
import jax.numpy as jnp

def _softmax(x, axis=-1):
    return jax.nn.softmax(x, axis=axis)

def _gelu(x):
    return jax.nn.gelu(x, approximate=True)

def _silu(x):
    return jax.nn.silu(x)

def _sigmoid(x):
    return jax.nn.sigmoid(x)

def _layernorm(x, axis=-1, eps=1e-05):
    m = jnp.mean(x, axis=axis, keepdims=True)
    v = jnp.var(x, axis=axis, keepdims=True)
    return (x - m) / jnp.sqrt(v + eps)

def _scatter_add(tgt, idx, src, axis=0):
    return tgt.at[idx].add(src)

def _segment_sum(src, seg, n):
    return jax.ops.segment_sum(src, seg, n)
kernel_name = 'mk_xattn_ffn_d1_seqx_r4_71cc5c'

def setup_inputs(seed: int=0):
    np.random.seed(seed)
    _w = jnp.asarray

    def _rec_inputs():
        import jax
        import jax.numpy as jnp
        _rk = jax.random.key(seed)
        x = 7.22e-05 + 1 * jax.random.normal(jax.random.fold_in(_rk, 1), (4, 1024, 256), jnp.float32)
        _lenS = 1024 - jax.random.randint(jax.random.fold_in(_rk, 7), (4,), 0, max(1, 1024 // 4) + 1, jnp.int32)
        _lenS2 = 64 - jax.random.randint(jax.random.fold_in(_rk, 8), (4,), 0, max(1, 64 // 4) + 1, jnp.int32)
        _ctx_768P = jax.random.normal(jax.random.fold_in(_rk, 11), (4, 16, 192), jnp.float32)
        _ctx_768c = jax.random.dirichlet(jax.random.fold_in(_rk, 511), 0.3 * jnp.ones((16,), jnp.float32), (4, 64))
        _ctx_768t = jnp.einsum('bsk,bkd->bsd', _ctx_768c, _ctx_768P)
        _ctx_768t = _ctx_768t * jax.lax.rsqrt(jnp.mean(jnp.square(_ctx_768t)) + 1e-12) * 0.953939
        ctx_768 = 2.09791e-05 + 1.00001 * (_ctx_768t + 0.3 * jax.random.normal(jax.random.fold_in(_rk, 611), (4, 64, 192), jnp.float32))
        return (x, ctx_768)
    x, ctx_768 = _rec_inputs()

    def _L0_xattn_setup():
        import jax, jax.numpy as jnp
        import numpy as np
        HEADS = 16
        DIM_HEAD = 64
        key = jax.random.key(seed)
        ks = jax.random.split(key, 7)
        B, Nq, Dq = (4, 512, 256)
        Nk, Dc = (256, 192)
        inner = HEADS * DIM_HEAD
        sq = 1.0 / np.sqrt(Dq)
        sc = 1.0 / np.sqrt(Dc)
        si = 1.0 / np.sqrt(inner)
        return {'x': jax.random.normal(ks[0], (B, Nq, Dq), dtype=jnp.float32), 'context': jax.random.normal(ks[1], (B, Nk, Dc), dtype=jnp.float32), 'Wq': jax.random.normal(ks[2], (Dq, inner), dtype=jnp.float32) * sq, 'Wk': jax.random.normal(ks[3], (Dc, inner), dtype=jnp.float32) * sc, 'Wv': jax.random.normal(ks[4], (Dc, inner), dtype=jnp.float32) * sc, 'Wo': jax.random.normal(ks[5], (inner, Dq), dtype=jnp.float32) * si, 'bo': jax.random.normal(ks[6], (Dq,), dtype=jnp.float32) * 0.01}
    _L0_xattn_all = _L0_xattn_setup()
    _L0_xattn_in = {k: v for k, v in _L0_xattn_all.items() if k in ('Wq', 'Wk', 'Wv', 'Wo', 'bo')}
    del _L0_xattn_all

    def _L0_ffn_setup():
        import jax, jax.numpy as jnp
        import numpy as np
        from jax import lax
        D = 256
        H = 352
        E = 8
        K = 2
        ROUTER_SCALE = 1.0

        def _expert(x, w1, b1, w3, b3, w2, b2):
            h = jax.nn.silu((x @ w1 + b1) * (x @ w3 + b3))
            return h @ w2 + b2
        key = jax.random.key(seed)
        ks = jax.random.split(key, 16)
        s = 0.02
        inp = {'x': jax.random.normal(ks[0], (2, 512, D), dtype=jnp.float32), 'gate_w': jax.random.normal(ks[1], (E, D), dtype=jnp.float32) * s, 'gate_b': jax.random.normal(ks[2], (E,), dtype=jnp.float32) * s, 'w1': jax.random.normal(ks[3], (E, D, H), dtype=jnp.float32) * s, 'b1': jax.random.normal(ks[4], (E, H), dtype=jnp.float32) * s, 'w3': jax.random.normal(ks[5], (E, D, H), dtype=jnp.float32) * s, 'b3': jax.random.normal(ks[6], (E, H), dtype=jnp.float32) * s, 'w2': jax.random.normal(ks[7], (E, H, D), dtype=jnp.float32) * s, 'b2': jax.random.normal(ks[8], (E, D), dtype=jnp.float32) * s, 'sw1': jax.random.normal(ks[9], (D, H), dtype=jnp.float32) * s, 'sb1': jax.random.normal(ks[10], (H,), dtype=jnp.float32) * s, 'sw3': jax.random.normal(ks[11], (D, H), dtype=jnp.float32) * s, 'sb3': jax.random.normal(ks[12], (H,), dtype=jnp.float32) * s, 'sw2': jax.random.normal(ks[13], (H, D), dtype=jnp.float32) * s, 'sb2': jax.random.normal(ks[14], (D,), dtype=jnp.float32) * s}
        return inp
    _L0_ffn_all = _L0_ffn_setup()
    _L0_ffn_in = {k: v for k, v in _L0_ffn_all.items() if k in ('gate_w', 'gate_b', 'w1', 'b1', 'w3', 'b3', 'w2', 'b2', 'sw1', 'sb1', 'sw3', 'sb3', 'sw2', 'sb2')}
    del _L0_ffn_all
    return {'x': x, 'ctx_768': ctx_768, 'L0_xattn_Wq': _L0_xattn_in['Wq'], 'L0_xattn_Wk': _L0_xattn_in['Wk'], 'L0_xattn_Wv': _L0_xattn_in['Wv'], 'L0_xattn_Wo': _L0_xattn_in['Wo'], 'L0_xattn_bo': _L0_xattn_in['bo'], 'L0_ffn_gate_w': _L0_ffn_in['gate_w'], 'L0_ffn_gate_b': _L0_ffn_in['gate_b'], 'L0_ffn_w1': _L0_ffn_in['w1'], 'L0_ffn_b1': _L0_ffn_in['b1'], 'L0_ffn_w3': _L0_ffn_in['w3'], 'L0_ffn_b3': _L0_ffn_in['b3'], 'L0_ffn_w2': _L0_ffn_in['w2'], 'L0_ffn_b2': _L0_ffn_in['b2'], 'L0_ffn_sw1': _L0_ffn_in['sw1'], 'L0_ffn_sb1': _L0_ffn_in['sb1'], 'L0_ffn_sw3': _L0_ffn_in['sw3'], 'L0_ffn_sb3': _L0_ffn_in['sb3'], 'L0_ffn_sw2': _L0_ffn_in['sw2'], 'L0_ffn_sb2': _L0_ffn_in['sb2']}

def reference(x, ctx_768, L0_xattn_Wq, L0_xattn_Wk, L0_xattn_Wv, L0_xattn_Wo, L0_xattn_bo, L0_ffn_gate_w, L0_ffn_gate_b, L0_ffn_w1, L0_ffn_b1, L0_ffn_w3, L0_ffn_b3, L0_ffn_w2, L0_ffn_b2, L0_ffn_sw1, L0_ffn_sb1, L0_ffn_sw3, L0_ffn_sb3, L0_ffn_sw2, L0_ffn_sb2):
    import jax
    import jax.numpy as jnp

    def _L0_xattn_ref(x, context, Wq, Wk, Wv, Wo, bo):
        import jax, jax.numpy as jnp
        import numpy as np
        HEADS = 16
        DIM_HEAD = 64
        B, Nq, _ = x.shape
        Nk = context.shape[1]
        h, dh = (HEADS, DIM_HEAD)
        q = (x @ Wq).reshape(B, Nq, h, dh)
        k = (context @ Wk).reshape(B, Nk, h, dh)
        v = (context @ Wv).reshape(B, Nk, h, dh)
        scale = 1.0 / jnp.sqrt(jnp.asarray(dh, dtype=x.dtype))
        scores = jnp.einsum('bqhd,bkhd->bhqk', q, k) * scale
        attn = jax.nn.softmax(scores, axis=-1)
        out = jnp.einsum('bhqk,bkhd->bqhd', attn, v).reshape(B, Nq, h * dh)
        return out @ Wo + bo

    def _L0_ffn_ref(x, gate_w, gate_b, w1, b1, w3, b3, w2, b2, sw1, sb1, sw3, sb3, sw2, sb2):
        import jax, jax.numpy as jnp
        import numpy as np
        from jax import lax
        D = 256
        H = 352
        E = 8
        K = 2
        ROUTER_SCALE = 1.0

        def _expert(x, w1, b1, w3, b3, w2, b2):
            h = jax.nn.silu((x @ w1 + b1) * (x @ w3 + b3))
            return h @ w2 + b2
        shape = x.shape
        xf = x.reshape(-1, D)
        T = xf.shape[0]
        scores = jax.nn.softmax(xf @ gate_w.T, axis=-1)
        biased = scores + gate_b
        _, idx = lax.top_k(biased, K)
        w = jnp.take_along_axis(scores, idx, axis=-1) * ROUTER_SCALE
        rw = jnp.zeros((T, E), dtype=xf.dtype).at[jnp.arange(T)[:, None], idx].add(w)
        h = jax.nn.silu((jnp.einsum('td,edh->teh', xf, w1) + b1) * (jnp.einsum('td,edh->teh', xf, w3) + b3))
        oe = jnp.einsum('teh,ehd->ted', h, w2) + b2
        y = jnp.einsum('te,ted->td', rw, oe)
        z = _expert(xf, sw1, sb1, sw3, sb3, sw2, sb2)
        return (y + z).reshape(shape)
    x = x + _L0_xattn_ref(_layernorm(x, axis=-1), ctx_768, L0_xattn_Wq, L0_xattn_Wk, L0_xattn_Wv, L0_xattn_Wo, L0_xattn_bo)
    x = x + _L0_ffn_ref(_layernorm(x, axis=-1), L0_ffn_gate_w, L0_ffn_gate_b, L0_ffn_w1, L0_ffn_b1, L0_ffn_w3, L0_ffn_b3, L0_ffn_w2, L0_ffn_b2, L0_ffn_sw1, L0_ffn_sb1, L0_ffn_sw3, L0_ffn_sb3, L0_ffn_sw2, L0_ffn_sb2)
    return x

_drawn_inputs = setup_inputs


def setup_inputs(seed=0):
    import zlib

    import numpy as np

    out = dict(_drawn_inputs(seed))
    spreads = {}
    factors = {'L0_xattn_bo': 6.21,
     'L0_ffn_gate_w': 8.0,
     'L0_ffn_gate_b': 8.0,
     'L0_ffn_w1': 8.0,
     'L0_ffn_b1': 8.0,
     'L0_ffn_w3': 8.0,
     'L0_ffn_b3': 8.0,
     'L0_ffn_w2': 8.0,
     'L0_ffn_b2': 40.155,
     'L0_ffn_sw1': 3.321,
     'L0_ffn_sb1': 32.212,
     'L0_ffn_sw3': 3.29,
     'L0_ffn_sb3': 33.647,
     'L0_ffn_sw2': 3.319,
     'L0_ffn_sb2': 26.664}
    for name, (base, spread) in spreads.items():
        noise = np.random.default_rng([zlib.crc32(name.encode()), seed]).standard_normal(out[name].shape)
        drawn = base * np.exp(spread * noise) if base else spread * noise
        out[name] = jnp.asarray(drawn.astype(out[name].dtype))
    for name, factor in factors.items():
        out[name] = (out[name] * factor).astype(out[name].dtype)
    return out
```

```python
from contextlib import ExitStack

import concourse.bass as bass
from concourse import mybir

F32 = mybir.dt.float32
F32R = mybir.dt.float32r
BF16 = mybir.dt.bfloat16
I32 = mybir.dt.int32
ALU = mybir.AluOpType
ACT = mybir.ActivationFunctionType
AX = mybir.AxisListType

P = 128
BANK = 512
LN_EPS = 1e-5
LOWEST = -3.0e38


def wait(eng, sem, n):
    if not isinstance(n, int) or n > 0:
        eng.wait_ge(sem, n)


def xattn_moe(nc, x, ctx, Wq, Wk, Wv, Wo, bo, gate_w, gate_b, w1, b1, w3, b3, w2, b2,
              sw1, sb1, sw3, sb3, sw2, sb2, out):
    B, N, D = x.shape
    _, NK, DC = ctx.shape
    INNER = Wq.shape[1]
    DH = 64
    HEADS = INNER // DH
    E, _, H = w1.shape
    TOP = 2
    T = B * N
    NT = T // P
    TPB = N // P
    KD = D // P
    HK = HEADS * NK
    NJ = INNER // P
    BK = B * NK
    KC = [(0, P), (P, DC - P)]
    SCALE = DH ** -0.5
    HS = 8
    H3 = 3 * P
    KH = H3 // P
    HR = H - (KH - 1) * P
    NU = TOP * NT + E - 1
    PADS = P
    assert HK == 2 * BANK and BK == 2 * P and D == 2 * P and NK == 64 and HR < P

    x_rows = x.rearrange("b n d -> (b n) d")
    out_rows = out.rearrange("b n d -> (b n) d")
    xn2_dram = nc.dram_tensor("xn2_scratch", [T + PADS, D], F32, kind="Internal").ap()
    x2_dram = nc.dram_tensor("x2_scratch", [T, D], F32, kind="Internal").ap()
    acc_dram = nc.dram_tensor("acc_scratch", [T + PADS, D], F32, kind="Internal").ap()
    slots_dram = nc.dram_tensor("slots_scratch", [P * NU, 2], I32, kind="Internal").ap()

    stack = ExitStack()
    with stack:
        def sb(name, shape, dt, on=stack):
            return on.enter_context(nc.sbuf_tensor(name, shape, dt))

        def sem(name):
            return stack.enter_context(nc.semaphore(name))

        ident = sb("ident", [P, P], F32)
        gateT = sb("gateT", [P, KD, E], F32)
        gateb_bc = sb("gateb_bc", [P, E], F32)
        minus_half = sb("minus_half", [P, 1], F32)
        eps = sb("eps", [P, 1], F32)
        record = sb("record", [P, NT, TOP, 2], I32)
        slot = sb("slot", [P, TOP, NT], I32)
        slot_col = sb("slot_col", [P, TOP, NT], I32)
        slot_row = sb("slot_row", [P, TOP, NT], I32)
        expert_of = sb("expert_of", [P, NU], I32)
        step_experts = sb("step_experts", [P, NU + 4], I32)
        slots = sb("slots", [P, NU, 2], I32)
        idx_in = sb("idx_in", [P, 2, 1], I32)
        idx_out = sb("idx_out", [P, 2, 1], I32)
        ws13h = sb("ws13h", [P, KD, 2 * H], F32R)
        ws2h = sb("ws2h", [P, KH, D], F32R)
        raw = ExitStack()
        ws13 = sb("ws13", [P, KD, 2 * H], F32, raw)
        ws2 = sb("ws2", [P, KH, D], F32, raw)
        raw.close()
        ws13l = sb("ws13l", [P, KD, 2 * H], F32R)
        ws2l = sb("ws2l", [P, KH, D], F32R)
        bs13 = sb("bs13", [P, 2 * H], F32)

        att = ExitStack()
        Ah = sb("Ah", [P, B, KD, HK], F32R, att)
        Al = sb("Al", [P, B, KD, HK], F32R, att)
        Uh = sb("Uh", [P, B, NJ, D], F32R, att)
        Ul = sb("Ul", [P, B, NJ, D], F32R, att)
        bo_bc = sb("bo_bc", [P, D], F32, att)
        pre = ExitStack()
        wq_sb = sb("wq_sb", [P, KD, INNER], F32, pre)
        wk_sb = sb("wk_sb", [P, 2, INNER], F32, pre)
        wv_sb = sb("wv_sb", [P, 2, INNER], F32, pre)
        wo_sb = sb("wo_sb", [P, NJ, D], F32, pre)
        ctx_sb = sb("ctx_sb", [P, 2, DC], F32, pre)
        ctxT = sb("ctxT", [P, 2, BK], F32, pre)
        wqT = sb("wqT", [P, 2, D], F32, pre)
        kT = sb("kT", [P, 2, BK], F32, pre)
        vT = sb("vT", [P, 2, B, 2, NK], F32, pre)
        pre.close()
        xin = sb("xin", [P, 2, D], F32, att)
        xres = sb("xres", [P, 2, D], F32, att)
        xn = sb("xn", [P, 2, D], F32, att)
        xTh = sb("xTh", [P, 2, D], F32R, att)
        xTl = sb("xTl", [P, 2, D], F32R, att)
        prob = sb("prob", [P, 2, HK], F32, att)
        pTh = sb("pTh", [P, 2, HK], F32R, att)
        pTl = sb("pTl", [P, 2, HK], F32R, att)
        x2 = sb("x2", [P, 2, D], F32, att)
        xn2 = sb("xn2", [P, 2, D], F32, att)
        xn2T = sb("xn2T", [P, 2, D], F32, att)
        st1 = sb("st1", [P, 2, 6], F32, att)
        mv1 = sb("mv1", [P, 2, 2], F32, att)
        rs1 = sb("rs1", [P, 2, 2], F32, att)
        nm1 = sb("nm1", [P, 2, 1], F32, att)
        st2 = sb("st2", [P, 2, 6], F32, att)
        mv2 = sb("mv2", [P, 2, 2], F32, att)
        rs2 = sb("rs2", [P, 2, 2], F32, att)
        nm2 = sb("nm2", [P, 2, 1], F32, att)
        hmax = sb("hmax", [P, 2, HEADS], F32, att)
        hsum = sb("hsum", [P, 2, HEADS], F32, att)
        nmax = sb("nmax", [P, 2, HEADS - HS], F32, att)
        hinv = sb("hinv", [P, 2, HEADS], F32, att)
        att.close()

        w13h = sb("w13h", [P, E, KD, 2 * H], F32R)
        w2h = sb("w2h", [P, E, KH, D], F32R)
        raw = ExitStack()
        w2_raw = sb("w2_raw", [P, E, KH, D], F32, raw)
        w13_raw = sb("w13_raw", [P, E, KD, 2 * H], F32, raw)
        raw.close()
        w2l = sb("w2l", [P, E, KH, D], F32R)
        math = ExitStack()
        sb("below_math", [P, E * KD * 2 * H - 3072 - 512], F32, math)
        mA = sb("mA", [P, NT, E], F32, math)
        score = sb("score", [P, NT, E], F32, math)
        biased = sb("biased", [P, NT, E], F32, math)
        mB = sb("mB", [P, NT, E], F32, math)
        first = sb("first", [P, NT, E], F32, math)
        second = sb("second", [P, NT, E], F32, math)
        chosen = sb("chosen", [P, NT, E], BF16, math)
        slot8 = sb("slot8", [P, NT, E], F32, math)
        big = sb("big", [P, NU, E], F32, math)
        v32 = sb("v32", [P, 8, NT], F32, math)
        math.close()
        w13l = sb("w13l", [P, E, KD, 2 * H], F32R)
        b13 = sb("b13", [P, E, 2 * H], F32)
        xrow = sb("xrow", [P, 2, D], F32)
        x2row = sb("x2row", [P, D], F32)
        uxTh = sb("uxTh", [P, 2, D], F32R)
        uxTl = sb("uxTl", [P, 2, D], F32R)
        hid = sb("hid", [P, 2, H3], F32)
        hTh = sb("hTh", [P, H3], F32R)
        hTl = sb("hTl", [P, H3], F32R)
        yrow = sb("yrow", [P, 2, D], F32)
        early = ExitStack()
        logits = sb("logits", [P, NT, E], F32, early)
        tri = sb("tri", [P, P], BF16, early)
        ones = sb("ones", [P, P], BF16, early)
        pref = sb("pref", [P, E], F32, early)
        upto = sb("upto", [P, E, E], F32, early)
        tile128 = sb("tile128", [P, NT], F32, early)
        unit_no = sb("unit_no", [P, NU], F32, early)
        early.close()
        uv = sb("uv", [P, 2, H], F32)

        ps = stack.enter_context(nc.psum_tensor("ps", [P, 8, BANK], F32))

        def f32(ap):
            return ap.bitcast(F32)

        def sems(name):
            return [sem(name + "_even"), sem(name + "_odd")]

        def before(t):
            return 16 * (t // 2)

        w_in = sem("w_in")
        wv_in = sem("wv_in")
        small_in = sem("small_in")
        sw_in = sem("sw_in")
        id_ok = sem("id_ok")
        raw2_zero = sem("raw2_zero")
        vT_zero = sem("vT_zero")
        hid_one = sem("hid_one")
        pad2_zero = sem("pad2_zero")
        const_ok = sem("const_ok")
        table_out = sem("table_out")
        pads_out = sem("pads_out")
        pre_pe = sem("pre_pe")
        pre_act = sem("pre_act")
        pre_dve = sem("pre_dve")
        sw_hi = sem("sw_hi")
        sw_lo = sem("sw_lo")
        x_in = sems("x_in")
        xres_in = sems("xres_in")
        st1_ok = sem("st1_ok")
        mv1_ok = sem("mv1_ok")
        eps1_ok = sem("eps1_ok")
        rstd1_ok = sem("rstd1_ok")
        nm1_ok = sem("nm1_ok")
        xn_ok = sem("xn_ok")
        T_ok = sem("T_ok")
        xTh_ok = sem("xTh_ok")
        xTl_ok = sem("xTl_ok")
        S_ok = sem("S_ok")
        max_ok = sem("max_ok")
        nmax_ok = sem("nmax_ok")
        sub_ok = sem("sub_ok")
        exp_ok = sem("exp_ok")
        sum_ok = sem("sum_ok")
        inv_ok = sem("inv_ok")
        norm_ok = sem("norm_ok")
        PT_ok = sem("PT_ok")
        pTh_ok = sem("pTh_ok")
        pTl_ok = sem("pTl_ok")
        O_ok = sem("O_ok")
        xb_ok = sem("xb_ok")
        x2_ok = sem("x2_ok")
        x2_out = sems("x2_out")
        st2_ok = sem("st2_ok")
        mv2_ok = sem("mv2_ok")
        eps2_ok = sem("eps2_ok")
        rstd2_ok = sem("rstd2_ok")
        nm2_ok = sem("nm2_ok")
        xn2_ok = sem("xn2_ok")
        xn2_out = sems("xn2_out")
        T2_ok = sem("T2_ok")
        xn2T_ok = sem("xn2T_ok")
        R_ok = sem("R_ok")
        lg_ok = sem("lg_ok")
        rt = sem("rt")
        rt_sub = sem("rt_sub")
        rt_exp = sem("rt_exp")
        chosen_ok = sem("chosen_ok")
        rank_ok = sem("rank_ok")
        slot_ok = sem("slot_ok")
        eid_ok = sem("eid_ok")
        scat_out = sem("scat_out")
        slots_in = sem("slots_in")
        idx_in_ok = sem("idx_in_ok")
        idx_out_ok = sem("idx_out_ok")
        done = sem("done")
        waited_dve = sem("waited_dve")
        waited_pool = sem("waited_pool")
        raw_in = sem("raw_in")
        w_hi = sem("w_hi")
        w_lo = sem("w_lo")
        b13_in = sem("b13_in")

        class Unit:
            def __init__(self, name):
                self.row_in = sems(name + "_row_in")
                self.X_ok = sem(name + "_X_ok")
                self.xTh_ok = sem(name + "_xTh_ok")
                self.xTl_ok = sem(name + "_xTl_ok")
                self.UV_ok = sem(name + "_UV_ok")
                self.bias_ok = sem(name + "_bias_ok")
                self.z_ok = sem(name + "_z_ok")
                self.h_ok = sem(name + "_h_ok")
                self.H_ok = sem(name + "_H_ok")
                self.hTh_ok = sem(name + "_hTh_ok")
                self.hTl_ok = sem(name + "_hTl_ok")
                self.Y_ok = sem(name + "_Y_ok")
                self.y_ok = sem(name + "_y_ok")
                self.y_out = sems(name + "_y_out")
                self.x2_in = sem(name + "_x2_in")

        sh = Unit("shared")
        ro = Unit("routed")

        def steps(eng, n, lead, lag, body, extra=0, skip=0):
            s0 = (lag + 2) // 2 * 2
            s1 = s0 + (n - lead - s0) // 2 * 2
            for s in range(-lead, s0):
                body(s, s % 2, None)
            if skip:
                with eng.Fori(s0 // 2, s0 // 2 + skip) as k:
                    body(2 * k, 0, None)
                    body(2 * k + 1, 1, None)
            if extra:
                with eng.Fori(0, extra) as k:
                    body(2 * k + (s0 + 2 * skip), 0, None)
                    body(2 * k + (s0 + 2 * skip + 1), 1, k)
            with eng.Fori(s0 // 2 + skip + extra, s1 // 2) as k:
                body(2 * k, 0, None)
                body(2 * k + 1, 1, None)
            for s in range(s1, n + lag):
                body(s, s % 2, None)

        def has(t, n):
            return not isinstance(t, int) or 0 <= t < n

        NA = 2 + 4 * NJ
        NPRE = NA + 3 * NJ

        def chunk_a(j, i):
            return 2 + 4 * j + i

        def chunk_u(j, i):
            return NA + 3 * j + i

        def split_chunks(c):
            n = 0
            for k in range(c):
                n += (k >= 2 and (k - 2) % 4 >= 2) if k < NA else (k - NA) % 3 >= 1
            return n

        def s_bank(p):
            return (1, 6)[p]

        PRE_SPLITS = split_chunks(NPRE)

        block = stack.enter_context(nc.Block())

        @block.sync
        def _(sp):
            sp.dma_start(ctx_sb[:, :, :], ctx.rearrange("b s c -> (b s) c").rearrange("(r p) c -> p r c", p=P)).then_inc(w_in, 16)
            sp.dma_start(wq_sb[:, :, :], Wq.rearrange("(k p) n -> p k n", p=P)).then_inc(w_in, 16)
            for i, (lo, n) in enumerate(KC):
                sp.dma_start(wk_sb[0:n, i, :], Wk[lo:lo + n, :]).then_inc(w_in, 16)
            for i, (lo, n) in enumerate(KC):
                sp.dma_start(wv_sb[0:n, i, :], Wv[lo:lo + n, :]).then_inc(wv_in, 16)
            sp.dma_start(wo_sb[:, :, :], Wo.rearrange("(j p) d -> p j d", p=P)).then_inc(wv_in, 16)
            sp.dma_start(ws13[:, :, 0:H], sw1.rearrange("(k p) h -> p k h", p=P)).then_inc(sw_in, 16)
            sp.dma_start(ws13[:, :, H:2 * H], sw3.rearrange("(k p) h -> p k h", p=P)).then_inc(sw_in, 16)
            sp.wait_ge(raw2_zero, 1)
            sp.dma_start(ws2[:, 0:KH - 1, :], sw2[0:(KH - 1) * P, :].rearrange("(c p) d -> p c d", p=P)).then_inc(sw_in, 16)
            sp.dma_start(ws2[0:HR, KH - 1, :], sw2[(KH - 1) * P:H, :]).then_inc(sw_in, 16)
            sp.dma_start(ws2[HR:HR + 1, KH - 1, :], sb2.rearrange("(a d) -> a d", a=1)).then_inc(sw_in, 16)
            sp.wait_ge(pre_pe, NPRE)
            sp.wait_ge(pre_act, NPRE)

            def tile_step(s, par, _):
                t = s + 3
                if has(t, NT):
                    wait(sp, xn_ok, t - 1)
                    sp.dma_start(xin[:, (par + 1) % 2, :], x_rows[bass.ts(t, P), :]).then_inc(x_in[(par + 1) % 2], 16)
                t = s - 5
                if has(t, NT):
                    wait(sp, xn2_ok, t + 1)
                    sp.dma_start(xn2_dram[bass.ts(t, P), :], xn2[:, (par + 1) % 2, :]).then_inc(xn2_out[(par + 1) % 2], 16)
                t = s - 4
                if has(t, NT):
                    wait(sp, x2_ok, t + 1)
                    sp.dma_start(x2_dram[bass.ts(t, P), :], x2[:, par, :]).then_inc(x2_out[par], 16)
                t = s - 2
                if has(t, NT):
                    wait(sp, x2_ok, t - 1)
                    sp.dma_start(xres[:, par, :], x_rows[bass.ts(t, P), :]).then_inc(xres_in[par], 16)

            steps(sp, NT, 3, 5, tile_step)

            for half in xn2_out + x2_out:
                sp.wait_ge(half, before(NT))
            sp.wait_ge(O_ok, NT)
            sp.wait_ge(lg_ok, NT)
            sp.wait_ge(x2_ok, NT)
            sp.dma_start(b13[:, :, 0:H], b1.rearrange("(a e) h -> a e h", a=1).to_broadcast([P, E, H])).then_inc(b13_in, 16)
            sp.dma_start(b13[:, :, H:2 * H], b3.rearrange("(a e) h -> a e h", a=1).to_broadcast([P, E, H])).then_inc(b13_in, 16)

            def shared_step(s, par, e):
                t = s + 2
                if has(t, NT):
                    wait(sp, sh.X_ok, t - 1)
                    sp.dma_start(xrow[:, par, :], xn2_dram[bass.ts(t, P), :]).then_inc(sh.row_in[par], 16)
                t = s - 4
                if has(t, NT):
                    wait(sp, sh.y_ok, t + 1)
                    sp.dma_start(acc_dram[bass.ts(t, P), :], yrow[:, par, :]).then_inc(sh.y_out[par], 16)
                t = s - 3
                if has(t, NT):
                    wait(sp, sh.y_ok, t)
                    sp.dma_start(x2row[:, :], x2_dram[bass.ts(t, P), :]).then_inc(sh.x2_in, 16)
                if e is not None:
                    one = bass.ds(e, 1)
                    sp.dma_start(w13_raw[:, one, :, 0:H], w1[one, :, :].rearrange("e (k p) h -> p e k h", p=P)).then_inc(raw_in, 16)
                    sp.dma_start(w13_raw[:, one, :, H:2 * H], w3[one, :, :].rearrange("e (k p) h -> p e k h", p=P)).then_inc(raw_in, 16)
                    sp.dma_start(w2_raw[:, one, 0:KH - 1, :], w2[one, 0:(KH - 1) * P, :].rearrange("e (c p) d -> p e c d", p=P)).then_inc(raw_in, 16)
                    sp.dma_start(w2_raw[0:HR, one, KH - 1, :], w2[one, (KH - 1) * P:H, :].rearrange("e p d -> p e d")).then_inc(raw_in, 16)
                    sp.dma_start(w2_raw[HR:HR + 1, one, KH - 1, :], b2[one, :].rearrange("e (a d) -> a e d", a=1)).then_inc(raw_in, 16)

            sp.wait_ge(eid_ok, 1)
            sp.wait_ge(pad2_zero, 1)
            steps(sp, NT, 2, 4, shared_step, extra=E)

            sp.wait_ge(scat_out, 16 * TOP * NT)
            sp.dma_start(slots[:, :, :], slots_dram.rearrange("(p n) c -> p n c", p=P)).then_inc(slots_in, 16)
            sp.wait_ge(ro.y_out[0], before(NU + 1))
            sp.wait_ge(ro.y_out[1], before(NU))
            sp.dma_start(out_rows.rearrange("(p n) d -> p (n d)", p=P), acc_dram[0:T, :].rearrange("(p n) d -> p (n d)", p=P)).then_inc(done, 16)
            sp.wait_ge(done, 16)

        @block.gpsimd
        def _(pool):
            pool.memset(ident[:, :], 0.0).then_inc(id_ok, 1)
            pool.wait_ge(id_ok, 1)
            pool.affine_select(out=ident[:, :], in_=ident[:, :], compare_op=ALU.not_equal, fill=1.0, base=0,
                               pattern=[[-1, P]], channel_multiplier=1).then_inc(id_ok, 1)
            pool.memset(ws2[:, KH - 1, :], 0.0).then_inc(raw2_zero, 1)
            pool.memset(vT[:, :, :, :, :], 0.0).then_inc(vT_zero, 1)
            pool.memset(minus_half[:, :], -0.5).then_inc(const_ok, 1)
            pool.memset(eps[:, :], LN_EPS).then_inc(const_ok, 1)
            pool.memset(ones[:, :], 1.0).then_inc(const_ok, 1)
            pool.memset(tri[:, :], 1.0).then_inc(const_ok, 1)
            pool.memset(upto[:, :, :], 1.0).then_inc(const_ok, 1)
            pool.iota(pref[:, :], pattern=[[-1, E]], base=E, channel_multiplier=0, allow_small_or_imprecise_dtypes=True).then_inc(const_ok, 1)
            pool.iota(tile128[:, :], pattern=[[P, NT]], base=0, channel_multiplier=0, allow_small_or_imprecise_dtypes=True).then_inc(const_ok, 1)
            pool.iota(unit_no[:, :], pattern=[[1, NU]], base=0, channel_multiplier=0, allow_small_or_imprecise_dtypes=True).then_inc(const_ok, 1)
            pool.iota(record[:, :, :, 0], pattern=[[P, NT], [0, TOP]], base=0, channel_multiplier=1).then_inc(const_ok, 1)
            pool.memset(slots[:, :, 1], 0).then_inc(const_ok, 1)
            pool.iota(slots[:, :, 0], pattern=[[0, NU]], base=T, channel_multiplier=1).then_inc(const_ok, 1)
            pool.wait_ge(const_ok, 11)
            pool.affine_select(out=tri[:, :], in_=tri[:, :], compare_op=ALU.is_gt, fill=0.0, base=0,
                               pattern=[[1, P]], channel_multiplier=-1).then_inc(const_ok, 1)
            pool.affine_select(out=upto[:, :, :], in_=upto[:, :, :], compare_op=ALU.is_ge, fill=0.0, base=0,
                               pattern=[[1, E], [-1, E]], channel_multiplier=0).then_inc(const_ok, 1)
            pool.dma_start(slots_dram.rearrange("(p n) c -> p n c", p=P), slots[:, :, :]).then_inc(table_out, 16)
            pool.wait_ge(small_in, 96)
            pool.wait_ge(pre_pe, NPRE)
            pool.wait_ge(pre_act, NPRE)
            pool.wait_ge(pre_dve, PRE_SPLITS)

            def tile_step(s, par, _):
                t = s + 1
                if has(t, NT):
                    p = (par + 1) % 2
                    wait(pool, mv1_ok, t + 1)
                    wait(pool, nm1_ok, t - 1)
                    wait(pool, xn_ok, t - 1)
                    pool.tensor_tensor(rs1[:, p, 0:1], mv1[:, p, 1:2], eps[:, :], ALU.add).then_inc(eps1_ok, 1)
                    wait(pool, eps1_ok, t + 1)
                    pool.tensor_tensor(rs1[:, p, 1:2], rs1[:, p, 0:1], minus_half[:, :], ALU.pow).then_inc(rstd1_ok, 1)
                t = s - 5
                if has(t, NT):
                    p = (par + 1) % 2
                    wait(pool, mv2_ok, t + 1)
                    wait(pool, nm2_ok, t - 1)
                    wait(pool, xn2_ok, t - 1)
                    pool.tensor_tensor(rs2[:, p, 0:1], mv2[:, p, 1:2], eps[:, :], ALU.add).then_inc(eps2_ok, 1)
                    wait(pool, eps2_ok, t + 1)
                    pool.tensor_tensor(rs2[:, p, 1:2], rs2[:, p, 0:1], minus_half[:, :], ALU.pow).then_inc(rstd2_ok, 1)
                t = s - 2
                if has(t, NT):
                    p = par
                    wait(pool, inv_ok, t + 1)
                    heads = prob[:, p, :].rearrange("p (h k) -> p h k", k=NK)
                    pool.tensor_tensor(heads, heads, hinv[:, p, :].unsqueeze(2).to_broadcast([P, HEADS, NK]),
                                       ALU.mult).then_inc(norm_ok, 1)
                t = s - 3
                if has(t, NT):
                    p = (par + 1) % 2
                    wait(pool, xres_in[p], before(t) + 16)
                    pool.tensor_tensor(xres[:, p, :], xres[:, p, :], bo_bc[:, :], ALU.add).then_inc(xb_ok, 1)

            steps(pool, NT, 1, 5, tile_step)

            for half in xn2_out + x2_out:
                pool.wait_ge(half, before(NT))
            pool.wait_ge(O_ok, NT)
            pool.wait_ge(lg_ok, NT)
            pool.memset(w2_raw[:, :, KH - 1, :], 0.0).then_inc(pad2_zero, 1)
            pool.memset(yrow[:, 0, :], 0.0).then_inc(hid_one, 1)
            pool.memset(hid[:, :, H:H3], 0.0).then_inc(hid_one, 1)
            pool.wait_ge(hid_one, 2)
            pool.memset(hid[:, :, H:H + 1], 1.0).then_inc(hid_one, 1)
            pool.dma_start(xn2_dram[T:T + PADS, :], yrow[:, 0, :]).then_inc(pads_out, 16)
            pool.dma_start(acc_dram[T:T + PADS, :], yrow[:, 0, :]).then_inc(pads_out, 16)

            pool.wait_ge(table_out, 16)
            pool.wait_ge(slot_ok, 1)
            for t in range(NT):
                for k in range(TOP):
                    pool.indirect_dma_start(slots_dram, bass.IndirectOffsetOnAxis(ap=slot[:, k, t:t + 1], axis=0),
                                            record[:, t, k, :], None).then_inc(scat_out, 16)
            pool.wait_ge(pads_out, 32)
            for half in sh.y_out:
                pool.wait_ge(half, before(NT))
            pool.wait_ge(slots_in, 16)

            def routed_step(s, par, _):
                t = s - 4
                if has(t, NU):
                    p = par
                    wait(pool, ro.y_out[1 - p], before(t + 1))
                    pool.tensor_copy(idx_out[:, p, :], slots[:, bass.ds(t, 1), 0]).then_inc(idx_out_ok, 1)
                    wait(pool, idx_out_ok, t + 1)
                    wait(pool, ro.y_ok, t + 1)
                    pool.sem_inc(waited_pool, 1)
                    pool.indirect_dma_start(acc_dram, bass.IndirectOffsetOnAxis(ap=idx_out[:, p, :], axis=0),
                                            yrow[:, p, :], None, compute_op=ALU.add).then_inc(ro.y_out[p], 16)
                t = s + 2
                if has(t, NU):
                    p = par
                    wait(pool, ro.row_in[p], before(t))
                    pool.tensor_copy(idx_in[:, p, :], slots[:, bass.ds(t, 1), 0]).then_inc(idx_in_ok, 1)
                    wait(pool, idx_in_ok, t + 1)
                    wait(pool, ro.X_ok, t - 1)
                    pool.sem_inc(waited_pool, 1)
                    pool.indirect_dma_start(xrow[:, p, :], None, xn2_dram,
                                            bass.IndirectOffsetOnAxis(ap=idx_in[:, p, :], axis=0)).then_inc(ro.row_in[p], 16)

            steps(pool, NU, 2, 4, routed_step)

        @block.scalar
        def _(act):
            act.dma_start(bo_bc[:, :], bo.rearrange("(a d) -> a d", a=1).to_broadcast([P, D])).then_inc(small_in, 16)
            act.dma_start(gateb_bc[:, :], gate_b.rearrange("(a d) -> a d", a=1).to_broadcast([P, E])).then_inc(small_in, 16)
            for k in range(KD):
                act.dma_start(gateT[:, k, :], gate_w[:, k * P:(k + 1) * P].rearrange("e p -> p e"),
                              allow_slow_non_contiguous=True).then_inc(small_in, 16)
            act.dma_start(bs13[:, 0:H], sb1.rearrange("(a d) -> a d", a=1).to_broadcast([P, H])).then_inc(small_in, 16)
            act.dma_start(bs13[:, H:2 * H], sb3.rearrange("(a d) -> a d", a=1).to_broadcast([P, H])).then_inc(small_in, 16)

            def leave(c, out, in_):
                act.wait_ge(pre_pe, c + 1)
                return act.activation(out, in_, ACT.Copy)

            leave(0, ctxT[:, 0, :], ps[:, 0, 0:BK]).then_inc(pre_act, 1)
            leave(1, ctxT[0:KC[1][1], 1, :], ps[0:KC[1][1], 1, 0:BK]).then_inc(pre_act, 1)
            for j in range(NJ):
                c = chunk_a(j, 0)
                if j >= 2:
                    act.wait_ge(pre_pe, chunk_a(j - 2, 3) + 1)
                leave(c, wqT[:, j % 2, :], ps[:, c % 8, 0:D]).then_inc(pre_act, 1)
                leave(c + 1, kT[:, j % 2, :], ps[:, (c + 1) % 8, 0:BK]).then_inc(pre_act, 1)
                for r in range(2):
                    h = 2 * j + r
                    leave(c + 2 + r, Ah[:, :, :, h * NK:(h + 1) * NK].rearrange("p b k n -> p k b n"),
                          ps[:, (c + 2 + r) % 8, :].rearrange("p (k b n) -> p k b n", k=KD, b=B)).then_inc(pre_act, 1)
            act.wait_ge(vT_zero, 1)
            for j in range(NJ):
                c = chunk_u(j, 0)
                if j >= 2:
                    act.wait_ge(pre_pe, chunk_u(j - 2, 2) + 1)
                for r in range(2):
                    half = slice(64 * r, 64 * r + 64)
                    last = leave(c, vT[half, j % 2, :, r, :],
                                 ps[half, c % 8, 0:BK].rearrange("p (b n) -> p b n", b=B))
                last.then_inc(pre_act, 1)
                for g in range(2):
                    leave(c + 1 + g, Uh[:, 2 * g:2 * g + 2, j, :],
                          ps[:, (c + 1 + g) % 8, :].rearrange("p (b d) -> p b d", b=2)).then_inc(pre_act, 1)
            act.wait_ge(sw_in, 80)
            act.activation(ws13h[:, :, :], ws13[:, :, :], ACT.Copy).then_inc(sw_hi, 1)
            act.activation(ws2h[:, :, :], ws2[:, :, :], ACT.Copy).then_inc(sw_hi, 1)
            act.wait_ge(pre_pe, NPRE)
            act.wait_ge(pre_dve, PRE_SPLITS)
            act.wait_ge(small_in, 96)

            def tile_step(s, par, _):
                t = s - 6
                if has(t, NT):
                    p = par
                    wait(act, T2_ok, t + 1)
                    wait(act, R_ok, t - 1)
                    act.activation(xn2T[:, p, :], ps[:, 0, 0:D], ACT.Copy).then_inc(xn2T_ok, 1)
                t = s - 5
                if has(t, NT):
                    p = (par + 1) % 2
                    wait(act, nm2_ok, t + 1)
                    wait(act, T2_ok, t - 1)
                    wait(act, xn2_out[p], before(t))
                    act.activation(xn2[:, p, :], x2[:, p, :], ACT.Identity, bias=nm2[:, p, :],
                                   scale=rs2[:, p, 1:2]).then_inc(xn2_ok, 1)
                t = s + 1
                if has(t, NT):
                    p = (par + 1) % 2
                    wait(act, nm1_ok, t + 1)
                    wait(act, T_ok, t - 1)
                    act.activation(xn[:, p, :], xin[:, p, :], ACT.Identity, bias=nm1[:, p, :],
                                   scale=rs1[:, p, 1:2]).then_inc(xn_ok, 1)
                t = s
                if has(t, NT):
                    p = par
                    wait(act, T_ok, t + 1)
                    wait(act, S_ok, t - 1)
                    act.activation(xTh[:, p, :], ps[:, 0, 0:D], ACT.Copy).then_inc(xTh_ok, 1)
                t = s - 3
                if has(t, NT):
                    p = (par + 1) % 2
                    wait(act, O_ok, t - 1)
                    for h in range(2):
                        wait(act, PT_ok, 2 * t + h + 1)
                        act.activation(pTh[:, p, h * BANK:(h + 1) * BANK], ps[:, 3 + h, :], ACT.Copy).then_inc(pTh_ok, 1)
                t = s - 1
                if has(t, NT):
                    p = (par + 1) % 2
                    wait(act, nmax_ok, t + 1)
                    wait(act, inv_ok, t - 1)
                    wait(act, PT_ok, 2 * t - 2)
                    for h in range(HS, HEADS):
                        act.activation(prob[:, p, h * NK:(h + 1) * NK], ps[:, s_bank(p) + h // 8, h % 8 * NK:(h % 8 + 1) * NK],
                                       ACT.Exp, bias=nmax[:, p, h - HS:h - HS + 1], scale=SCALE,
                                       accum_out=hsum[:, p, h:h + 1])
                    wait(act, sub_ok, t + 1)
                    act.activation(prob[:, p, 0:HS * NK], prob[:, p, 0:HS * NK], ACT.Exp, scale=SCALE).then_inc(exp_ok, 1)

            steps(act, NT, 1, 6, tile_step)

            act.wait_ge(rt_sub, 1)
            act.activation(score[:, :, :], mA[:, :, :], ACT.Exp).then_inc(rt_exp, 1)

            def unit_step(u, n, s, par, routed):
                t = s - 4
                if has(t, n) and routed:
                    p = par
                    wait(act, u.Y_ok, t + 1)
                    wait(act, u.y_out[p], before(t))
                    act.activation(yrow[:, p, :], ps[:, 6 + p, 0:D], ACT.Copy,
                                   scale=slots[:, bass.ds(t, 1), 1].bitcast(F32)).then_inc(u.y_ok, 1)
                t = s
                if has(t, n):
                    p = par
                    wait(act, u.X_ok, t + 1)
                    wait(act, u.UV_ok, t - 1)
                    act.activation(uxTh[:, p, :], ps[:, 0, 0:D], ACT.Copy).then_inc(u.xTh_ok, 1)
                t = s - 3
                if has(t, n):
                    wait(act, u.H_ok, t + 1)
                    wait(act, u.Y_ok, t)
                    act.activation(hTh[:, :], ps[:, 5, 0:H3], ACT.Copy).then_inc(u.hTh_ok, 1)
                t = s - 2
                if has(t, n):
                    p = par
                    wait(act, u.z_ok, t + 1)
                    act.activation(hid[:, p, 0:H], hid[:, p, 0:H], ACT.Silu).then_inc(u.h_ok, 1)

            def shared_step(s, par, e):
                unit_step(sh, NT, s, par, False)
                if e is not None:
                    wait(act, raw_in, 80 * e + 80)
                    for k in range(KD):
                        act.activation(w13h[:, bass.ds(e, 1), k, :], w13_raw[:, bass.ds(e, 1), k, :], ACT.Copy).then_inc(w_hi, 1)
                    high, raw = [a[:, bass.ds(e, 1), :, :].rearrange("p e c d -> p (e c d)") for a in (w2h, w2_raw)]
                    act.activation(high, raw, ACT.Copy).then_inc(w_hi, 1)

            act.wait_ge(lg_ok, NT)
            act.wait_ge(hid_one, 3)
            steps(act, NT, 0, 4, shared_step, extra=E, skip=2)
            for half in sh.y_out:
                act.wait_ge(half, before(NT))
            act.wait_ge(slots_in, 16)
            steps(act, NU, 0, 4, lambda s, par, _: unit_step(ro, NU, s, par, True))

        @block.vector
        def _(dve):
            def low(c, n, out, in_, high):
                dve.wait_ge(pre_act, c + 1)
                dve.tensor_tensor(out, in_, high, ALU.subtract).then_inc(pre_dve, 1)

            for j in range(NJ):
                for r in range(2):
                    c = chunk_a(j, 2 + r)
                    h = 2 * j + r
                    cols = slice(h * NK, (h + 1) * NK)
                    for k in range(KD):
                        if k == 0:
                            dve.wait_ge(pre_act, c + 1)
                        last = dve.tensor_tensor(Al[:, :, k, cols],
                                                 ps[:, c % 8, k * BK:(k + 1) * BK].rearrange("p (b n) -> p b n", b=B),
                                                 f32(Ah[:, :, k, cols]), ALU.subtract)
                    last.then_inc(pre_dve, 1)
            for j in range(NJ):
                for g in range(2):
                    c = chunk_u(j, 1 + g)
                    low(c, 0, Ul[:, 2 * g:2 * g + 2, j, :], ps[:, c % 8, :].rearrange("p (b d) -> p b d", b=2),
                        f32(Uh[:, 2 * g:2 * g + 2, j, :]))
            dve.wait_ge(sw_hi, 1)
            dve.tensor_tensor(ws13l[:, :, :], ws13[:, :, :], f32(ws13h[:, :, :]), ALU.subtract).then_inc(sw_lo, 1)
            dve.wait_ge(sw_hi, 2)
            dve.tensor_tensor(ws2l[:, :, :], ws2[:, :, :], f32(ws2h[:, :, :]), ALU.subtract).then_inc(sw_lo, 1)
            dve.wait_ge(pre_pe, NPRE)
            dve.wait_ge(pre_act, NPRE)

            def heads(ap):
                return ap.rearrange("p (h k) -> p h k", k=NK)

            def tile_step(s, par, _):
                t = s - 2
                if has(t, NT):
                    p = par
                    wait(dve, exp_ok, t + 1)
                    dve.tensor_reduce(hsum[:, p, 0:HS], heads(prob[:, p, 0:HS * NK]), AX.X, ALU.add).then_inc(sum_ok, 1)
                    wait(dve, sum_ok, t + 1)
                    wait(dve, norm_ok, t - 1)
                    dve.reciprocal(hinv[:, p, :], hsum[:, p, :]).then_inc(inv_ok, 1)
                t = s - 5
                if has(t, NT):
                    p = (par + 1) % 2
                    wait(dve, rstd2_ok, t + 1)
                    wait(dve, xn2_ok, t - 1)
                    dve.scalar_tensor_tensor(out=nm2[:, p, :], in0=mv2[:, p, 0:1], scalar=-1.0, in1=rs2[:, p, 1:2],
                                             op0=ALU.mult, op1=ALU.mult).then_inc(nm2_ok, 1)
                t = s + 1
                if has(t, NT):
                    p = (par + 1) % 2
                    wait(dve, rstd1_ok, t + 1)
                    wait(dve, xn_ok, t - 1)
                    dve.scalar_tensor_tensor(out=nm1[:, p, :], in0=mv1[:, p, 0:1], scalar=-1.0, in1=rs1[:, p, 1:2],
                                             op0=ALU.mult, op1=ALU.mult).then_inc(nm1_ok, 1)
                t = s - 6
                if has(t, NT):
                    wait(dve, R_ok, t + 1)
                    dve.tensor_copy(logits[:, bass.ds(t, 1), :].rearrange("p a e -> p (a e)"), ps[:, 0, 0:E]).then_inc(lg_ok, 1)
                t = s + 2
                if has(t, NT):
                    p = par
                    wait(dve, x_in[p], before(t) + 16)
                    dve.bn_stats(st1[:, p, :], xin[:, p, :]).then_inc(st1_ok, 1)
                    wait(dve, st1_ok, t + 1)
                    wait(dve, rstd1_ok, t - 1)
                    dve.sem_inc(waited_dve, 1)
                    dve.bn_aggr(mv1[:, p, :], st1[:, p, :]).then_inc(mv1_ok, 1)
                t = s - 1
                if has(t, NT):
                    p = (par + 1) % 2
                    wait(dve, S_ok, t + 1)
                    scores = ps[:, s_bank(p):s_bank(p) + 2, :].rearrange("p a (h k) -> p (a h) k", k=NK)
                    dve.tensor_reduce(hmax[:, p, :], scores, AX.X, ALU.max).then_inc(max_ok, 1)
                    wait(dve, max_ok, t + 1)
                    wait(dve, exp_ok, t - 1)
                    dve.tensor_scalar(nmax[:, p, :], hmax[:, p, HS:HEADS], -SCALE, None, ALU.mult).then_inc(nmax_ok, 1)
                    wait(dve, PT_ok, 2 * t - 2)
                    dve.tensor_tensor(heads(prob[:, p, 0:HS * NK]), scores[:, 0:HS, :],
                                      hmax[:, p, 0:HS].unsqueeze(2).to_broadcast([P, HS, NK]),
                                      ALU.subtract).then_inc(sub_ok, 1)
                t = s
                if has(t, NT):
                    p = par
                    wait(dve, xTh_ok, t + 1)
                    wait(dve, S_ok, t - 1)
                    dve.tensor_tensor(xTl[:, p, :], ps[:, 0, 0:D], f32(xTh[:, p, :]), ALU.subtract).then_inc(xTl_ok, 1)
                t = s - 3
                if has(t, NT):
                    p = (par + 1) % 2
                    for h in range(2):
                        cols = slice(h * BANK, (h + 1) * BANK)
                        wait(dve, pTh_ok, 2 * t + h + 1)
                        dve.tensor_tensor(pTl[:, p, cols], ps[:, 3 + h, :], f32(pTh[:, p, cols]),
                                          ALU.subtract).then_inc(pTl_ok, 1)
                t = s - 4
                if has(t, NT):
                    p = par
                    wait(dve, O_ok, t + 1)
                    wait(dve, xb_ok, t + 1)
                    wait(dve, x2_out[p], before(t))
                    wait(dve, xn2_ok, t - 1)
                    dve.tensor_tensor(x2[:, p, :], ps[:, 5, 0:D], xres[:, p, :], ALU.add).then_inc(x2_ok, 1)
                    wait(dve, x2_ok, t + 1)
                    dve.bn_stats(st2[:, p, :], x2[:, p, :]).then_inc(st2_ok, 1)
                    wait(dve, st2_ok, t + 1)
                    wait(dve, rstd2_ok, t - 1)
                    dve.sem_inc(waited_dve, 1)
                    dve.bn_aggr(mv2[:, p, :], st2[:, p, :]).then_inc(mv2_ok, 1)

            steps(dve, NT, 2, 6, tile_step)

            linked = [0]

            def link(ins):
                linked[0] += 1
                ins.then_inc(rt, 1)
                dve.wait_ge(rt, linked[0])

            def over_e(ap):
                return ap.unsqueeze(2).to_broadcast([P, NT, E])

            dve.wait_ge(lg_ok, NT)
            dve.wait_ge(O_ok, NT)
            dve.wait_ge(const_ok, 13)
            link(dve.tensor_reduce(v32[:, 0, :], logits[:, :, :], AX.X, ALU.max))
            dve.tensor_tensor(mA[:, :, :], logits[:, :, :], over_e(v32[:, 0, :]), ALU.subtract).then_inc(rt_sub, 1)
            dve.wait_ge(rt_exp, 1)
            link(dve.tensor_reduce(v32[:, 1, :], score[:, :, :], AX.X, ALU.add))
            link(dve.reciprocal(v32[:, 2, :], v32[:, 1, :]))
            link(dve.tensor_tensor(score[:, :, :], score[:, :, :], over_e(v32[:, 2, :]), ALU.mult))
            link(dve.tensor_tensor(biased[:, :, :], score[:, :, :],
                                   gateb_bc[:, :].unsqueeze(1).to_broadcast([P, NT, E]), ALU.add))
            for k, mark in enumerate((first, second)):
                link(dve.tensor_reduce(v32[:, 3, :], biased[:, :, :], AX.X, ALU.max))
                link(dve.tensor_tensor(mA[:, :, :], biased[:, :, :], over_e(v32[:, 3, :]), ALU.is_ge))
                link(dve.tensor_tensor(mA[:, :, :], mA[:, :, :],
                                       pref[:, :].unsqueeze(1).to_broadcast([P, NT, E]), ALU.mult))
                link(dve.tensor_reduce(v32[:, 3, :], mA[:, :, :], AX.X, ALU.max))
                link(dve.tensor_tensor(mark[:, :, :], mA[:, :, :], over_e(v32[:, 3, :]), ALU.is_equal))
                if k == 0:
                    link(dve.scalar_tensor_tensor(out=biased[:, :, :], in0=mark[:, :, :], scalar=LOWEST,
                                                  in1=biased[:, :, :], op0=ALU.mult, op1=ALU.add))
            dve.tensor_tensor(chosen[:, :, :], first[:, :, :], second[:, :, :], ALU.add).then_inc(chosen_ok, 1)
            for k, mark in enumerate((first, second)):
                link(dve.tensor_tensor(mA[:, :, :], mark[:, :, :], score[:, :, :], ALU.mult))
                link(dve.tensor_reduce(record[:, :, k, 1].bitcast(F32), mA[:, :, :], AX.X, ALU.add))
            dve.wait_ge(rank_ok, 2)
            rows = v32[:, 4, 0:E]
            tiles = v32[:, 4, E:2 * E]
            ends = v32[:, 4, 2 * E:3 * E]
            begin = v32[:, 4, 3 * E:4 * E]
            link(dve.tensor_reduce(rows, ps[:, 1, 0:NT * E].rearrange("p (t e) -> p e t", e=E), AX.X, ALU.add))
            link(dve.tensor_tensor(mA[:, :, :].rearrange("p t e -> p (t e)").rearrange("p (e t) -> p e t", e=E),
                                   rows.unsqueeze(2).to_broadcast([P, E, NT]),
                                   tile128[:, :].unsqueeze(1).to_broadcast([P, E, NT]), ALU.is_gt))
            link(dve.tensor_reduce(tiles, mA[:, :, :].rearrange("p t e -> p (t e)").rearrange("p (e t) -> p e t", e=E),
                                   AX.X, ALU.add))
            ee = mB[:, 0:E, :]
            link(dve.tensor_tensor(ee, upto[:, :, :], tiles.unsqueeze(1).to_broadcast([P, E, E]), ALU.mult))
            link(dve.tensor_reduce(ends, ee, AX.X, ALU.add))
            link(dve.tensor_tensor(begin, ends, tiles, ALU.subtract))
            link(dve.scalar_tensor_tensor(out=slot8[:, :, :], in0=begin.unsqueeze(1).to_broadcast([P, NT, E]),
                                          scalar=float(P), in1=ps[:, 0, 0:NT * E].rearrange("p (t e) -> p t e", e=E),
                                          op0=ALU.mult, op1=ALU.add))
            for k, mark in enumerate((first, second)):
                link(dve.tensor_tensor(mA[:, :, :], mark[:, :, :], slot8[:, :, :], ALU.mult))
                link(dve.tensor_reduce(v32[:, 5 + k, :], mA[:, :, :], AX.X, ALU.add))
            link(dve.tensor_copy(slot[:, :, :], v32[:, 5:5 + TOP, :]))
            link(dve.tensor_scalar(slot_col[:, :, :], slot[:, :, :], 7, None, ALU.logical_shift_right))
            link(dve.tensor_scalar(slot_row[:, :, :], slot[:, :, :], P - 1, None, ALU.bitwise_and))
            dve.scalar_tensor_tensor(out=slot[:, :, :], in0=slot_row[:, :, :], scalar=float(NU), in1=slot_col[:, :, :],
                                     op0=ALU.mult, op1=ALU.add).then_inc(slot_ok, 1)
            link(dve.tensor_tensor(big[:, :, :], unit_no[:, :].unsqueeze(2).to_broadcast([P, NU, E]),
                                   ends.unsqueeze(1).to_broadcast([P, NU, E]), ALU.is_ge))
            passed = mB[:, :, :].rearrange("p t e -> p (t e)")[:, 0:NU]
            link(dve.tensor_reduce(passed, big[:, :, :], AX.X, ALU.add))
            link(dve.tensor_scalar(expert_of[:, :], passed, float(E - 1), None, ALU.min))
            link(dve.memset(step_experts[:, :], 0))
            link(dve.tensor_copy(step_experts[:, 1:1 + NU], expert_of[:, :]))
            dve.scalar_tensor_tensor(out=step_experts[:, 4:4 + NU], in0=expert_of[:, :], scalar=float(E),
                                     in1=step_experts[:, 4:4 + NU], op0=ALU.mult, op1=ALU.add).then_inc(eid_ok, 1)

            def unit_step(u, n, s, par, routed):
                t = s - 4
                if has(t, n) and not routed:
                    p = par
                    wait(dve, u.Y_ok, t + 1)
                    wait(dve, u.x2_in, 16 * t + 16)
                    wait(dve, u.y_out[p], before(t))
                    dve.tensor_tensor(yrow[:, p, :], ps[:, 6 + p, 0:D], x2row[:, :], ALU.add).then_inc(u.y_ok, 1)
                t = s
                if has(t, n):
                    p = par
                    wait(dve, u.xTh_ok, t + 1)
                    wait(dve, u.UV_ok, t - 1)
                    dve.tensor_tensor(uxTl[:, p, :], ps[:, 0, 0:D], f32(uxTh[:, p, :]), ALU.subtract).then_inc(u.xTl_ok, 1)
                t = s - 3
                if has(t, n):
                    wait(dve, u.hTh_ok, t + 1)
                    wait(dve, u.Y_ok, t)
                    dve.tensor_tensor(hTl[:, :], ps[:, 5, 0:H3], f32(hTh[:, :]), ALU.subtract).then_inc(u.hTl_ok, 1)
                t = s - 1
                if has(t, n):
                    p = (par + 1) % 2
                    if routed:
                        e = dve.value_load(expert_of[0:1, bass.ds(t, 1)], min_val=0, max_val=E - 1)
                        bias = b13[:, bass.ds(e, 1), :].rearrange("p e (a h) -> p (e a) h", a=2)
                    else:
                        bias = bs13[:, :].rearrange("p (a h) -> p a h", a=2)
                    wait(dve, u.UV_ok, t + 1)
                    wait(dve, u.z_ok, t)
                    dve.tensor_tensor(uv[:, :, :], ps[:, 1 + 2 * p:3 + 2 * p, 0:H], bias, ALU.add).then_inc(u.bias_ok, 1)
                    wait(dve, u.bias_ok, t + 1)
                    wait(dve, u.H_ok, t - 1)
                    dve.tensor_tensor(hid[:, p, 0:H], uv[:, 0, :], uv[:, 1, :], ALU.mult).then_inc(u.z_ok, 1)

            def shared_step(s, par, e):
                unit_step(sh, NT, s, par, False)
                if e is not None:
                    for k in range(KD):
                        wait(dve, w_hi, 3 * e + k + 1)
                        dve.tensor_tensor(w13l[:, bass.ds(e, 1), k, :], w13_raw[:, bass.ds(e, 1), k, :],
                                          f32(w13h[:, bass.ds(e, 1), k, :]), ALU.subtract).then_inc(w_lo, 1)
                    wait(dve, w_hi, 3 * e + 3)
                    flat = [a[:, bass.ds(e, 1), :, :].rearrange("p e c d -> p (e c d)") for a in (w2l, w2_raw, w2h)]
                    dve.tensor_tensor(flat[0], flat[1], f32(flat[2]),
                                      ALU.subtract).then_inc(w_lo, 1)

            dve.wait_ge(pads_out, 32)
            dve.wait_ge(hid_one, 3)
            dve.wait_ge(small_in, 96)
            steps(dve, NT, 0, 4, shared_step, extra=E, skip=2)
            dve.wait_ge(b13_in, 32)
            steps(dve, NU, 0, 4, lambda s, par, _: unit_step(ro, NU, s, par, True))

        @block.tensor
        def _(pe):
            PARTS = ((0, 0), (1, 0), (0, 1))

            def product(out, stationary, moving, n):
                last = None
                for k in range(n):
                    for i, (a, b) in enumerate(PARTS):
                        last = pe.matmul(out, stationary(k, a), moving(k, b), start=(k == 0 and i == 0),
                                         stop=(k == n - 1 and i == len(PARTS) - 1))
                return last

            def bank_free(c):
                if c >= 8:
                    pe.wait_ge(pre_act, c - 7)
                    n = split_chunks(c - 7)
                    if n:
                        pe.wait_ge(pre_dve, n)

            pe.wait_ge(id_ok, 2)
            pe.wait_ge(w_in, 64)
            for i, (lo, n) in enumerate(KC):
                for r in range(2):
                    last = pe.transpose(ps[0:n, i, r * P:(r + 1) * P], ctx_sb[:, r, lo:lo + n], ident[:, :])
                last.then_inc(pre_pe, 1)
            for j in range(NJ):
                cols = slice(j * P, (j + 1) * P)
                c = chunk_a(j, 0)
                bank_free(c)
                for k in range(KD):
                    last = pe.transpose(ps[:, c % 8, k * P:(k + 1) * P], wq_sb[:, k, cols], ident[:, :])
                last.then_inc(pre_pe, 1)
                if j == 0:
                    pe.wait_ge(pre_act, 2)
                bank_free(c + 1)
                for i, (lo, n) in enumerate(KC):
                    last = pe.matmul(ps[:, (c + 1) % 8, 0:BK], wk_sb[0:n, i, cols], ctxT[0:n, i, :],
                                     start=(i == 0), stop=(i == 1))
                last.then_inc(pre_pe, 1)
                pe.wait_ge(pre_act, c + 2)
                for r in range(2):
                    bank_free(c + 2 + r)
                    half = slice(64 * r, 64 * r + 64)
                    for k in range(KD):
                        last = pe.matmul(ps[:, (c + 2 + r) % 8, k * BK:(k + 1) * BK], wqT[half, j % 2, k * P:(k + 1) * P],
                                         kT[half, j % 2, :], start=True, stop=True)
                    last.then_inc(pre_pe, 1)
            pe.wait_ge(wv_in, 48)
            for j in range(NJ):
                cols = slice(j * P, (j + 1) * P)
                c = chunk_u(j, 0)
                bank_free(c)
                for i, (lo, n) in enumerate(KC):
                    last = pe.matmul(ps[:, c % 8, 0:BK], wv_sb[0:n, i, cols], ctxT[0:n, i, :],
                                     start=(i == 0), stop=(i == 1))
                last.then_inc(pre_pe, 1)
                pe.wait_ge(pre_act, c + 1)
                for g in range(2):
                    bank_free(c + 1 + g)
                    for b in range(2):
                        last = pe.matmul(ps[:, (c + 1 + g) % 8, b * D:(b + 1) * D],
                                         vT[:, j % 2, 2 * g + b, :, :].rearrange("p a n -> p (a n)"),
                                         wo_sb[:, j, :], start=True, stop=True)
                    last.then_inc(pre_pe, 1)
            pe.wait_ge(pre_act, NPRE)
            pe.wait_ge(pre_dve, PRE_SPLITS)
            pe.wait_ge(small_in, 96)

            def tile_step(s, par, _):
                def scores(t, p, g):
                    b = t // TPB
                    return product(ps[:, s_bank(p) + g, :],
                                   lambda k, part: (xTh, xTl)[part][:, p, k * P:(k + 1) * P],
                                   lambda k, part: (Ah, Al)[part][:, bass.ds(b, 1), k, g * BANK:(g + 1) * BANK]
                                   .rearrange("p a n -> p (a n)"), KD)

                t = s - 1
                if has(t, NT):
                    wait(pe, xTl_ok, t + 1)
                    wait(pe, exp_ok, t - 1)
                    scores(t, (par + 1) % 2, 0)
                t = s - 6
                if has(t, NT):
                    p = par
                    wait(pe, xn2T_ok, t + 1)
                    for k in range(KD):
                        last = pe.matmul(ps[:, 0, 0:E], xn2T[:, p, k * P:(k + 1) * P], gateT[:, k, :],
                                         start=(k == 0), stop=(k == KD - 1))
                    last.then_inc(R_ok, 1)
                t = s - 1
                if has(t, NT):
                    scores(t, (par + 1) % 2, 1).then_inc(S_ok, 1)
                t = s
                if has(t, NT):
                    p = par
                    wait(pe, xn_ok, t + 1)
                    wait(pe, xTl_ok, t)
                    wait(pe, lg_ok, t - 5)
                    for k in range(KD):
                        last = pe.transpose(ps[:, 0, k * P:(k + 1) * P], xn[:, p, k * P:(k + 1) * P], ident[:, :])
                    last.then_inc(T_ok, 1)
                t = s - 3
                if has(t, NT):
                    p = (par + 1) % 2
                    wait(pe, norm_ok, t + 1)
                    for h in range(2):
                        wait(pe, pTl_ok, 2 * t + h - 1)
                        for i in range(NJ // 2):
                            j = h * (NJ // 2) + i
                            last = pe.transpose(ps[:, 3 + h, i * P:(i + 1) * P], prob[:, p, j * P:(j + 1) * P], ident[:, :])
                        last.then_inc(PT_ok, 1)
                t = s - 4
                if has(t, NT):
                    p = par
                    b = t // TPB
                    wait(pe, pTl_ok, 2 * t + 2)
                    wait(pe, x2_ok, t)
                    product(ps[:, 5, 0:D],
                            lambda k, part: (pTh, pTl)[part][:, p, k * P:(k + 1) * P],
                            lambda k, part: (Uh, Ul)[part][:, bass.ds(b, 1), k, :].rearrange("p a d -> p (a d)"),
                            NJ).then_inc(O_ok, 1)
                t = s - 5
                if has(t, NT):
                    p = (par + 1) % 2
                    wait(pe, xn2_ok, t + 1)
                    wait(pe, lg_ok, t)
                    wait(pe, xTl_ok, s + 1 if has(s, NT) else NT)
                    for k in range(KD):
                        last = pe.transpose(ps[:, 0, k * P:(k + 1) * P], xn2[:, p, k * P:(k + 1) * P], ident[:, :])
                    last.then_inc(T2_ok, 1)

            steps(pe, NT, 0, 6, tile_step)

            pe.wait_ge(chosen_ok, 1)
            pe.wait_ge(x2_ok, NT)
            pe.wait_ge(lg_ok, NT)
            flat = chosen[:, :, :].rearrange("p t e -> p (t e)")
            pe.matmul(ps[:, 1, 0:NT * E], ones[:, :], flat, start=True, stop=True).then_inc(rank_ok, 1)
            pe.matmul(ps[:, 0, 0:NT * E], tri[:, :], flat, start=True, stop=False, skip_group_check=True)
            for t in range(NT - 1):
                n = NT - 1 - t
                last = pe.matmul(ps[:, 0, (t + 1) * E:NT * E], ones[:, :],
                                 chosen[:, t:t + 1, :].to_broadcast([P, n, E]), start=False, stop=(t == NT - 2),
                                 skip_group_check=True)
            last.then_inc(rank_ok, 1)
            pe.wait_ge(slot_ok, 1)

            def unit_step(u, n, s, par, routed):
                def weights(parts, e, k, part, cols):
                    if not routed:
                        return parts[part][:, k, cols]
                    return parts[part][:, bass.ds(e, 1), k, cols].rearrange("p a n -> p (a n)")

                e_uv = e_y = None
                if routed:
                    both = pe.value_load(step_experts[0:1, bass.ds(s, 1)], min_val=0, max_val=E * E - 1)
                    e_uv, e_y = both % E, both // E

                t = s - 4
                if has(t, n):
                    p = par
                    wait(pe, u.hTl_ok, t + 1)
                    wait(pe, u.y_ok, t - 1)
                    w2s = (w2h, w2l) if routed else (ws2h, ws2l)
                    product(ps[:, 6 + p, 0:D],
                            lambda k, part: (hTh, hTl)[part][:, k * P:(k + 1) * P],
                            lambda k, part: weights(w2s, e_y, k, part, slice(0, D)), KH).then_inc(u.Y_ok, 1)
                t = s
                if has(t, n):
                    p = par
                    wait(pe, u.row_in[p], before(t) + 16)
                    wait(pe, u.xTl_ok, t)
                    for k in range(KD):
                        last = pe.transpose(ps[:, 0, k * P:(k + 1) * P], xrow[:, p, k * P:(k + 1) * P], ident[:, :])
                    last.then_inc(u.X_ok, 1)
                t = s - 3
                if has(t, n):
                    p = (par + 1) % 2
                    wait(pe, u.h_ok, t + 1)
                    wait(pe, u.hTl_ok, t)
                    for k in range(KH):
                        last = pe.transpose(ps[:, 5, k * P:(k + 1) * P], hid[:, p, k * P:(k + 1) * P], ident[:, :])
                    last.then_inc(u.H_ok, 1)
                t = s - 1
                if has(t, n):
                    p = (par + 1) % 2
                    wait(pe, u.xTl_ok, t + 1)
                    wait(pe, u.bias_ok, t - 1)
                    w13 = (w13h, w13l) if routed else (ws13h, ws13l)
                    for g in range(2):
                        last = product(ps[:, 1 + 2 * p + g, 0:H],
                                       lambda k, part: (uxTh, uxTl)[part][:, p, k * P:(k + 1) * P],
                                       lambda k, part: weights(w13, e_uv, k, part, slice(g * H, (g + 1) * H)), KD)
                    last.then_inc(u.UV_ok, 1)

            pe.wait_ge(sw_lo, 2)
            steps(pe, NT, 0, 4, lambda s, par, _: unit_step(sh, NT, s, par, False), extra=E)
            pe.wait_ge(w_lo, 3 * E)
            pe.wait_ge(eid_ok, 1)
            steps(pe, NU, 0, 4, lambda s, par, _: unit_step(ro, NU, s, par, True))


_INS = ['x', 'ctx_768', 'L0_xattn_Wq', 'L0_xattn_Wk', 'L0_xattn_Wv', 'L0_xattn_Wo', 'L0_xattn_bo',
        'L0_ffn_gate_w', 'L0_ffn_gate_b', 'L0_ffn_w1', 'L0_ffn_b1', 'L0_ffn_w3', 'L0_ffn_b3', 'L0_ffn_w2', 'L0_ffn_b2',
        'L0_ffn_sw1', 'L0_ffn_sb1', 'L0_ffn_sw3', 'L0_ffn_sb3', 'L0_ffn_sw2', 'L0_ffn_sb2']


def kernel(**inputs):
    import numpy as _np
    import concourse.bacc as _bacc
    from concourse import mybir as _mybir
    from concourse.bass_utils import run_bass_kernel_spmd as _run

    nc = _bacc.Bacc("TRN2", target_bir_lowering=False, num_devices=1)
    arrays, args = {}, []
    for name in _INS:
        a = _np.ascontiguousarray(inputs[name])
        arrays[f"in_{name}"] = a
        args.append(nc.dram_tensor(f"in_{name}", a.shape, _mybir.dt.from_np(a.dtype), kind="ExternalInput").ap())
    out = nc.dram_tensor("out_x", inputs['x'].shape, _mybir.dt.float32, kind="ExternalOutput")
    xattn_moe(nc, *args, out.ap())
    r = _run(nc, [arrays], core_ids=[0])
    return r.results[0]["out_x"]
```

```python
from contextlib import ExitStack

import concourse.bass as bass
from concourse import mybir

F32 = mybir.dt.float32
F32R = mybir.dt.float32r
BF16 = mybir.dt.bfloat16
I32 = mybir.dt.int32
ALU = mybir.AluOpType
ACT = mybir.ActivationFunctionType
AX = mybir.AxisListType

P = 128
BANK = 512
PADS = P
LN_EPS = 1e-5
LOWEST = -3.0e38


def wait(eng, sem, n):
    if not isinstance(n, int) or n > 0:
        eng.wait_ge(sem, n)


def xattn_moe(nc, x, ctx, Wq, Wk, Wv, Wo, bo, gate_w, gate_b, w1, b1, w3, b3, w2, b2,
              sw1, sb1, sw3, sb3, sw2, sb2, out):
    B, N, D = x.shape
    _, NK, DC = ctx.shape
    INNER = Wq.shape[1]
    DH = 64
    HEADS = INNER // DH
    E, _, H = w1.shape
    E_DVE = E // 2
    TOP = 2
    T = B * N
    NT = T // P
    TPB = N // P
    KD = D // P
    HK = HEADS * NK
    NJ = INNER // P
    BK = B * NK
    KC = [(0, P), (P, DC - P)]
    SCALE = DH ** -0.5
    HS = 8
    H3 = 3 * P
    KH = H3 // P
    HR = H - (KH - 1) * P
    NU = TOP * NT + E - 1
    assert HK == 2 * BANK and BK == 2 * P and D == 2 * P and NK == 64 and HR < P

    x_rows = x.rearrange("b n d -> (b n) d")
    xn2_dram = nc.dram_tensor("xn2_scratch", [T + PADS, D], F32, kind="Internal").ap()
    x2_dram = nc.dram_tensor("x2_scratch", [T, D], F32, kind="Internal").ap()
    slots_dram = nc.dram_tensor("slots_scratch", [P * NU, 2], I32, kind="Internal").ap()

    stack = ExitStack()
    with stack:
        def sb(name, shape, dt, on=stack):
            return on.enter_context(nc.sbuf_tensor(name, shape, dt))

        def sem(name):
            return stack.enter_context(nc.semaphore(name))

        ident = sb("ident", [P, P], F32)
        gateT = sb("gateT", [P, KD, E], F32)
        gateb_bc = sb("gateb_bc", [P, E], F32)
        minus_half = sb("minus_half", [P, 1], F32)
        eps = sb("eps", [P, 1], F32)
        record = sb("record", [P, NT, TOP, 2], I32)
        slot = sb("slot", [P, TOP, NT], I32)
        slot_col = sb("slot_col", [P, TOP, NT], I32)
        slot_row = sb("slot_row", [P, TOP, NT], I32)
        expert_of = sb("expert_of", [P, NU], I32)
        step_experts = sb("step_experts", [P, NU + 4], I32)
        slots = sb("slots", [P, NU, 2], I32)
        idx_in = sb("idx_in", [P, 2, 1], I32)
        idx_out = sb("idx_out", [P, 2, 1], I32)
        ws13h = sb("ws13h", [P, KD, 2 * H], F32R)
        ws2h = sb("ws2h", [P, KH, D], F32R)
        raw = ExitStack()
        ws13 = sb("ws13", [P, KD, 2 * H], F32, raw)
        ws2 = sb("ws2", [P, KH, D], F32, raw)
        raw.close()
        ws13l = sb("ws13l", [P, KD, 2 * H], F32R)
        ws2l = sb("ws2l", [P, KH, D], F32R)
        bs13 = sb("bs13", [P, 2 * H], F32)

        att = ExitStack()
        Ah = sb("Ah", [P, B, KD, HK], F32R, att)
        Al = sb("Al", [P, B, KD, HK], F32R, att)
        pre = ExitStack()
        wq_sb = sb("wq_sb", [P, KD, INNER], F32, pre)
        wkh = sb("wkh", [P, 2, INNER], F32R, pre)
        raw = ExitStack()
        wk_raw = sb("wk_raw", [P, 2, INNER], F32, raw)
        raw.close()
        wkl = sb("wkl", [P, 2, INNER], F32R, pre)
        wqTh = sb("wqTh", [P, 2, D], F32R, pre)
        wqTl = sb("wqTl", [P, 2, D], F32R, pre)
        kTh = sb("kTh", [P, 2, 2, BK], F32R, pre)
        kTl = sb("kTl", [P, 2, 2, BK], F32R, pre)
        ctx_sb = sb("ctx_sb", [P, 2, DC], F32, pre)
        zeros = sb("zeros", [P, 2 * 2 * BK], F32, pre)
        pre.close()
        Uh = sb("Uh", [P, B, NJ, D], F32R, att)
        Ul = sb("Ul", [P, B, NJ, D], F32R, att)
        bo_bc = sb("bo_bc", [P, D], F32, att)
        xin = sb("xin", [P, 2, D], F32, att)
        xn = sb("xn", [P, 2, D], F32, att)
        xTh = sb("xTh", [P, 2, D], F32R, att)
        xTl = sb("xTl", [P, 2, D], F32R, att)
        st1 = sb("st1", [P, 2, 6], F32, att)
        mv1 = sb("mv1", [P, 2, 2], F32, att)
        rs1 = sb("rs1", [P, 2, 2], F32, att)
        nm1 = sb("nm1", [P, 2, 1], F32, att)
        pre = ExitStack()
        raw = ExitStack()
        wv_raw = sb("wv_raw", [P, 2, INNER], F32, raw)
        wo_raw = sb("wo_raw", [P, NJ, D], F32, raw)
        raw.close()
        wvl = sb("wvl", [P, 2, INNER], F32R, pre)
        wol = sb("wol", [P, NJ, D], F32R, pre)
        wvh = sb("wvh", [P, 2, INNER], F32R, pre)
        woh = sb("woh", [P, NJ, D], F32R, pre)
        ctxTh = sb("ctxTh", [P, 2, BK], F32R, pre)
        ctxTl = sb("ctxTl", [P, 2, BK], F32R, pre)
        vTh = sb("vTh", [P, 2, B, 2, NK], F32R, pre)
        vTl = sb("vTl", [P, 2, B, 2, NK], F32R, pre)
        pre.close()
        xres = sb("xres", [P, 2, D], F32, att)
        prob = sb("prob", [P, 2, HK], F32, att)
        pTh = sb("pTh", [P, 2, HK], F32R, att)
        pTl = sb("pTl", [P, 2, HK], F32R, att)
        x2 = sb("x2", [P, 2, D], F32, att)
        xn2 = sb("xn2", [P, 2, D], F32, att)
        xn2T = sb("xn2T", [P, 2, D], F32, att)
        st2 = sb("st2", [P, 2, 6], F32, att)
        mv2 = sb("mv2", [P, 2, 2], F32, att)
        rs2 = sb("rs2", [P, 2, 2], F32, att)
        nm2 = sb("nm2", [P, 2, 1], F32, att)
        hmax = sb("hmax", [P, 2, HEADS], F32, att)
        hsum = sb("hsum", [P, 2, HEADS], F32, att)
        nmax = sb("nmax", [P, 2, HEADS - HS], F32, att)
        hinv = sb("hinv", [P, 2, HEADS], F32, att)
        att.close()

        w13h = sb("w13h", [P, E, KD, 2 * H], F32R)
        w2h = sb("w2h", [P, E, KH, D], F32R)
        raw = ExitStack()
        w2_raw = sb("w2_raw", [P, E, KH, D], F32, raw)
        w13_raw = sb("w13_raw", [P, E, KD, 2 * H], F32, raw)
        raw.close()
        w2l = sb("w2l", [P, E, KH, D], F32R)
        math = ExitStack()
        sb("below_math", [P, E * KD * 2 * H - 3072 - 512], F32, math)
        mA = sb("mA", [P, NT, E], F32, math)
        score = sb("score", [P, NT, E], F32, math)
        biased = sb("biased", [P, NT, E], F32, math)
        mB = sb("mB", [P, NT, E], F32, math)
        first = sb("first", [P, NT, E], F32, math)
        second = sb("second", [P, NT, E], F32, math)
        chosen = sb("chosen", [P, NT, E], BF16, math)
        slot8 = sb("slot8", [P, NT, E], F32, math)
        big = sb("big", [P, NU, E], F32, math)
        v32 = sb("v32", [P, 8, NT], F32, math)
        math.close()
        w13l = sb("w13l", [P, E, KD, 2 * H], F32R)
        b13 = sb("b13", [P, E, 2 * H], F32)
        xrow = sb("xrow", [P, 2, D], F32)
        x2row = sb("x2row", [P, 2, D], F32)
        uxTh = sb("uxTh", [P, 2, D], F32R)
        uxTl = sb("uxTl", [P, 2, D], F32R)
        hid = sb("hid", [P, 2, H3], F32)
        hTh = sb("hTh", [P, H3], F32R)
        hTl = sb("hTl", [P, H3], F32R)
        yrow = sb("yrow", [P, 2, D], F32)
        early = ExitStack()
        logits = sb("logits", [P, NT, E], F32, early)
        tri = sb("tri", [P, P], BF16, early)
        ones = sb("ones", [P, P], BF16, early)
        pref = sb("pref", [P, E], F32, early)
        upto = sb("upto", [P, E, E], F32, early)
        tile128 = sb("tile128", [P, NT], F32, early)
        unit_no = sb("unit_no", [P, NU], F32, early)
        early.close()
        uv = sb("uv", [P, 2, H], F32)

        ps = stack.enter_context(nc.psum_tensor("ps", [P, 8, BANK], F32))

        def f32(ap):
            return ap.bitcast(F32)

        def sems(name):
            return [sem(name + "_even"), sem(name + "_odd")]

        def before(t):
            return 16 * (t // 2)

        ctx_in = sem("ctx_in")
        wq_in = sem("wq_in")
        wk_in = sem("wk_in")
        wv_in = sem("wv_in")
        wo_in = sem("wo_in")
        small_in = sem("small_in")
        sw_in = sem("sw_in")
        id_ok = sem("id_ok")
        raw2_zero = sem("raw2_zero")
        zeros_ok = sem("zeros_ok")
        kT_zero = sem("kT_zero")
        vT_zero = sem("vT_zero")
        pre_w_hi = sem("pre_w_hi")
        pre_w_lo = sem("pre_w_lo")
        hid_one = sem("hid_one")
        pad2_zero = sem("pad2_zero")
        const_ok = sem("const_ok")
        table_out = sem("table_out")
        pads_out = sem("pads_out")
        pre_pe = sem("pre_pe")
        pre_act = sem("pre_act")
        pre_dve = sem("pre_dve")
        sw_hi = sem("sw_hi")
        sw_lo = sem("sw_lo")
        x_in = sems("x_in")
        xres_in = sems("xres_in")
        st1_ok = sem("st1_ok")
        mv1_ok = sem("mv1_ok")
        eps1_ok = sem("eps1_ok")
        rstd1_ok = sem("rstd1_ok")
        nm1_ok = sem("nm1_ok")
        xn_ok = sem("xn_ok")
        T_ok = sem("T_ok")
        xTh_ok = sem("xTh_ok")
        xTl_ok = sem("xTl_ok")
        S_ok = sem("S_ok")
        max_ok = sem("max_ok")
        nmax_ok = sem("nmax_ok")
        sub_ok = sem("sub_ok")
        exp_ok = sem("exp_ok")
        sum_ok = sem("sum_ok")
        inv_ok = sem("inv_ok")
        norm_ok = sem("norm_ok")
        PT_ok = sem("PT_ok")
        pTh_ok = sem("pTh_ok")
        pTl_ok = sem("pTl_ok")
        O_ok = sem("O_ok")
        xb_ok = sem("xb_ok")
        x2_ok = sem("x2_ok")
        x2_out = sems("x2_out")
        st2_ok = sem("st2_ok")
        mv2_ok = sem("mv2_ok")
        eps2_ok = sem("eps2_ok")
        rstd2_ok = sem("rstd2_ok")
        nm2_ok = sem("nm2_ok")
        xn2_ok = sem("xn2_ok")
        xn2_out = sems("xn2_out")
        T2_ok = sem("T2_ok")
        xn2T_ok = sem("xn2T_ok")
        R_ok = sem("R_ok")
        lg_ok = sem("lg_ok")
        rt = sem("rt")
        rt_sub = sem("rt_sub")
        rt_exp = sem("rt_exp")
        chosen_ok = sem("chosen_ok")
        rank_ok = sem("rank_ok")
        slot_ok = sem("slot_ok")
        eid_ok = sem("eid_ok")
        scat_out = sem("scat_out")
        slots_in = sem("slots_in")
        idx_in_ok = sem("idx_in_ok")
        idx_out_ok = sem("idx_out_ok")
        waited_dve = sem("waited_dve")
        waited_pool = sem("waited_pool")
        raw_in = sem("raw_in")
        w_hi = sem("w_hi")
        w_lo = sem("w_lo")
        w_lo_pool = sem("w_lo_pool")
        b13_in = sem("b13_in")

        class Unit:
            def __init__(self, name):
                self.row_in = sems(name + "_row_in")
                self.X_ok = sem(name + "_X_ok")
                self.xTh_ok = sem(name + "_xTh_ok")
                self.xTl_ok = sem(name + "_xTl_ok")
                self.UV_ok = sem(name + "_UV_ok")
                self.bias_ok = sem(name + "_bias_ok")
                self.z_ok = sem(name + "_z_ok")
                self.h_ok = sem(name + "_h_ok")
                self.H_ok = sem(name + "_H_ok")
                self.hTh_ok = sem(name + "_hTh_ok")
                self.hTl_ok = sem(name + "_hTl_ok")
                self.Y_ok = sem(name + "_Y_ok")
                self.y_ok = sem(name + "_y_ok")
                self.y_out = sems(name + "_y_out")
                self.x2_in = sems(name + "_x2_in")

        sh = Unit("shared")
        ro = Unit("routed")

        def steps(eng, n, lead, lag, body, extra=0, skip=0, begun=None, per=2):
            s0 = (lag + 2) // 2 * 2
            s1 = s0 + (n - lead - s0) // per * per
            for s in range(-lead if begun is None else begun, s0):
                body(s, s % 2, None)

            def loop(start, end, numbered=False):
                with eng.Fori(0, (end - start) // per) as k:
                    for i in range(per):
                        body(per * k + (start + i), i % 2, per // 2 * k + i // 2 if numbered and i % 2 else None)

            if skip:
                loop(s0, s0 + 2 * skip)
            if extra:
                loop(s0 + 2 * skip, s0 + 2 * (skip + extra), True)
            loop(s0 + 2 * (skip + extra), s1)
            for s in range(s1, n + lag):
                body(s, s % 2, None)

        def has(t, n):
            return not isinstance(t, int) or 0 <= t < n

        halves = [(slice(0, DH), 0), (slice(DH, P), 1)]

        plan = [("C", 0, 0), ("C", 0, 1), ("W", 0, 0), ("K", 0, 0)]
        for j in range(NJ):
            plan += [("W", j + 1, 0), ("K", j + 1, 0)] if j + 1 < NJ else [("V", 0, 0)]
            plan += [("A", j, 0), ("A", j, 1)]
        for j in range(NJ):
            plan += [("V", j + 1, 0)] if j + 1 < NJ else []
            plan += [("U", j, 0), ("U", j, 1)]
        number = {what: c for c, what in enumerate(plan)}
        NPRE = len(plan)

        w_plan = [("K", j) for j in range(NJ)] + [(kind, j) for j in range(NJ) for kind in "VO"]
        w_number = {what: c for c, what in enumerate(w_plan)}

        def w_pieces(kind, j, name):
            if kind == "O":
                return [{"raw": wo_raw, "high": woh, "low": wol}[name][:, j, :]]
            w = {"K": {"raw": wk_raw, "high": wkh, "low": wkl}, "V": {"raw": wv_raw, "high": wvh, "low": wvl}}[kind][name]
            return [w[0:n, i, j * P:(j + 1) * P] for i, (_, n) in enumerate(KC)]

        def s_bank(p):
            return (1, 6)[p]


        block = stack.enter_context(nc.Block())

        @block.sync
        def _(sp):
            def tile_step(s, par, _):
                t = s + 3
                if has(t, NT):
                    wait(sp, xn_ok, t - 1)
                    sp.dma_start(xin[:, (par + 1) % 2, :], x_rows[bass.ts(t, P), :]).then_inc(x_in[(par + 1) % 2], 16)
                t = s - 5
                if has(t, NT):
                    wait(sp, xn2_ok, t + 1)
                    sp.dma_start(xn2_dram[bass.ts(t, P), :], xn2[:, (par + 1) % 2, :]).then_inc(xn2_out[(par + 1) % 2], 16)
                t = s - 4
                if has(t, NT):
                    wait(sp, x2_ok, t + 1)
                    sp.dma_start(x2_dram[bass.ts(t, P), :], x2[:, par, :]).then_inc(x2_out[par], 16)
                t = s - 2
                if has(t, NT):
                    wait(sp, x2_ok, t - 1)
                    sp.dma_start(xres[:, par, :], x_rows[bass.ts(t, P), :]).then_inc(xres_in[par], 16)

            for s in (-3, -2):
                tile_step(s, s % 2, None)
            sp.dma_start(ctx_sb[:, :, :], ctx.rearrange("b s c -> (b s) c").rearrange("(r p) c -> p r c", p=P)).then_inc(ctx_in, 16)
            for i, (lo, n) in enumerate(KC):
                sp.dma_start(wk_raw[0:n, i, :], Wk[lo:lo + n, :]).then_inc(wk_in, 16)
            sp.dma_start(wq_sb[:, :, :], Wq.rearrange("(k p) n -> p k n", p=P)).then_inc(wq_in, 16)
            for i, (lo, n) in enumerate(KC):
                sp.dma_start(wv_raw[0:n, i, :], Wv[lo:lo + n, :]).then_inc(wv_in, 16)
            sp.dma_start(wo_raw[:, :, :], Wo.rearrange("(j p) d -> p j d", p=P)).then_inc(wo_in, 16)
            sp.dma_start(ws13[:, :, 0:H], sw1.rearrange("(k p) h -> p k h", p=P)).then_inc(sw_in, 16)
            sp.dma_start(ws13[:, :, H:2 * H], sw3.rearrange("(k p) h -> p k h", p=P)).then_inc(sw_in, 16)
            sp.wait_ge(raw2_zero, 1)
            sp.dma_start(ws2[:, 0:KH - 1, :], sw2[0:(KH - 1) * P, :].rearrange("(c p) d -> p c d", p=P)).then_inc(sw_in, 16)
            sp.dma_start(ws2[0:HR, KH - 1, :], sw2[(KH - 1) * P:H, :]).then_inc(sw_in, 16)
            sp.dma_start(ws2[HR:HR + 1, KH - 1, :], sb2.rearrange("(a d) -> a d", a=1)).then_inc(sw_in, 16)
            tile_step(-1, 1, None)
            sp.wait_ge(pre_pe, NPRE)
            sp.wait_ge(pre_dve, NPRE)
            steps(sp, NT, 3, 5, tile_step, begun=0, per=6)

            for half in xn2_out + x2_out:
                sp.wait_ge(half, before(NT))
            sp.wait_ge(O_ok, NT)
            sp.wait_ge(lg_ok, NT)
            sp.wait_ge(x2_ok, NT)
            sp.dma_start(b13[:, :, 0:H], b1.rearrange("(a e) h -> a e h", a=1).to_broadcast([P, E, H])).then_inc(b13_in, 16)
            sp.dma_start(b13[:, :, H:2 * H], b3.rearrange("(a e) h -> a e h", a=1).to_broadcast([P, E, H])).then_inc(b13_in, 16)

            def shared_step(s, par, e):
                t = s + 2
                if has(t, NT):
                    wait(sp, sh.X_ok, t - 1)
                    sp.dma_start(xrow[:, par, :], xn2_dram[bass.ts(t, P), :]).then_inc(sh.row_in[par], 16)
                t = s - 4
                if has(t, NT):
                    wait(sp, sh.y_ok, t + 1)
                    sp.dma_start(out[bass.ts(t, P), :], yrow[:, par, :]).then_inc(sh.y_out[par], 16)
                t = s - 2
                if has(t, NT):
                    wait(sp, sh.y_ok, t - 1)
                    sp.dma_start(x2row[:, par, :], x2_dram[bass.ts(t, P), :]).then_inc(sh.x2_in[par], 16)
                if e is not None:
                    one = bass.ds(e, 1)
                    sp.dma_start(w13_raw[:, one, :, 0:H], w1[one, :, :].rearrange("e (k p) h -> p e k h", p=P)).then_inc(raw_in, 16)
                    sp.dma_start(w13_raw[:, one, :, H:2 * H], w3[one, :, :].rearrange("e (k p) h -> p e k h", p=P)).then_inc(raw_in, 16)
                    sp.dma_start(w2_raw[:, one, 0:KH - 1, :], w2[one, 0:(KH - 1) * P, :].rearrange("e (c p) d -> p e c d", p=P)).then_inc(raw_in, 16)
                    sp.dma_start(w2_raw[0:HR, one, KH - 1, :], w2[one, (KH - 1) * P:H, :].rearrange("e p d -> p e d")).then_inc(raw_in, 16)
                    sp.dma_start(w2_raw[HR:HR + 1, one, KH - 1, :], b2[one, :].rearrange("e (a d) -> a e d", a=1)).then_inc(raw_in, 16)

            sp.wait_ge(eid_ok, 1)
            sp.wait_ge(pad2_zero, 1)
            steps(sp, NT, 2, 4, shared_step, extra=E, per=4)

            sp.wait_ge(scat_out, 16 * TOP * NT)
            sp.dma_start(slots[:, :, :], slots_dram.rearrange("(p n) c -> p n c", p=P)).then_inc(slots_in, 16)
            sp.wait_ge(ro.y_out[0], before(NU + 1))
            sp.wait_ge(ro.y_out[1], before(NU))

        @block.gpsimd
        def _(pool):
            pool.memset(ident[:, :], 0.0).then_inc(id_ok, 1)
            pool.wait_ge(id_ok, 1)
            pool.affine_select(out=ident[:, :], in_=ident[:, :], compare_op=ALU.not_equal, fill=1.0, base=0,
                               pattern=[[-1, P]], channel_multiplier=1).then_inc(id_ok, 1)
            pool.memset(ws2[:, KH - 1, :], 0.0).then_inc(raw2_zero, 1)
            pool.memset(zeros[:, :], 0.0).then_inc(zeros_ok, 1)
            pool.memset(minus_half[:, :], -0.5).then_inc(const_ok, 1)
            pool.memset(eps[:, :], LN_EPS).then_inc(const_ok, 1)
            pool.iota(record[:, :, :, 0], pattern=[[P, NT], [0, TOP]], base=0, channel_multiplier=1).then_inc(const_ok, 1)
            pool.memset(slots[:, :, 1], 0).then_inc(const_ok, 1)
            pool.iota(slots[:, :, 0], pattern=[[0, NU]], base=T, channel_multiplier=1).then_inc(const_ok, 1)
            pool.wait_ge(const_ok, 5)
            pool.dma_start(slots_dram.rearrange("(p n) c -> p n c", p=P), slots[:, :, :]).then_inc(table_out, 16)
            def tile_step(s, par, _):
                t = s + 1
                if has(t, NT):
                    p = (par + 1) % 2
                    wait(pool, mv1_ok, t + 1)
                    wait(pool, nm1_ok, t - 1)
                    wait(pool, xn_ok, t - 1)
                    pool.tensor_tensor(rs1[:, p, 0:1], mv1[:, p, 1:2], eps[:, :], ALU.add).then_inc(eps1_ok, 1)
                    wait(pool, eps1_ok, t + 1)
                    pool.tensor_tensor(rs1[:, p, 1:2], rs1[:, p, 0:1], minus_half[:, :], ALU.pow).then_inc(rstd1_ok, 1)
                t = s - 5
                if has(t, NT):
                    p = (par + 1) % 2
                    wait(pool, mv2_ok, t + 1)
                    wait(pool, nm2_ok, t - 1)
                    wait(pool, xn2_ok, t - 1)
                    pool.tensor_tensor(rs2[:, p, 0:1], mv2[:, p, 1:2], eps[:, :], ALU.add).then_inc(eps2_ok, 1)
                    wait(pool, eps2_ok, t + 1)
                    pool.tensor_tensor(rs2[:, p, 1:2], rs2[:, p, 0:1], minus_half[:, :], ALU.pow).then_inc(rstd2_ok, 1)
                t = s - 2
                if has(t, NT):
                    p = par
                    wait(pool, inv_ok, t + 1)
                    heads = prob[:, p, :].rearrange("p (h k) -> p h k", k=NK)
                    pool.tensor_tensor(heads, heads, hinv[:, p, :].unsqueeze(2).to_broadcast([P, HEADS, NK]),
                                       ALU.mult).then_inc(norm_ok, 1)
                t = s - 3
                if has(t, NT):
                    p = (par + 1) % 2
                    wait(pool, xres_in[p], before(t) + 16)
                    pool.tensor_tensor(xres[:, p, :], xres[:, p, :], bo_bc[:, :], ALU.add).then_inc(xb_ok, 1)

            tile_step(-1, 1, None)
            for c, (kind, j) in enumerate(w_plan):
                pool.wait_ge(pre_w_hi, c + 1)
                for low, raw, high in zip(*(w_pieces(kind, j, name) for name in ("low", "raw", "high"))):
                    last = pool.tensor_tensor(low, raw, f32(high), ALU.subtract)
                last.then_inc(pre_w_lo, 1)
            pool.wait_ge(small_in, 96)
            pool.wait_ge(pre_pe, NPRE)
            pool.wait_ge(pre_act, NPRE)
            pool.wait_ge(pre_dve, NPRE)
            pool.memset(ones[:, :], 1.0).then_inc(const_ok, 1)
            pool.memset(tri[:, :], 1.0).then_inc(const_ok, 1)
            pool.memset(upto[:, :, :], 1.0).then_inc(const_ok, 1)
            pool.iota(pref[:, :], pattern=[[-1, E]], base=E, channel_multiplier=0, allow_small_or_imprecise_dtypes=True).then_inc(const_ok, 1)
            pool.iota(tile128[:, :], pattern=[[P, NT]], base=0, channel_multiplier=0, allow_small_or_imprecise_dtypes=True).then_inc(const_ok, 1)
            pool.iota(unit_no[:, :], pattern=[[1, NU]], base=0, channel_multiplier=0, allow_small_or_imprecise_dtypes=True).then_inc(const_ok, 1)
            pool.wait_ge(const_ok, 11)
            pool.affine_select(out=tri[:, :], in_=tri[:, :], compare_op=ALU.is_gt, fill=0.0, base=0,
                               pattern=[[1, P]], channel_multiplier=-1).then_inc(const_ok, 1)
            pool.affine_select(out=upto[:, :, :], in_=upto[:, :, :], compare_op=ALU.is_ge, fill=0.0, base=0,
                               pattern=[[1, E], [-1, E]], channel_multiplier=0).then_inc(const_ok, 1)
            steps(pool, NT, 1, 5, tile_step, begun=0, per=6)

            for half in xn2_out + x2_out:
                pool.wait_ge(half, before(NT))
            pool.wait_ge(O_ok, NT)
            pool.wait_ge(lg_ok, NT)
            pool.memset(w2_raw[:, :, KH - 1, :], 0.0).then_inc(pad2_zero, 1)
            pool.memset(yrow[:, 0, :], 0.0).then_inc(hid_one, 1)
            pool.memset(hid[:, :, H:H3], 0.0).then_inc(hid_one, 1)
            pool.wait_ge(hid_one, 2)
            pool.memset(hid[:, :, H:H + 1], 1.0).then_inc(hid_one, 1)
            pool.dma_start(xn2_dram[T:T + PADS, :], yrow[:, 0, :]).then_inc(pads_out, 16)
            pool.dma_start(out[T:T + PADS, :], yrow[:, 0, :]).then_inc(pads_out, 16)

            pool.wait_ge(table_out, 16)
            pool.wait_ge(slot_ok, 1)
            for t in range(NT):
                for k in range(TOP):
                    pool.indirect_dma_start(slots_dram, bass.IndirectOffsetOnAxis(ap=slot[:, k, t:t + 1], axis=0),
                                            record[:, t, k, :], None).then_inc(scat_out, 16)
            with pool.Fori(E_DVE, E) as e:
                one = bass.ds(e, 1)
                wait(pool, w_hi, 3 * e + 3)
                for k in range(KD):
                    pool.tensor_tensor(w13l[:, one, k, :], w13_raw[:, one, k, :], f32(w13h[:, one, k, :]),
                                       ALU.subtract).then_inc(w_lo_pool, 1)
                flat = [a[:, one, :, :].rearrange("p e c d -> p (e c d)") for a in (w2l, w2_raw, w2h)]
                pool.tensor_tensor(flat[0], flat[1], f32(flat[2]), ALU.subtract).then_inc(w_lo_pool, 1)
            pool.wait_ge(pads_out, 32)
            pool.wait_ge(slots_in, 16)
            pool.wait_ge(sh.X_ok, NT)

            def routed_step(s, par, _):
                t = s - 4
                if has(t, NU):
                    p = par
                    if isinstance(t, int) and t == 0:
                        for half in sh.y_out:
                            pool.wait_ge(half, before(NT))
                    wait(pool, ro.y_out[1 - p], before(t + 1))
                    pool.tensor_copy(idx_out[:, p, :], slots[:, bass.ds(t, 1), 0]).then_inc(idx_out_ok, 1)
                    wait(pool, idx_out_ok, t + 1)
                    wait(pool, ro.y_ok, t + 1)
                    pool.sem_inc(waited_pool, 1)
                    pool.indirect_dma_start(out, bass.IndirectOffsetOnAxis(ap=idx_out[:, p, :], axis=0),
                                            yrow[:, p, :], None, compute_op=ALU.add).then_inc(ro.y_out[p], 16)
                t = s + 2
                if has(t, NU):
                    p = par
                    wait(pool, ro.row_in[p], before(t))
                    pool.tensor_copy(idx_in[:, p, :], slots[:, bass.ds(t, 1), 0]).then_inc(idx_in_ok, 1)
                    wait(pool, idx_in_ok, t + 1)
                    wait(pool, ro.X_ok, t - 1)
                    pool.sem_inc(waited_pool, 1)
                    pool.indirect_dma_start(xrow[:, p, :], None, xn2_dram,
                                            bass.IndirectOffsetOnAxis(ap=idx_in[:, p, :], axis=0)).then_inc(ro.row_in[p], 16)

            steps(pool, NU, 2, 4, routed_step, per=4)

        @block.scalar
        def _(act):
            act.dma_start(bo_bc[:, :], bo.rearrange("(a d) -> a d", a=1).to_broadcast([P, D])).then_inc(small_in, 16)
            act.dma_start(gateb_bc[:, :], gate_b.rearrange("(a d) -> a d", a=1).to_broadcast([P, E])).then_inc(small_in, 16)
            for k in range(KD):
                act.dma_start(gateT[:, k, :], gate_w[:, k * P:(k + 1) * P].rearrange("e p -> p e"),
                              allow_slow_non_contiguous=True).then_inc(small_in, 16)
            act.dma_start(bs13[:, 0:H], sb1.rearrange("(a d) -> a d", a=1).to_broadcast([P, H])).then_inc(small_in, 16)
            act.dma_start(bs13[:, H:2 * H], sb3.rearrange("(a d) -> a d", a=1).to_broadcast([P, H])).then_inc(small_in, 16)

            def tile_step(s, par, _):
                t = s - 6
                if has(t, NT):
                    p = par
                    wait(act, T2_ok, t + 1)
                    wait(act, R_ok, t - 1)
                    act.activation(xn2T[:, p, :], ps[:, 0, 0:D], ACT.Copy).then_inc(xn2T_ok, 1)
                t = s - 5
                if has(t, NT):
                    p = (par + 1) % 2
                    wait(act, nm2_ok, t + 1)
                    wait(act, T2_ok, t - 1)
                    wait(act, xn2_out[p], before(t))
                    act.activation(xn2[:, p, :], x2[:, p, :], ACT.Identity, bias=nm2[:, p, :],
                                   scale=rs2[:, p, 1:2]).then_inc(xn2_ok, 1)
                t = s + 1
                if has(t, NT):
                    p = (par + 1) % 2
                    wait(act, nm1_ok, t + 1)
                    wait(act, T_ok, t - 1)
                    act.activation(xn[:, p, :], xin[:, p, :], ACT.Identity, bias=nm1[:, p, :],
                                   scale=rs1[:, p, 1:2]).then_inc(xn_ok, 1)
                t = s
                if has(t, NT):
                    p = par
                    wait(act, T_ok, t + 1)
                    wait(act, S_ok, t - 1)
                    act.activation(xTh[:, p, :], ps[:, 0, 0:D], ACT.Copy).then_inc(xTh_ok, 1)
                t = s - 3
                if has(t, NT):
                    p = (par + 1) % 2
                    wait(act, O_ok, t - 1)
                    for h in range(2):
                        wait(act, PT_ok, 2 * t + h + 1)
                        act.activation(pTh[:, p, h * BANK:(h + 1) * BANK], ps[:, 3 + h, :], ACT.Copy).then_inc(pTh_ok, 1)
                t = s - 1
                if has(t, NT):
                    p = (par + 1) % 2
                    wait(act, nmax_ok, t + 1)
                    wait(act, inv_ok, t - 1)
                    wait(act, PT_ok, 2 * t - 2)
                    for h in range(HS, HEADS):
                        act.activation(prob[:, p, h * NK:(h + 1) * NK], ps[:, s_bank(p) + h // 8, h % 8 * NK:(h % 8 + 1) * NK],
                                       ACT.Exp, bias=nmax[:, p, h - HS:h - HS + 1], scale=SCALE,
                                       accum_out=hsum[:, p, h:h + 1])
                    wait(act, sub_ok, t + 1)
                    act.activation(prob[:, p, 0:HS * NK], prob[:, p, 0:HS * NK], ACT.Exp, scale=SCALE).then_inc(exp_ok, 1)

            tile_step(-1, 1, None)
            def leave(c, out, in_):
                act.wait_ge(pre_pe, c + 1)
                return act.activation(out, in_, ACT.Copy)

            def high(kind, j):
                if j < NJ:
                    for sem_in, n in {"K": ((wk_in, 32),), "V": ((wv_in, 32),), "O": ((wo_in, 16),)}[kind]:
                        act.wait_ge(sem_in, n)
                    for out_, in_ in zip(w_pieces(kind, j, "high"), w_pieces(kind, j, "raw")):
                        last = act.activation(out_, in_, ACT.Copy)
                    last.then_inc(pre_w_hi, 1)

            for c, (kind, j, i) in enumerate(plan):
                bank = ps[:, c % 8, :]
                if kind == "C":
                    n = KC[i][1]
                    leave(c, ctxTh[0:n, i, :], ps[0:n, c % 8, 0:BK]).then_inc(pre_act, 1)
                    if i == 1:
                        high("K", 0)
                elif kind == "W":
                    high("K", j + 1)
                    if j == NJ - 1:
                        high("V", 0)
                        high("O", 0)
                    leave(c, wqTh[:, j % 2, :], bank[:, 0:D]).then_inc(pre_act, 1)
                elif kind == "K":
                    if j == 0:
                        act.wait_ge(kT_zero, 2)
                    for half, r in halves:
                        last = leave(c, kTh[half, j % 2, r, :], ps[half, c % 8, 0:BK])
                    last.then_inc(pre_act, 1)
                elif kind == "A":
                    for r in range(2):
                        last = leave(c, Ah[:, :, i, (2 * j + r) * NK:(2 * j + r + 1) * NK],
                                     bank[:, r * BK:(r + 1) * BK].rearrange("p (b n) -> p b n", b=B))
                    last.then_inc(pre_act, 1)
                elif kind == "V":
                    high("V", j + 1)
                    high("O", j + 1)
                    if j == 0:
                        act.wait_ge(vT_zero, 2)
                    for half, r in halves:
                        last = leave(c, vTh[half, j % 2, :, r, :],
                                     ps[half, c % 8, 0:BK].rearrange("p (b n) -> p b n", b=B))
                    last.then_inc(pre_act, 1)
                else:
                    leave(c, Uh[:, 2 * i:2 * i + 2, j, :], bank.rearrange("p (b d) -> p b d", b=2)).then_inc(pre_act, 1)
            act.wait_ge(pre_pe, NPRE)
            act.wait_ge(pre_dve, NPRE)
            act.wait_ge(small_in, 96)
            tile_step(0, 0, None)
            act.wait_ge(sw_in, 80)
            act.activation(ws13h[:, :, :], ws13[:, :, :], ACT.Copy).then_inc(sw_hi, 1)
            act.activation(ws2h[:, :, :], ws2[:, :, :], ACT.Copy).then_inc(sw_hi, 1)
            steps(act, NT, 1, 6, tile_step, begun=1, per=6)

            act.wait_ge(rt_sub, 1)
            act.activation(score[:, :, :], mA[:, :, :], ACT.Exp).then_inc(rt_exp, 1)

            def unit_step(u, n, s, par, routed):
                t = s - 4
                if has(t, n) and routed:
                    p = par
                    if isinstance(t, int) and t == 0:
                        act.wait_ge(slots_in, 16)
                        for half in sh.y_out:
                            act.wait_ge(half, before(NT))
                    wait(act, u.Y_ok, t + 1)
                    wait(act, u.y_out[p], before(t))
                    act.activation(yrow[:, p, :], ps[:, 6 + p, 0:D], ACT.Copy,
                                   scale=slots[:, bass.ds(t, 1), 1].bitcast(F32)).then_inc(u.y_ok, 1)
                t = s
                if has(t, n):
                    p = par
                    wait(act, u.X_ok, t + 1)
                    wait(act, u.UV_ok, t - 1)
                    act.activation(uxTh[:, p, :], ps[:, 0, 0:D], ACT.Copy).then_inc(u.xTh_ok, 1)
                t = s - 3
                if has(t, n):
                    wait(act, u.H_ok, t + 1)
                    wait(act, u.Y_ok, t)
                    act.activation(hTh[:, :], ps[:, 5, 0:H3], ACT.Copy).then_inc(u.hTh_ok, 1)
                t = s - 2
                if has(t, n):
                    p = par
                    wait(act, u.z_ok, t + 1)
                    act.activation(hid[:, p, 0:H], hid[:, p, 0:H], ACT.Silu).then_inc(u.h_ok, 1)

            def shared_step(s, par, e):
                unit_step(sh, NT, s, par, False)
                if e is not None:
                    wait(act, raw_in, 80 * e + 80)
                    for k in range(KD):
                        act.activation(w13h[:, bass.ds(e, 1), k, :], w13_raw[:, bass.ds(e, 1), k, :], ACT.Copy).then_inc(w_hi, 1)
                    high, raw = [a[:, bass.ds(e, 1), :, :].rearrange("p e c d -> p (e c d)") for a in (w2h, w2_raw)]
                    act.activation(high, raw, ACT.Copy).then_inc(w_hi, 1)

            act.wait_ge(lg_ok, NT)
            act.wait_ge(hid_one, 3)
            steps(act, NT, 0, 4, shared_step, extra=E, skip=2, per=4)
            steps(act, NU, 0, 4, lambda s, par, _: unit_step(ro, NU, s, par, True), per=4)

        @block.vector
        def _(dve):
            def heads(ap):
                return ap.rearrange("p (h k) -> p h k", k=NK)

            def tile_step(s, par, _):
                t = s - 2
                if has(t, NT):
                    p = par
                    wait(dve, exp_ok, t + 1)
                    dve.tensor_reduce(hsum[:, p, 0:HS], heads(prob[:, p, 0:HS * NK]), AX.X, ALU.add).then_inc(sum_ok, 1)
                    wait(dve, sum_ok, t + 1)
                    wait(dve, norm_ok, t - 1)
                    dve.reciprocal(hinv[:, p, :], hsum[:, p, :]).then_inc(inv_ok, 1)
                t = s - 5
                if has(t, NT):
                    p = (par + 1) % 2
                    wait(dve, rstd2_ok, t + 1)
                    wait(dve, xn2_ok, t - 1)
                    dve.scalar_tensor_tensor(out=nm2[:, p, :], in0=mv2[:, p, 0:1], scalar=-1.0, in1=rs2[:, p, 1:2],
                                             op0=ALU.mult, op1=ALU.mult).then_inc(nm2_ok, 1)
                t = s + 1
                if has(t, NT):
                    p = (par + 1) % 2
                    wait(dve, rstd1_ok, t + 1)
                    wait(dve, xn_ok, t - 1)
                    dve.scalar_tensor_tensor(out=nm1[:, p, :], in0=mv1[:, p, 0:1], scalar=-1.0, in1=rs1[:, p, 1:2],
                                             op0=ALU.mult, op1=ALU.mult).then_inc(nm1_ok, 1)
                t = s - 6
                if has(t, NT):
                    wait(dve, R_ok, t + 1)
                    dve.tensor_copy(logits[:, bass.ds(t, 1), :].rearrange("p a e -> p (a e)"), ps[:, 0, 0:E]).then_inc(lg_ok, 1)
                t = s + 2
                if has(t, NT):
                    p = par
                    wait(dve, x_in[p], before(t) + 16)
                    dve.bn_stats(st1[:, p, :], xin[:, p, :]).then_inc(st1_ok, 1)
                    wait(dve, st1_ok, t + 1)
                    wait(dve, rstd1_ok, t - 1)
                    dve.sem_inc(waited_dve, 1)
                    dve.bn_aggr(mv1[:, p, :], st1[:, p, :]).then_inc(mv1_ok, 1)
                t = s - 1
                if has(t, NT):
                    p = (par + 1) % 2
                    wait(dve, S_ok, t + 1)
                    scores = ps[:, s_bank(p):s_bank(p) + 2, :].rearrange("p a (h k) -> p (a h) k", k=NK)
                    dve.tensor_reduce(hmax[:, p, :], scores, AX.X, ALU.max).then_inc(max_ok, 1)
                    wait(dve, max_ok, t + 1)
                    wait(dve, exp_ok, t - 1)
                    dve.tensor_scalar(nmax[:, p, :], hmax[:, p, HS:HEADS], -SCALE, None, ALU.mult).then_inc(nmax_ok, 1)
                    wait(dve, PT_ok, 2 * t - 2)
                    dve.tensor_tensor(heads(prob[:, p, 0:HS * NK]), scores[:, 0:HS, :],
                                      hmax[:, p, 0:HS].unsqueeze(2).to_broadcast([P, HS, NK]),
                                      ALU.subtract).then_inc(sub_ok, 1)
                t = s
                if has(t, NT):
                    p = par
                    wait(dve, xTh_ok, t + 1)
                    wait(dve, S_ok, t - 1)
                    dve.tensor_tensor(xTl[:, p, :], ps[:, 0, 0:D], f32(xTh[:, p, :]), ALU.subtract).then_inc(xTl_ok, 1)
                t = s - 3
                if has(t, NT):
                    p = (par + 1) % 2
                    for h in range(2):
                        cols = slice(h * BANK, (h + 1) * BANK)
                        wait(dve, pTh_ok, 2 * t + h + 1)
                        dve.tensor_tensor(pTl[:, p, cols], ps[:, 3 + h, :], f32(pTh[:, p, cols]),
                                          ALU.subtract).then_inc(pTl_ok, 1)
                t = s - 4
                if has(t, NT):
                    p = par
                    wait(dve, O_ok, t + 1)
                    wait(dve, xb_ok, t + 1)
                    wait(dve, x2_out[p], before(t))
                    wait(dve, xn2_ok, t - 1)
                    dve.tensor_tensor(x2[:, p, :], ps[:, 5, 0:D], xres[:, p, :], ALU.add).then_inc(x2_ok, 1)
                    wait(dve, x2_ok, t + 1)
                    dve.bn_stats(st2[:, p, :], x2[:, p, :]).then_inc(st2_ok, 1)
                    wait(dve, st2_ok, t + 1)
                    wait(dve, rstd2_ok, t - 1)
                    dve.sem_inc(waited_dve, 1)
                    dve.bn_aggr(mv2[:, p, :], st2[:, p, :]).then_inc(mv2_ok, 1)

            for s in (-2, -1):
                tile_step(s, s % 2, None)
            dve.wait_ge(zeros_ok, 1)
            for k in (kTh, kTl):
                dve.tensor_copy(k[:, :, :, :].rearrange("p a r n -> p (a r n)"), zeros[:, :]).then_inc(kT_zero, 1)
            for v in (vTh, vTl):
                dve.tensor_copy(v[:, :, :, :, :].rearrange("p a b r n -> p (a b r n)"), zeros[:, :]).then_inc(vT_zero, 1)
            dve.wait_ge(kT_zero, 2)
            dve.wait_ge(vT_zero, 2)
            for c, (kind, j, i) in enumerate(plan):
                bank = ps[:, c % 8, :]
                dve.wait_ge(pre_act, c + 1)
                if kind == "C":
                    n = KC[i][1]
                    last = dve.tensor_tensor(ctxTl[0:n, i, :], ps[0:n, c % 8, 0:BK], f32(ctxTh[0:n, i, :]), ALU.subtract)
                elif kind == "W":
                    last = dve.tensor_tensor(wqTl[:, j % 2, :], bank[:, 0:D], f32(wqTh[:, j % 2, :]), ALU.subtract)
                elif kind == "K":
                    for half, r in halves:
                        last = dve.tensor_tensor(kTl[half, j % 2, r, :], ps[half, c % 8, 0:BK],
                                                 f32(kTh[half, j % 2, r, :]), ALU.subtract)
                elif kind == "A":
                    for r in range(2):
                        cols = slice((2 * j + r) * NK, (2 * j + r + 1) * NK)
                        last = dve.tensor_tensor(Al[:, :, i, cols],
                                                 bank[:, r * BK:(r + 1) * BK].rearrange("p (b n) -> p b n", b=B),
                                                 f32(Ah[:, :, i, cols]), ALU.subtract)
                elif kind == "V":
                    for half, r in halves:
                        last = dve.tensor_tensor(vTl[half, j % 2, :, r, :],
                                                 ps[half, c % 8, 0:BK].rearrange("p (b n) -> p b n", b=B),
                                                 f32(vTh[half, j % 2, :, r, :]), ALU.subtract)
                else:
                    last = dve.tensor_tensor(Ul[:, 2 * i:2 * i + 2, j, :], bank.rearrange("p (b d) -> p b d", b=2),
                                             f32(Uh[:, 2 * i:2 * i + 2, j, :]), ALU.subtract)
                last.then_inc(pre_dve, 1)
            dve.wait_ge(pre_pe, NPRE)
            dve.wait_ge(pre_act, NPRE)
            tile_step(0, 0, None)
            dve.wait_ge(sw_hi, 1)
            dve.tensor_tensor(ws13l[:, :, :], ws13[:, :, :], f32(ws13h[:, :, :]), ALU.subtract).then_inc(sw_lo, 1)
            dve.wait_ge(sw_hi, 2)
            dve.tensor_tensor(ws2l[:, :, :], ws2[:, :, :], f32(ws2h[:, :, :]), ALU.subtract).then_inc(sw_lo, 1)
            steps(dve, NT, 2, 6, tile_step, begun=1, per=6)

            linked = [0]

            def link(ins):
                linked[0] += 1
                ins.then_inc(rt, 1)
                dve.wait_ge(rt, linked[0])

            def over_e(ap):
                return ap.unsqueeze(2).to_broadcast([P, NT, E])

            dve.wait_ge(lg_ok, NT)
            dve.wait_ge(O_ok, NT)
            dve.wait_ge(const_ok, 13)
            link(dve.tensor_reduce(v32[:, 0, :], logits[:, :, :], AX.X, ALU.max))
            dve.tensor_tensor(mA[:, :, :], logits[:, :, :], over_e(v32[:, 0, :]), ALU.subtract).then_inc(rt_sub, 1)
            dve.wait_ge(rt_exp, 1)
            link(dve.tensor_reduce(v32[:, 1, :], score[:, :, :], AX.X, ALU.add))
            link(dve.reciprocal(v32[:, 2, :], v32[:, 1, :]))
            link(dve.tensor_tensor(score[:, :, :], score[:, :, :], over_e(v32[:, 2, :]), ALU.mult))
            link(dve.tensor_tensor(biased[:, :, :], score[:, :, :],
                                   gateb_bc[:, :].unsqueeze(1).to_broadcast([P, NT, E]), ALU.add))
            for k, mark in enumerate((first, second)):
                link(dve.tensor_reduce(v32[:, 3, :], biased[:, :, :], AX.X, ALU.max))
                link(dve.tensor_tensor(mA[:, :, :], biased[:, :, :], over_e(v32[:, 3, :]), ALU.is_ge))
                link(dve.tensor_tensor(mA[:, :, :], mA[:, :, :],
                                       pref[:, :].unsqueeze(1).to_broadcast([P, NT, E]), ALU.mult))
                link(dve.tensor_reduce(v32[:, 3, :], mA[:, :, :], AX.X, ALU.max))
                link(dve.tensor_tensor(mark[:, :, :], mA[:, :, :], over_e(v32[:, 3, :]), ALU.is_equal))
                if k == 0:
                    link(dve.scalar_tensor_tensor(out=biased[:, :, :], in0=mark[:, :, :], scalar=LOWEST,
                                                  in1=biased[:, :, :], op0=ALU.mult, op1=ALU.add))
            dve.tensor_tensor(chosen[:, :, :], first[:, :, :], second[:, :, :], ALU.add).then_inc(chosen_ok, 1)
            for k, mark in enumerate((first, second)):
                link(dve.tensor_tensor(mA[:, :, :], mark[:, :, :], score[:, :, :], ALU.mult))
                link(dve.tensor_reduce(record[:, :, k, 1].bitcast(F32), mA[:, :, :], AX.X, ALU.add))
            dve.wait_ge(rank_ok, 2)
            rows = v32[:, 4, 0:E]
            tiles = v32[:, 4, E:2 * E]
            ends = v32[:, 4, 2 * E:3 * E]
            begin = v32[:, 4, 3 * E:4 * E]
            link(dve.tensor_reduce(rows, ps[:, 1, 0:NT * E].rearrange("p (t e) -> p e t", e=E), AX.X, ALU.add))
            link(dve.tensor_tensor(mA[:, :, :].rearrange("p t e -> p (t e)").rearrange("p (e t) -> p e t", e=E),
                                   rows.unsqueeze(2).to_broadcast([P, E, NT]),
                                   tile128[:, :].unsqueeze(1).to_broadcast([P, E, NT]), ALU.is_gt))
            link(dve.tensor_reduce(tiles, mA[:, :, :].rearrange("p t e -> p (t e)").rearrange("p (e t) -> p e t", e=E),
                                   AX.X, ALU.add))
            ee = mB[:, 0:E, :]
            link(dve.tensor_tensor(ee, upto[:, :, :], tiles.unsqueeze(1).to_broadcast([P, E, E]), ALU.mult))
            link(dve.tensor_reduce(ends, ee, AX.X, ALU.add))
            link(dve.tensor_tensor(begin, ends, tiles, ALU.subtract))
            link(dve.scalar_tensor_tensor(out=slot8[:, :, :], in0=begin.unsqueeze(1).to_broadcast([P, NT, E]),
                                          scalar=float(P), in1=ps[:, 0, 0:NT * E].rearrange("p (t e) -> p t e", e=E),
                                          op0=ALU.mult, op1=ALU.add))
            for k, mark in enumerate((first, second)):
                link(dve.tensor_tensor(mA[:, :, :], mark[:, :, :], slot8[:, :, :], ALU.mult))
                link(dve.tensor_reduce(v32[:, 5 + k, :], mA[:, :, :], AX.X, ALU.add))
            link(dve.tensor_copy(slot[:, :, :], v32[:, 5:5 + TOP, :]))
            link(dve.tensor_scalar(slot_col[:, :, :], slot[:, :, :], 7, None, ALU.logical_shift_right))
            link(dve.tensor_scalar(slot_row[:, :, :], slot[:, :, :], P - 1, None, ALU.bitwise_and))
            dve.scalar_tensor_tensor(out=slot[:, :, :], in0=slot_row[:, :, :], scalar=float(NU), in1=slot_col[:, :, :],
                                     op0=ALU.mult, op1=ALU.add).then_inc(slot_ok, 1)
            link(dve.tensor_tensor(big[:, :, :], unit_no[:, :].unsqueeze(2).to_broadcast([P, NU, E]),
                                   ends.unsqueeze(1).to_broadcast([P, NU, E]), ALU.is_ge))
            passed = mB[:, :, :].rearrange("p t e -> p (t e)")[:, 0:NU]
            link(dve.tensor_reduce(passed, big[:, :, :], AX.X, ALU.add))
            link(dve.tensor_scalar(expert_of[:, :], passed, float(E - 1), None, ALU.min))
            link(dve.memset(step_experts[:, :], 0))
            link(dve.tensor_copy(step_experts[:, 1:1 + NU], expert_of[:, :]))
            dve.scalar_tensor_tensor(out=step_experts[:, 4:4 + NU], in0=expert_of[:, :], scalar=float(E),
                                     in1=step_experts[:, 4:4 + NU], op0=ALU.mult, op1=ALU.add).then_inc(eid_ok, 1)

            def unit_step(u, n, s, par, routed):
                t = s - 4
                if has(t, n) and not routed:
                    p = par
                    wait(dve, u.Y_ok, t + 1)
                    wait(dve, u.x2_in[p], before(t) + 16)
                    wait(dve, u.y_out[p], before(t))
                    dve.tensor_tensor(yrow[:, p, :], ps[:, 6 + p, 0:D], x2row[:, p, :], ALU.add).then_inc(u.y_ok, 1)
                t = s
                if has(t, n):
                    p = par
                    wait(dve, u.xTh_ok, t + 1)
                    wait(dve, u.UV_ok, t - 1)
                    dve.tensor_tensor(uxTl[:, p, :], ps[:, 0, 0:D], f32(uxTh[:, p, :]), ALU.subtract).then_inc(u.xTl_ok, 1)
                t = s - 3
                if has(t, n):
                    wait(dve, u.hTh_ok, t + 1)
                    wait(dve, u.Y_ok, t)
                    dve.tensor_tensor(hTl[:, :], ps[:, 5, 0:H3], f32(hTh[:, :]), ALU.subtract).then_inc(u.hTl_ok, 1)
                t = s - 1
                if has(t, n):
                    p = (par + 1) % 2
                    if routed:
                        e = dve.value_load(expert_of[0:1, bass.ds(t, 1)], min_val=0, max_val=E - 1)
                        bias = b13[:, bass.ds(e, 1), :].rearrange("p e (a h) -> p (e a) h", a=2)
                    else:
                        bias = bs13[:, :].rearrange("p (a h) -> p a h", a=2)
                    wait(dve, u.UV_ok, t + 1)
                    wait(dve, u.z_ok, t)
                    dve.tensor_tensor(uv[:, :, :], ps[:, 1 + 2 * p:3 + 2 * p, 0:H], bias, ALU.add).then_inc(u.bias_ok, 1)
                    wait(dve, u.bias_ok, t + 1)
                    wait(dve, u.H_ok, t - 1)
                    dve.tensor_tensor(hid[:, p, 0:H], uv[:, 0, :], uv[:, 1, :], ALU.mult).then_inc(u.z_ok, 1)

            def shared_step(s, par, e):
                unit_step(sh, NT, s, par, False)
                if e is not None:
                    for k in range(KD):
                        wait(dve, w_hi, 3 * e + k + 1)
                        dve.tensor_tensor(w13l[:, bass.ds(e, 1), k, :], w13_raw[:, bass.ds(e, 1), k, :],
                                          f32(w13h[:, bass.ds(e, 1), k, :]), ALU.subtract).then_inc(w_lo, 1)
                    wait(dve, w_hi, 3 * e + 3)
                    flat = [a[:, bass.ds(e, 1), :, :].rearrange("p e c d -> p (e c d)") for a in (w2l, w2_raw, w2h)]
                    dve.tensor_tensor(flat[0], flat[1], f32(flat[2]),
                                      ALU.subtract).then_inc(w_lo, 1)

            dve.wait_ge(pads_out, 32)
            dve.wait_ge(hid_one, 3)
            dve.wait_ge(small_in, 96)
            steps(dve, NT, 0, 4, shared_step, extra=E_DVE, skip=2, per=4)
            dve.wait_ge(b13_in, 32)
            steps(dve, NU, 0, 4, lambda s, par, _: unit_step(ro, NU, s, par, True), per=4)

        @block.tensor
        def _(pe):
            PARTS = ((0, 0), (1, 0), (0, 1))

            def product(out, stationary, moving, n):
                last = None
                for k in range(n):
                    for i, (a, b) in enumerate(PARTS):
                        last = pe.matmul(out, stationary(k, a), moving(k, b), start=(k == 0 and i == 0),
                                         stop=(k == n - 1 and i == len(PARTS) - 1))
                return last

            pe.wait_ge(id_ok, 2)
            for c, (kind, j, i) in enumerate(plan):
                cols = slice(j * P, (j + 1) * P)
                bank = ps[:, c % 8, :]
                if c >= 8:
                    pe.wait_ge(pre_dve, c - 7)
                if kind == "C":
                    pe.wait_ge(ctx_in, 16)
                    lo, n = KC[i]
                    for r in range(2):
                        last = pe.transpose(ps[0:n, c % 8, r * P:(r + 1) * P], ctx_sb[:, r, lo:lo + n], ident[:, :])
                elif kind == "W":
                    pe.wait_ge(wq_in, 16)
                    for k in range(KD):
                        last = pe.transpose(bank[:, k * P:(k + 1) * P], wq_sb[:, k, cols], ident[:, :])
                elif kind in "KV":
                    pe.wait_ge(pre_w_lo, w_number[kind, j] + 1)
                    pe.wait_ge(pre_dve, 2)
                    w = (wkh, wkl) if kind == "K" else (wvh, wvl)
                    last = product(bank[:, 0:BK], lambda k, part: w[part][0:KC[k][1], k, cols],
                                   lambda k, part: (ctxTh, ctxTl)[part][0:KC[k][1], k, :], len(KC))
                elif kind == "A":
                    pe.wait_ge(pre_dve, number["K", j, 0] + 1)
                    last = product(bank, lambda _, part: (wqTh, wqTl)[part][:, j % 2, i * P:(i + 1) * P],
                                   lambda _, part: (kTh, kTl)[part][:, j % 2, :, :].rearrange("p r n -> p (r n)"), 1)
                else:
                    pe.wait_ge(pre_w_lo, w_number["O", j] + 1)
                    pe.wait_ge(pre_dve, number["V", j, 0] + 1)
                    for b in range(2):
                        last = product(bank[:, b * D:(b + 1) * D],
                                       lambda _, part: (vTh, vTl)[part][:, j % 2, 2 * i + b, :, :].rearrange("p a n -> p (a n)"),
                                       lambda _, part: (woh, wol)[part][:, j, :], 1)
                last.then_inc(pre_pe, 1)
            pe.wait_ge(pre_act, NPRE)
            pe.wait_ge(pre_dve, NPRE)
            pe.wait_ge(small_in, 96)

            def tile_step(s, par, _):
                def scores(t, p, g):
                    b = t // TPB
                    return product(ps[:, s_bank(p) + g, :],
                                   lambda k, part: (xTh, xTl)[part][:, p, k * P:(k + 1) * P],
                                   lambda k, part: (Ah, Al)[part][:, bass.ds(b, 1), k, g * BANK:(g + 1) * BANK]
                                   .rearrange("p a n -> p (a n)"), KD)

                t = s - 1
                if has(t, NT):
                    wait(pe, xTl_ok, t + 1)
                    wait(pe, exp_ok, t - 1)
                    scores(t, (par + 1) % 2, 0)
                t = s - 6
                if has(t, NT):
                    p = par
                    wait(pe, xn2T_ok, t + 1)
                    for k in range(KD):
                        last = pe.matmul(ps[:, 0, 0:E], xn2T[:, p, k * P:(k + 1) * P], gateT[:, k, :],
                                         start=(k == 0), stop=(k == KD - 1))
                    last.then_inc(R_ok, 1)
                t = s - 1
                if has(t, NT):
                    scores(t, (par + 1) % 2, 1).then_inc(S_ok, 1)
                t = s
                if has(t, NT):
                    p = par
                    wait(pe, xn_ok, t + 1)
                    wait(pe, xTl_ok, t)
                    wait(pe, lg_ok, t - 5)
                    for k in range(KD):
                        last = pe.transpose(ps[:, 0, k * P:(k + 1) * P], xn[:, p, k * P:(k + 1) * P], ident[:, :])
                    last.then_inc(T_ok, 1)
                t = s - 3
                if has(t, NT):
                    p = (par + 1) % 2
                    wait(pe, norm_ok, t + 1)
                    for h in range(2):
                        wait(pe, pTl_ok, 2 * t + h - 1)
                        for i in range(NJ // 2):
                            j = h * (NJ // 2) + i
                            last = pe.transpose(ps[:, 3 + h, i * P:(i + 1) * P], prob[:, p, j * P:(j + 1) * P], ident[:, :])
                        last.then_inc(PT_ok, 1)
                t = s - 4
                if has(t, NT):
                    p = par
                    b = t // TPB
                    wait(pe, pTl_ok, 2 * t + 2)
                    wait(pe, x2_ok, t)
                    product(ps[:, 5, 0:D],
                            lambda k, part: (pTh, pTl)[part][:, p, k * P:(k + 1) * P],
                            lambda k, part: (Uh, Ul)[part][:, bass.ds(b, 1), k, :].rearrange("p a d -> p (a d)"),
                            NJ).then_inc(O_ok, 1)
                t = s - 5
                if has(t, NT):
                    p = (par + 1) % 2
                    wait(pe, xn2_ok, t + 1)
                    wait(pe, lg_ok, t)
                    wait(pe, xTl_ok, s + 1 if has(s, NT) else NT)
                    for k in range(KD):
                        last = pe.transpose(ps[:, 0, k * P:(k + 1) * P], xn2[:, p, k * P:(k + 1) * P], ident[:, :])
                    last.then_inc(T2_ok, 1)

            steps(pe, NT, 0, 6, tile_step, per=6)

            pe.wait_ge(chosen_ok, 1)
            pe.wait_ge(x2_ok, NT)
            pe.wait_ge(lg_ok, NT)
            flat = chosen[:, :, :].rearrange("p t e -> p (t e)")
            pe.matmul(ps[:, 1, 0:NT * E], ones[:, :], flat, start=True, stop=True).then_inc(rank_ok, 1)
            pe.matmul(ps[:, 0, 0:NT * E], tri[:, :], flat, start=True, stop=False, skip_group_check=True)
            for t in range(NT - 1):
                n = NT - 1 - t
                last = pe.matmul(ps[:, 0, (t + 1) * E:NT * E], ones[:, :],
                                 chosen[:, t:t + 1, :].to_broadcast([P, n, E]), start=False, stop=(t == NT - 2),
                                 skip_group_check=True)
            last.then_inc(rank_ok, 1)
            pe.wait_ge(slot_ok, 1)

            def unit_step(u, n, s, par, routed):
                def weights(parts, e, k, part, cols):
                    if not routed:
                        return parts[part][:, k, cols]
                    return parts[part][:, bass.ds(e, 1), k, cols].rearrange("p a n -> p (a n)")

                e_uv = e_y = None
                if routed:
                    both = pe.value_load(step_experts[0:1, bass.ds(s, 1)], min_val=0, max_val=E * E - 1)
                    e_uv, e_y = both % E, both // E

                t = s - 4
                if has(t, n):
                    p = par
                    wait(pe, u.hTl_ok, t + 1)
                    wait(pe, u.y_ok, t - 1)
                    w2s = (w2h, w2l) if routed else (ws2h, ws2l)
                    product(ps[:, 6 + p, 0:D],
                            lambda k, part: (hTh, hTl)[part][:, k * P:(k + 1) * P],
                            lambda k, part: weights(w2s, e_y, k, part, slice(0, D)), KH).then_inc(u.Y_ok, 1)
                t = s
                if has(t, n):
                    p = par
                    wait(pe, u.row_in[p], before(t) + 16)
                    wait(pe, u.xTl_ok, t)
                    for k in range(KD):
                        last = pe.transpose(ps[:, 0, k * P:(k + 1) * P], xrow[:, p, k * P:(k + 1) * P], ident[:, :])
                    last.then_inc(u.X_ok, 1)
                t = s - 3
                if has(t, n):
                    p = (par + 1) % 2
                    wait(pe, u.h_ok, t + 1)
                    wait(pe, u.hTl_ok, t)
                    for k in range(KH):
                        last = pe.transpose(ps[:, 5, k * P:(k + 1) * P], hid[:, p, k * P:(k + 1) * P], ident[:, :])
                    last.then_inc(u.H_ok, 1)
                t = s - 1
                if has(t, n):
                    p = (par + 1) % 2
                    wait(pe, u.xTl_ok, t + 1)
                    wait(pe, u.bias_ok, t - 1)
                    w13 = (w13h, w13l) if routed else (ws13h, ws13l)
                    for g in range(2):
                        last = product(ps[:, 1 + 2 * p + g, 0:H],
                                       lambda k, part: (uxTh, uxTl)[part][:, p, k * P:(k + 1) * P],
                                       lambda k, part: weights(w13, e_uv, k, part, slice(g * H, (g + 1) * H)), KD)
                    last.then_inc(u.UV_ok, 1)

            pe.wait_ge(sw_lo, 2)
            steps(pe, NT, 0, 4, lambda s, par, _: unit_step(sh, NT, s, par, False), per=4)
            pe.wait_ge(w_lo, 3 * E_DVE)
            pe.wait_ge(w_lo_pool, 3 * (E - E_DVE))
            pe.wait_ge(eid_ok, 1)
            steps(pe, NU, 0, 4, lambda s, par, _: unit_step(ro, NU, s, par, True), per=4)


_INS = ['x', 'ctx_768', 'L0_xattn_Wq', 'L0_xattn_Wk', 'L0_xattn_Wv', 'L0_xattn_Wo', 'L0_xattn_bo',
        'L0_ffn_gate_w', 'L0_ffn_gate_b', 'L0_ffn_w1', 'L0_ffn_b1', 'L0_ffn_w3', 'L0_ffn_b3', 'L0_ffn_w2', 'L0_ffn_b2',
        'L0_ffn_sw1', 'L0_ffn_sb1', 'L0_ffn_sw3', 'L0_ffn_sb3', 'L0_ffn_sw2', 'L0_ffn_sb2']


def kernel(**inputs):
    import numpy as _np
    import concourse.bacc as _bacc
    from concourse import mybir as _mybir
    from concourse.bass_utils import run_bass_kernel_spmd as _run

    nc = _bacc.Bacc("TRN2", target_bir_lowering=False, num_devices=1)
    arrays, args = {}, []
    for name in _INS:
        a = _np.ascontiguousarray(inputs[name])
        arrays[f"in_{name}"] = a
        args.append(nc.dram_tensor(f"in_{name}", a.shape, _mybir.dt.from_np(a.dtype), kind="ExternalInput").ap())
    b, n, d = inputs['x'].shape
    out = nc.dram_tensor("out_x", (b * n + PADS, d), _mybir.dt.float32, kind="ExternalOutput")
    xattn_moe(nc, *args, out.ap())
    r = _run(nc, [arrays], core_ids=[0])
    return r.results[0]["out_x"][:b * n].reshape(b, n, d)
```

```python
from contextlib import ExitStack

import concourse.bass as bass
from concourse import mybir

F32 = mybir.dt.float32
F32R = mybir.dt.float32r
BF16 = mybir.dt.bfloat16
I32 = mybir.dt.int32
ALU = mybir.AluOpType
ACT = mybir.ActivationFunctionType
AX = mybir.AxisListType

P = 128
BANK = 512
PADS = P
LN_EPS = 1e-5
LOWEST = -3.0e38


def wait(eng, sem, n):
    if not isinstance(n, int) or n > 0:
        eng.wait_ge(sem, n)


def xattn_moe(nc, x, ctx, Wq, Wk, Wv, Wo, bo, gate_w, gate_b, w1, b1, w3, b3, w2, b2,
              sw1, sb1, sw3, sb3, sw2, sb2, out):
    B, N, D = x.shape
    _, NK, DC = ctx.shape
    INNER = Wq.shape[1]
    DH = 64
    HEADS = INNER // DH
    E, _, H = w1.shape
    E_DVE = E // 4
    TOP = 2
    T = B * N
    NT = T // P
    TPB = N // P
    KD = D // P
    HK = HEADS * NK
    NJ = INNER // P
    BK = B * NK
    KC = [(0, P), (P, DC - P)]
    SCALE = DH ** -0.5
    HS = 8
    H3 = 3 * P
    KH = H3 // P
    HR = H - (KH - 1) * P
    NU = TOP * NT + E - 1
    assert HK == 2 * BANK and BK == 2 * P and D == 2 * P and NK == 64 and HR < P

    x_rows = x.rearrange("b n d -> (b n) d")
    xn2_dram = nc.dram_tensor("xn2_scratch", [T + PADS, D], F32, kind="Internal").ap()
    x2_dram = nc.dram_tensor("x2_scratch", [T, D], F32, kind="Internal").ap()
    slots_dram = nc.dram_tensor("slots_scratch", [P * NU, 2], I32, kind="Internal").ap()

    stack = ExitStack()
    with stack:
        def sb(name, shape, dt, on=stack):
            return on.enter_context(nc.sbuf_tensor(name, shape, dt))

        def sem(name):
            return stack.enter_context(nc.semaphore(name))

        ident = sb("ident", [P, P], F32)
        gateT = sb("gateT", [P, KD, E], F32)
        gateb_bc = sb("gateb_bc", [P, E], F32)
        minus_half = sb("minus_half", [P, 1], F32)
        eps = sb("eps", [P, 1], F32)
        record = sb("record", [P, NT, TOP, 2], I32)
        slot = sb("slot", [P, TOP, NT], I32)
        slot_col = sb("slot_col", [P, TOP, NT], I32)
        slot_row = sb("slot_row", [P, TOP, NT], I32)
        expert_of = sb("expert_of", [P, NU], I32)
        step_experts = sb("step_experts", [P, NU + 4], I32)
        slots = sb("slots", [P, NU, 2], I32)
        idx_in = sb("idx_in", [P, 2, 1], I32)
        idx_out = sb("idx_out", [P, 2, 1], I32)
        ws13h = sb("ws13h", [P, KD, 2 * H], F32R)
        ws2h = sb("ws2h", [P, KH, D], F32R)
        raw = ExitStack()
        ws13 = sb("ws13", [P, KD, 2 * H], F32, raw)
        ws2 = sb("ws2", [P, KH, D], F32, raw)
        raw.close()
        ws13l = sb("ws13l", [P, KD, 2 * H], F32R)
        ws2l = sb("ws2l", [P, KH, D], F32R)
        bs13 = sb("bs13", [P, 2 * H], F32)

        att = ExitStack()
        Ah = sb("Ah", [P, B, KD, HK], F32R, att)
        Al = sb("Al", [P, B, KD, HK], F32R, att)
        pre = ExitStack()
        wq_sb = sb("wq_sb", [P, KD, INNER], F32, pre)
        wkh = sb("wkh", [P, 2, INNER], F32R, pre)
        raw = ExitStack()
        wk_raw = sb("wk_raw", [P, 2, INNER], F32, raw)
        raw.close()
        wkl = sb("wkl", [P, 2, INNER], F32R, pre)
        wqTh = sb("wqTh", [P, 2, D], F32R, pre)
        wqTl = sb("wqTl", [P, 2, D], F32R, pre)
        kTh = sb("kTh", [P, 2, 2, BK], F32R, pre)
        kTl = sb("kTl", [P, 2, 2, BK], F32R, pre)
        ctx_sb = sb("ctx_sb", [P, 2, DC], F32, pre)
        zeros = sb("zeros", [P, 2 * 2 * BK], F32, pre)
        pre.close()
        Uh = sb("Uh", [P, B, NJ, D], F32R, att)
        Ul = sb("Ul", [P, B, NJ, D], F32R, att)
        bo_bc = sb("bo_bc", [P, D], F32, att)
        xin = sb("xin", [P, 2, D], F32, att)
        xn = sb("xn", [P, 2, D], F32, att)
        xTh = sb("xTh", [P, 2, D], F32R, att)
        xTl = sb("xTl", [P, 2, D], F32R, att)
        st1 = sb("st1", [P, 2, 6], F32, att)
        mv1 = sb("mv1", [P, 2, 2], F32, att)
        rs1 = sb("rs1", [P, 2, 2], F32, att)
        nm1 = sb("nm1", [P, 2, 1], F32, att)
        pre = ExitStack()
        raw = ExitStack()
        wv_raw = sb("wv_raw", [P, 2, INNER], F32, raw)
        wo_raw = sb("wo_raw", [P, NJ, D], F32, raw)
        raw.close()
        wvl = sb("wvl", [P, 2, INNER], F32R, pre)
        wol = sb("wol", [P, NJ, D], F32R, pre)
        wvh = sb("wvh", [P, 2, INNER], F32R, pre)
        woh = sb("woh", [P, NJ, D], F32R, pre)
        ctxTh = sb("ctxTh", [P, 2, BK], F32R, pre)
        ctxTl = sb("ctxTl", [P, 2, BK], F32R, pre)
        vTh = sb("vTh", [P, 2, B, 2, NK], F32R, pre)
        vTl = sb("vTl", [P, 2, B, 2, NK], F32R, pre)
        pre.close()
        xres = sb("xres", [P, 2, D], F32, att)
        prob = sb("prob", [P, 2, HK], F32, att)
        pTh = sb("pTh", [P, 2, HK], F32R, att)
        pTl = sb("pTl", [P, 2, HK], F32R, att)
        x2 = sb("x2", [P, 2, D], F32, att)
        xn2 = sb("xn2", [P, 2, D], F32, att)
        xn2T = sb("xn2T", [P, 2, D], F32, att)
        st2 = sb("st2", [P, 2, 6], F32, att)
        mv2 = sb("mv2", [P, 2, 2], F32, att)
        rs2 = sb("rs2", [P, 2, 2], F32, att)
        nm2 = sb("nm2", [P, 2, 1], F32, att)
        hmax = sb("hmax", [P, 2, HEADS], F32, att)
        hsum = sb("hsum", [P, 2, HEADS], F32, att)
        nmax = sb("nmax", [P, 2, HEADS - HS], F32, att)
        hinv = sb("hinv", [P, 2, HEADS], F32, att)
        att.close()

        w13h = sb("w13h", [P, E, KD, 2 * H], F32R)
        w2h = sb("w2h", [P, E, KH, D], F32R)
        raw = ExitStack()
        w2_raw = sb("w2_raw", [P, E, KH, D], F32, raw)
        w13_raw = sb("w13_raw", [P, E, KD, 2 * H], F32, raw)
        raw.close()
        w2l = sb("w2l", [P, E, KH, D], F32R)
        math = ExitStack()
        sb("below_math", [P, E * KD * 2 * H - 3072 - 512], F32, math)
        mA = sb("mA", [P, NT, E], F32, math)
        score = sb("score", [P, NT, E], F32, math)
        biased = sb("biased", [P, NT, E], F32, math)
        mB = sb("mB", [P, NT, E], F32, math)
        first = sb("first", [P, NT, E], F32, math)
        second = sb("second", [P, NT, E], F32, math)
        chosen = sb("chosen", [P, NT, E], BF16, math)
        slot8 = sb("slot8", [P, NT, E], F32, math)
        big = sb("big", [P, NU, E], F32, math)
        v32 = sb("v32", [P, 8, NT], F32, math)
        math.close()
        w13l = sb("w13l", [P, E, KD, 2 * H], F32R)
        b13 = sb("b13", [P, E, 2 * H], F32)
        xrow = sb("xrow", [P, 2, D], F32)
        x2row = sb("x2row", [P, 2, D], F32)
        uxTh = sb("uxTh", [P, 2, D], F32R)
        uxTl = sb("uxTl", [P, 2, D], F32R)
        hid = sb("hid", [P, 2, H3], F32)
        hTh = sb("hTh", [P, H3], F32R)
        hTl = sb("hTl", [P, H3], F32R)
        yrow = sb("yrow", [P, 2, D], F32)
        logits = sb("logits", [P, NT, E], F32)
        tri = sb("tri", [P, P], BF16)
        ones = sb("ones", [P, P], BF16)
        pref = sb("pref", [P, E], F32)
        upto = sb("upto", [P, E, E], F32)
        tile128 = sb("tile128", [P, NT], F32)
        unit_no = sb("unit_no", [P, NU], F32)
        uv = sb("uv", [P, 2, H], F32)

        ps = stack.enter_context(nc.psum_tensor("ps", [P, 8, BANK], F32))

        def f32(ap):
            return ap.bitcast(F32)

        def sems(name):
            return [sem(name + "_even"), sem(name + "_odd")]

        def before(t):
            return 16 * (t // 2)

        ctx_in = sem("ctx_in")
        wq_in = sem("wq_in")
        wk_in = sem("wk_in")
        wv_in = sem("wv_in")
        wo_in = sem("wo_in")
        small_in = sem("small_in")
        sw_in = sem("sw_in")
        id_ok = sem("id_ok")
        raw2_zero = sem("raw2_zero")
        zeros_ok = sem("zeros_ok")
        kT_zero = sem("kT_zero")
        vT_zero = sem("vT_zero")
        pre_w_hi = sem("pre_w_hi")
        pre_w_lo = sem("pre_w_lo")
        hid_one = sem("hid_one")
        pad2_zero = sem("pad2_zero")
        const_ok = sem("const_ok")
        table_out = sem("table_out")
        pads_out = sem("pads_out")
        pre_pe = sem("pre_pe")
        pre_act = sem("pre_act")
        pre_dve = sem("pre_dve")
        sw_hi = sem("sw_hi")
        sw_lo = sem("sw_lo")
        x_in = sems("x_in")
        xres_in = sems("xres_in")
        st1_ok = sem("st1_ok")
        mv1_ok = sem("mv1_ok")
        eps1_ok = sem("eps1_ok")
        rstd1_ok = sem("rstd1_ok")
        nm1_ok = sem("nm1_ok")
        xn_ok = sem("xn_ok")
        T_ok = sem("T_ok")
        xTh_ok = sem("xTh_ok")
        xTl_ok = sem("xTl_ok")
        S_ok = sem("S_ok")
        max_ok = sem("max_ok")
        nmax_ok = sem("nmax_ok")
        sub_ok = sem("sub_ok")
        exp_ok = sem("exp_ok")
        sum_ok = sem("sum_ok")
        inv_ok = sem("inv_ok")
        norm_ok = sem("norm_ok")
        PT_ok = sem("PT_ok")
        pTh_ok = sem("pTh_ok")
        pTl_ok = sem("pTl_ok")
        O_ok = sem("O_ok")
        xb_ok = sem("xb_ok")
        x2_ok = sem("x2_ok")
        x2_out = sems("x2_out")
        st2_ok = sem("st2_ok")
        mv2_ok = sem("mv2_ok")
        eps2_ok = sem("eps2_ok")
        rstd2_ok = sem("rstd2_ok")
        nm2_ok = sem("nm2_ok")
        xn2_ok = sem("xn2_ok")
        xn2_out = sems("xn2_out")
        T2_ok = sem("T2_ok")
        xn2T_ok = sem("xn2T_ok")
        R_ok = sem("R_ok")
        lg_ok = sem("lg_ok")
        rt = sem("rt")
        rt_sub = sem("rt_sub")
        rt_exp = sem("rt_exp")
        chosen_ok = sem("chosen_ok")
        rank_ok = sem("rank_ok")
        slot_ok = sem("slot_ok")
        eid_ok = sem("eid_ok")
        scat_out = sem("scat_out")
        slots_in = sem("slots_in")
        idx_in_ok = sem("idx_in_ok")
        idx_out_ok = sem("idx_out_ok")
        waited_dve = sem("waited_dve")
        waited_pool = sem("waited_pool")
        raw_in = [sem("raw_in_even"), sem("raw_in_odd")]
        w_hi = sem("w_hi")
        w_lo = sem("w_lo")
        w_lo_pool = sem("w_lo_pool")
        b13_in = sem("b13_in")

        row_in = sems("row_in")
        gather_in = sems("gather_in")
        X_ok = sem("X_ok")
        uxTh_ok = sem("uxTh_ok")
        uxTl_ok = sem("uxTl_ok")
        UV_ok = sem("UV_ok")
        bias_ok = sem("bias_ok")
        z_ok = sem("z_ok")
        h_ok = sem("h_ok")
        H_ok = sem("H_ok")
        hTh_ok = sem("hTh_ok")
        hTl_ok = sem("hTl_ok")
        Y_ok = sem("Y_ok")
        x2row_in = sems("x2row_in")
        sum_row_ok = sem("sum_row_ok")
        y_ok = sem("y_ok")
        sum_row_out = sems("sum_row_out")
        y_out = sems("y_out")
        NALL = NT + NU

        def steps(eng, n, lead, lag, body, begun=None, per=2):
            s0 = (lag + 2) // 2 * 2
            s1 = s0 + (n - lead - s0) // per * per
            for s in range(-lead if begun is None else begun, s0):
                body(s, s % 2)
            loop(eng, s0, s1, body, per)
            for s in range(s1, n + lag):
                body(s, s % 2)

        def loop(eng, start, end, body, per):
            if start == end:
                return
            with eng.Fori(0, (end - start) // per) as k:
                for i in range(per):
                    body(per * k + (start + i), i % 2)

        def weight_loop(eng, start, end, body, weight):
            if start == end:
                return
            with eng.Fori(0, (end - start) // 4) as k:
                for i in range(4):
                    body(4 * k + (start + i), i % 2)
                    if i % 2:
                        weight(2 * k + i // 2, i // 2, k)

        LAG = 4
        LOOP_FROM = LAG + 2

        def expert_steps(eng, body, begun=0, per=4, routed_per=6, weights=(0, 0), weight=None):
            w0 = LOOP_FROM + weights[0]
            w1 = w0 + 2 * weights[1]
            s1 = w1 + (NT - w1) // per * per
            r0 = NT + LAG + 2
            r1 = r0 + (NALL - r0) // routed_per * routed_per

            def shared(s, par):
                body(s, par, False)

            for s in range(begun, LOOP_FROM):
                body(s, s % 2, None)
            loop(eng, LOOP_FROM, w0, shared, per)
            weight_loop(eng, w0, w1, shared, weight)
            loop(eng, w1, s1, shared, per)
            for s in range(s1, r0):
                body(s, s % 2, None)
            loop(eng, r0, r1, lambda s, par: body(s, par, True), routed_per)
            for s in range(r1, NALL + LAG):
                body(s, s % 2, True)

        def is_routed(t, routed):
            return t >= NT if routed is None else routed

        def has(t, n):
            return not isinstance(t, int) or 0 <= t < n

        halves = [(slice(0, DH), 0), (slice(DH, P), 1)]

        plan = [("C", 0, 0), ("C", 0, 1), ("W", 0, 0), ("K", 0, 0)]
        for j in range(NJ):
            plan += [("W", j + 1, 0), ("K", j + 1, 0)] if j + 1 < NJ else [("V", 0, 0)]
            plan += [("A", j, 0), ("A", j, 1)]
        for j in range(NJ):
            plan += [("V", j + 1, 0)] if j + 1 < NJ else []
            plan += [("U", j, 0), ("U", j, 1)]
        number = {what: c for c, what in enumerate(plan)}
        NPRE = len(plan)

        w_plan = [("K", j) for j in range(NJ)] + [(kind, j) for j in range(NJ) for kind in "VO"]
        w_number = {what: c for c, what in enumerate(w_plan)}

        def w_pieces(kind, j, name):
            if kind == "O":
                return [{"raw": wo_raw, "high": woh, "low": wol}[name][:, j, :]]
            w = {"K": {"raw": wk_raw, "high": wkh, "low": wkl},
                 "V": {"raw": wv_raw, "high": wvh, "low": wvl}}[kind][name]
            return [w[0:n, i, j * P:(j + 1) * P] for i, (_, n) in enumerate(KC)]

        def s_bank(p):
            return (1, 6)[p]

        block = stack.enter_context(nc.Block())

        @block.sync
        def _(sp):
            def tile_step(s, par):
                t = s + 3
                if has(t, NT):
                    wait(sp, xn_ok, t - 1)
                    sp.dma_start(xin[:, (par + 1) % 2, :], x_rows[bass.ts(t, P), :]).then_inc(x_in[(par + 1) % 2], 16)
                t = s - 5
                if has(t, NT):
                    wait(sp, xn2_ok, t + 1)
                    sp.dma_start(xn2_dram[bass.ts(t, P), :],
                                 xn2[:, (par + 1) % 2, :]).then_inc(xn2_out[(par + 1) % 2], 16)
                t = s - 4
                if has(t, NT):
                    wait(sp, x2_ok, t + 1)
                    sp.dma_start(x2_dram[bass.ts(t, P), :], x2[:, par, :]).then_inc(x2_out[par], 16)
                t = s - 2
                if has(t, NT):
                    wait(sp, x2_ok, t - 1)
                    sp.dma_start(xres[:, par, :], x_rows[bass.ts(t, P), :]).then_inc(xres_in[par], 16)

            for s in (-3, -2):
                tile_step(s, s % 2)
            sp.dma_start(ctx_sb[:, :, :], ctx.rearrange("b s c -> (b s) c").rearrange("(r p) c -> p r c", p=P)
                         ).then_inc(ctx_in, 16)
            for i, (lo, n) in enumerate(KC):
                sp.dma_start(wk_raw[0:n, i, :], Wk[lo:lo + n, :]).then_inc(wk_in, 16)
            sp.dma_start(wq_sb[:, :, :], Wq.rearrange("(k p) n -> p k n", p=P)).then_inc(wq_in, 16)
            for i, (lo, n) in enumerate(KC):
                sp.dma_start(wv_raw[0:n, i, :], Wv[lo:lo + n, :]).then_inc(wv_in, 16)
            sp.dma_start(wo_raw[:, :, :], Wo.rearrange("(j p) d -> p j d", p=P)).then_inc(wo_in, 16)
            sp.dma_start(bo_bc[:, :], bo.rearrange("(a d) -> a d", a=1).to_broadcast([P, D])).then_inc(small_in, 16)
            sp.dma_start(gateb_bc[:, :], gate_b.rearrange("(a d) -> a d", a=1).to_broadcast([P, E])).then_inc(small_in, 16)
            for k in range(KD):
                sp.dma_start(gateT[:, k, :], gate_w[:, k * P:(k + 1) * P].rearrange("e p -> p e"),
                              allow_slow_non_contiguous=True).then_inc(small_in, 16)
            sp.dma_start(bs13[:, 0:H], sb1.rearrange("(a d) -> a d", a=1).to_broadcast([P, H])).then_inc(small_in, 16)
            sp.dma_start(bs13[:, H:2 * H], sb3.rearrange("(a d) -> a d", a=1).to_broadcast([P, H])).then_inc(small_in, 16)
            sp.dma_start(ws13[:, :, 0:H], sw1.rearrange("(k p) h -> p k h", p=P)).then_inc(sw_in, 16)
            sp.dma_start(ws13[:, :, H:2 * H], sw3.rearrange("(k p) h -> p k h", p=P)).then_inc(sw_in, 16)
            sp.wait_ge(raw2_zero, 1)
            sp.dma_start(ws2[:, 0:KH - 1, :], sw2[0:(KH - 1) * P, :].rearrange("(c p) d -> p c d", p=P)).then_inc(sw_in, 16)
            sp.dma_start(ws2[0:HR, KH - 1, :], sw2[(KH - 1) * P:H, :]).then_inc(sw_in, 16)
            sp.dma_start(ws2[HR:HR + 1, KH - 1, :], sb2.rearrange("(a d) -> a d", a=1)).then_inc(sw_in, 16)
            tile_step(-1, 1)
            sp.wait_ge(pre_pe, NPRE)
            sp.wait_ge(pre_dve, NPRE)
            steps(sp, NT, 3, 5, tile_step, begun=0, per=6)

            for half in xn2_out + x2_out:
                sp.wait_ge(half, before(NT))
            sp.wait_ge(O_ok, NT)
            sp.wait_ge(lg_ok, NT)
            sp.wait_ge(x2_ok, NT)

            def shared_step(s, par):
                t = s + 2
                if has(t, NT):
                    wait(sp, X_ok, t - 1)
                    sp.dma_start(xrow[:, par, :], xn2_dram[bass.ts(t, P), :]).then_inc(row_in[par], 16)
                t = s - 4
                if has(t, NT):
                    wait(sp, sum_row_ok, t + 1)
                    sp.dma_start(out[bass.ts(t, P), :], yrow[:, par, :]).then_inc(sum_row_out[par], 16)
                t = s - 2
                if has(t, NT):
                    wait(sp, sum_row_ok, t - 1)
                    sp.dma_start(x2row[:, par, :], x2_dram[bass.ts(t, P), :]).then_inc(x2row_in[par], 16)

            def weight(e, par, half):
                sp.wait_ge(eid_ok, 1)
                sp.wait_ge(pad2_zero, 1)
                wait(sp, raw_in[par], 80 * half)
                one = bass.ds(e, 1)
                sp.dma_start(w13_raw[:, one, :, 0:H],
                             w1[one, :, :].rearrange("e (k p) h -> p e k h", p=P)).then_inc(raw_in[par], 16)
                sp.dma_start(w13_raw[:, one, :, H:2 * H],
                             w3[one, :, :].rearrange("e (k p) h -> p e k h", p=P)).then_inc(raw_in[par], 16)
                sp.dma_start(w2_raw[:, one, 0:KH - 1, :],
                             w2[one, 0:(KH - 1) * P, :].rearrange("e (c p) d -> p e c d",
                                                                  p=P)).then_inc(raw_in[par], 16)
                sp.dma_start(w2_raw[0:HR, one, KH - 1, :],
                             w2[one, (KH - 1) * P:H, :].rearrange("e p d -> p e d")).then_inc(raw_in[par], 16)
                sp.dma_start(w2_raw[HR:HR + 1, one, KH - 1, :],
                             b2[one, :].rearrange("e (a d) -> a e d", a=1)).then_inc(raw_in[par], 16)
                for i, b in enumerate((b1, b3)):
                    sp.dma_start(b13[:, one, i * H:(i + 1) * H],
                                 b[one, :].rearrange("(a e) h -> a e h",
                                                     a=1).to_broadcast([P, 1, H])).then_inc(b13_in, 16)

            lead = 2
            for s in range(-lead, LOOP_FROM):
                shared_step(s, s % 2)
            w_end = LOOP_FROM + 2 * E
            s1 = w_end + (NT - lead - w_end) // 4 * 4
            weight_loop(sp, LOOP_FROM, w_end, shared_step, weight)
            loop(sp, w_end, s1, shared_step, 4)
            for s in range(s1, NT + LAG):
                shared_step(s, s % 2)

            sp.wait_ge(y_out[0], before(NU + 1))
            sp.wait_ge(y_out[1], before(NU))

        @block.gpsimd
        def _(pool):
            pool.memset(ident[:, :], 0.0).then_inc(id_ok, 1)
            pool.wait_ge(id_ok, 1)
            pool.affine_select(out=ident[:, :], in_=ident[:, :], compare_op=ALU.not_equal, fill=1.0, base=0,
                               pattern=[[-1, P]], channel_multiplier=1).then_inc(id_ok, 1)
            pool.memset(ws2[:, KH - 1, :], 0.0).then_inc(raw2_zero, 1)
            pool.memset(zeros[:, :], 0.0).then_inc(zeros_ok, 1)
            pool.memset(minus_half[:, :], -0.5).then_inc(const_ok, 1)
            pool.memset(eps[:, :], LN_EPS).then_inc(const_ok, 1)
            pool.iota(record[:, :, :, 0], pattern=[[P, NT], [0, TOP]], base=0,
                      channel_multiplier=1).then_inc(const_ok, 1)
            pool.memset(slots[:, :, 1], 0).then_inc(const_ok, 1)
            pool.iota(slots[:, :, 0], pattern=[[0, NU]], base=T, channel_multiplier=1).then_inc(const_ok, 1)
            pool.wait_ge(const_ok, 5)
            pool.dma_start(slots_dram.rearrange("(p n) c -> p n c", p=P), slots[:, :, :]).then_inc(table_out, 16)
            def tile_step(s, par):
                t = s + 1
                if has(t, NT):
                    p = (par + 1) % 2
                    wait(pool, mv1_ok, t + 1)
                    wait(pool, nm1_ok, t - 1)
                    wait(pool, xn_ok, t - 1)
                    pool.tensor_tensor(rs1[:, p, 0:1], mv1[:, p, 1:2], eps[:, :], ALU.add).then_inc(eps1_ok, 1)
                    wait(pool, eps1_ok, t + 1)
                    pool.tensor_tensor(rs1[:, p, 1:2], rs1[:, p, 0:1], minus_half[:, :],
                                       ALU.pow).then_inc(rstd1_ok, 1)
                t = s - 5
                if has(t, NT):
                    p = (par + 1) % 2
                    wait(pool, mv2_ok, t + 1)
                    wait(pool, nm2_ok, t - 1)
                    wait(pool, xn2_ok, t - 1)
                    pool.tensor_tensor(rs2[:, p, 0:1], mv2[:, p, 1:2], eps[:, :], ALU.add).then_inc(eps2_ok, 1)
                    wait(pool, eps2_ok, t + 1)
                    pool.tensor_tensor(rs2[:, p, 1:2], rs2[:, p, 0:1], minus_half[:, :],
                                       ALU.pow).then_inc(rstd2_ok, 1)
                t = s - 2
                if has(t, NT):
                    p = par
                    wait(pool, inv_ok, t + 1)
                    heads = prob[:, p, :].rearrange("p (h k) -> p h k", k=NK)
                    pool.tensor_tensor(heads, heads, hinv[:, p, :].unsqueeze(2).to_broadcast([P, HEADS, NK]),
                                       ALU.mult).then_inc(norm_ok, 1)
                t = s - 3
                if has(t, NT):
                    p = (par + 1) % 2
                    wait(pool, xres_in[p], before(t) + 16)
                    pool.tensor_tensor(xres[:, p, :], xres[:, p, :], bo_bc[:, :], ALU.add).then_inc(xb_ok, 1)

            for s in (-1, 0):
                tile_step(s, s % 2)
            for c, (kind, j) in enumerate(w_plan):
                pool.wait_ge(pre_w_hi, c + 1)
                for low, raw, high in zip(*(w_pieces(kind, j, name) for name in ("low", "raw", "high"))):
                    last = pool.tensor_tensor(low, raw, f32(high), ALU.subtract)
                last.then_inc(pre_w_lo, 1)
            pool.wait_ge(small_in, 96)
            pool.wait_ge(pre_pe, NPRE)
            pool.wait_ge(pre_act, NPRE)
            pool.wait_ge(pre_dve, NPRE)
            pool.memset(ones[:, :], 1.0).then_inc(const_ok, 1)
            pool.memset(tri[:, :], 1.0).then_inc(const_ok, 1)
            pool.memset(upto[:, :, :], 1.0).then_inc(const_ok, 1)
            pool.iota(pref[:, :], pattern=[[-1, E]], base=E, channel_multiplier=0,
                      allow_small_or_imprecise_dtypes=True).then_inc(const_ok, 1)
            pool.iota(tile128[:, :], pattern=[[P, NT]], base=0, channel_multiplier=0,
                      allow_small_or_imprecise_dtypes=True).then_inc(const_ok, 1)
            pool.iota(unit_no[:, :], pattern=[[1, NU]], base=0, channel_multiplier=0,
                      allow_small_or_imprecise_dtypes=True).then_inc(const_ok, 1)
            pool.wait_ge(const_ok, 11)
            pool.affine_select(out=tri[:, :], in_=tri[:, :], compare_op=ALU.is_gt, fill=0.0, base=0,
                               pattern=[[1, P]], channel_multiplier=-1).then_inc(const_ok, 1)
            pool.affine_select(out=upto[:, :, :], in_=upto[:, :, :], compare_op=ALU.is_ge, fill=0.0, base=0,
                               pattern=[[1, E], [-1, E]], channel_multiplier=0).then_inc(const_ok, 1)
            steps(pool, NT, 1, 5, tile_step, begun=1, per=6)

            for half in xn2_out + x2_out:
                pool.wait_ge(half, before(NT))
            pool.wait_ge(O_ok, NT)
            pool.wait_ge(lg_ok, NT)
            pool.memset(w2_raw[:, :, KH - 1, :], 0.0).then_inc(pad2_zero, 1)
            pool.memset(yrow[:, 0, :], 0.0).then_inc(hid_one, 1)
            pool.memset(hid[:, :, H:H3], 0.0).then_inc(hid_one, 1)
            pool.wait_ge(hid_one, 2)
            pool.memset(hid[:, :, H:H + 1], 1.0).then_inc(hid_one, 1)
            pool.dma_start(xn2_dram[T:T + PADS, :], yrow[:, 0, :]).then_inc(pads_out, 16)
            pool.dma_start(out[T:T + PADS, :], yrow[:, 0, :]).then_inc(pads_out, 16)

            pool.wait_ge(sw_hi, 1)
            pool.tensor_tensor(ws13l[:, :, :], ws13[:, :, :], f32(ws13h[:, :, :]), ALU.subtract).then_inc(sw_lo, 1)
            pool.wait_ge(sw_hi, 2)
            pool.tensor_tensor(ws2l[:, :, :], ws2[:, :, :], f32(ws2h[:, :, :]), ALU.subtract).then_inc(sw_lo, 1)
            pool.wait_ge(table_out, 16)
            pool.wait_ge(slot_ok, 1)
            for t in range(NT):
                for k in range(TOP):
                    pool.indirect_dma_start(slots_dram, bass.IndirectOffsetOnAxis(ap=slot[:, k, t:t + 1], axis=0),
                                            record[:, t, k, :], None).then_inc(scat_out, 16)
            pool.wait_ge(scat_out, 16 * TOP * NT)
            pool.dma_start(slots[:, :, :], slots_dram.rearrange("(p n) c -> p n c", p=P)).then_inc(slots_in, 16)
            with pool.Fori(E_DVE, E) as e:
                one = bass.ds(e, 1)
                wait(pool, w_hi, 3 * e + 3)
                for k in range(KD):
                    pool.tensor_tensor(w13l[:, one, k, :], w13_raw[:, one, k, :], f32(w13h[:, one, k, :]),
                                       ALU.subtract).then_inc(w_lo_pool, 1)
                flat = [a[:, one, :, :].rearrange("p e c d -> p (e c d)") for a in (w2l, w2_raw, w2h)]
                pool.tensor_tensor(flat[0], flat[1], f32(flat[2]), ALU.subtract).then_inc(w_lo_pool, 1)
            pool.wait_ge(pads_out, 32)
            pool.wait_ge(slots_in, 16)

            def routed_step(s, par):
                t = s - 4
                if has(t, NU):
                    p = par
                    if isinstance(t, int) and t == 0:
                        for half in sum_row_out:
                            pool.wait_ge(half, before(NT))
                    wait(pool, y_out[1 - p], before(t + 1))
                    pool.tensor_copy(idx_out[:, p, :], slots[:, bass.ds(t, 1), 0]).then_inc(idx_out_ok, 1)
                    wait(pool, idx_out_ok, t + 1)
                    wait(pool, y_ok, t + 1)
                    pool.sem_inc(waited_pool, 1)
                    pool.indirect_dma_start(out, bass.IndirectOffsetOnAxis(ap=idx_out[:, p, :], axis=0),
                                            yrow[:, p, :], None, compute_op=ALU.add).then_inc(y_out[p], 16)
                t = s + 2
                if has(t, NU):
                    p = par
                    wait(pool, gather_in[p], before(t))
                    pool.tensor_copy(idx_in[:, p, :], slots[:, bass.ds(t, 1), 0]).then_inc(idx_in_ok, 1)
                    wait(pool, idx_in_ok, t + 1)
                    wait(pool, X_ok, NT + t - 1)
                    pool.sem_inc(waited_pool, 1)
                    pool.indirect_dma_start(xrow[:, p, :], None, xn2_dram,
                                            bass.IndirectOffsetOnAxis(ap=idx_in[:, p, :],
                                                                      axis=0)).then_inc(gather_in[p], 16)

            steps(pool, NU, 2, 4, routed_step, per=6)

        @block.scalar
        def _(act):
            def tile_step(s, par):
                t = s - 6
                if has(t, NT):
                    p = par
                    wait(act, T2_ok, t + 1)
                    wait(act, R_ok, t - 1)
                    act.activation(xn2T[:, p, :], ps[:, 0, 0:D], ACT.Copy).then_inc(xn2T_ok, 1)
                t = s - 5
                if has(t, NT):
                    p = (par + 1) % 2
                    wait(act, nm2_ok, t + 1)
                    wait(act, T2_ok, t - 1)
                    wait(act, xn2_out[p], before(t))
                    act.activation(xn2[:, p, :], x2[:, p, :], ACT.Identity, bias=nm2[:, p, :],
                                   scale=rs2[:, p, 1:2]).then_inc(xn2_ok, 1)
                t = s + 1
                if has(t, NT):
                    p = (par + 1) % 2
                    wait(act, nm1_ok, t + 1)
                    wait(act, T_ok, t - 1)
                    act.activation(xn[:, p, :], xin[:, p, :], ACT.Identity, bias=nm1[:, p, :],
                                   scale=rs1[:, p, 1:2]).then_inc(xn_ok, 1)
                t = s
                if has(t, NT):
                    p = par
                    wait(act, T_ok, t + 1)
                    wait(act, S_ok, t - 1)
                    act.activation(xTh[:, p, :], ps[:, 0, 0:D], ACT.Copy).then_inc(xTh_ok, 1)
                t = s - 3
                if has(t, NT):
                    p = (par + 1) % 2
                    wait(act, O_ok, t - 1)
                    for h in range(2):
                        wait(act, PT_ok, 2 * t + h + 1)
                        act.activation(pTh[:, p, h * BANK:(h + 1) * BANK], ps[:, 3 + h, :],
                                       ACT.Copy).then_inc(pTh_ok, 1)
                t = s - 1
                if has(t, NT):
                    p = (par + 1) % 2
                    wait(act, nmax_ok, t + 1)
                    wait(act, inv_ok, t - 1)
                    wait(act, PT_ok, 2 * t - 2)
                    for h in range(HS, HEADS):
                        act.activation(prob[:, p, h * NK:(h + 1) * NK],
                                       ps[:, s_bank(p) + h // 8, h % 8 * NK:(h % 8 + 1) * NK],
                                       ACT.Exp, bias=nmax[:, p, h - HS:h - HS + 1], scale=SCALE,
                                       accum_out=hsum[:, p, h:h + 1])
                    wait(act, sub_ok, t + 1)
                    act.activation(prob[:, p, 0:HS * NK], prob[:, p, 0:HS * NK], ACT.Exp,
                                   scale=SCALE).then_inc(exp_ok, 1)

            tile_step(-1, 1)
            def leave(c, out, in_):
                act.wait_ge(pre_pe, c + 1)
                return act.activation(out, in_, ACT.Copy)

            def high(kind, j):
                if j < NJ:
                    for sem_in, n in {"K": ((wk_in, 32),), "V": ((wv_in, 32),), "O": ((wo_in, 16),)}[kind]:
                        act.wait_ge(sem_in, n)
                    for out_, in_ in zip(w_pieces(kind, j, "high"), w_pieces(kind, j, "raw")):
                        last = act.activation(out_, in_, ACT.Copy)
                    last.then_inc(pre_w_hi, 1)

            for c, (kind, j, i) in enumerate(plan):
                bank = ps[:, c % 8, :]
                if kind == "C":
                    n = KC[i][1]
                    leave(c, ctxTh[0:n, i, :], ps[0:n, c % 8, 0:BK]).then_inc(pre_act, 1)
                    if i == 1:
                        high("K", 0)
                elif kind == "W":
                    high("K", j + 1)
                    if j == NJ - 1:
                        high("V", 0)
                        high("O", 0)
                    leave(c, wqTh[:, j % 2, :], bank[:, 0:D]).then_inc(pre_act, 1)
                elif kind == "K":
                    if j == 0:
                        act.wait_ge(kT_zero, 2)
                    for half, r in halves:
                        last = leave(c, kTh[half, j % 2, r, :], ps[half, c % 8, 0:BK])
                    last.then_inc(pre_act, 1)
                elif kind == "A":
                    for r in range(2):
                        last = leave(c, Ah[:, :, i, (2 * j + r) * NK:(2 * j + r + 1) * NK],
                                     bank[:, r * BK:(r + 1) * BK].rearrange("p (b n) -> p b n", b=B))
                    last.then_inc(pre_act, 1)
                elif kind == "V":
                    high("V", j + 1)
                    high("O", j + 1)
                    if j == 0:
                        act.wait_ge(vT_zero, 2)
                    for half, r in halves:
                        last = leave(c, vTh[half, j % 2, :, r, :],
                                     ps[half, c % 8, 0:BK].rearrange("p (b n) -> p b n", b=B))
                    last.then_inc(pre_act, 1)
                else:
                    leave(c, Uh[:, 2 * i:2 * i + 2, j, :],
                          bank.rearrange("p (b d) -> p b d", b=2)).then_inc(pre_act, 1)
            act.wait_ge(pre_pe, NPRE)
            act.wait_ge(pre_dve, NPRE)
            act.wait_ge(small_in, 96)
            steps(act, NT, 1, 6, tile_step, begun=0, per=6)

            act.wait_ge(rt_sub, 1)
            act.activation(score[:, :, :], mA[:, :, :], ACT.Exp).then_inc(rt_exp, 1)
            act.wait_ge(sw_in, 80)
            act.activation(ws13h[:, :, :], ws13[:, :, :], ACT.Copy).then_inc(sw_hi, 1)
            act.activation(ws2h[:, :, :], ws2[:, :, :], ACT.Copy).then_inc(sw_hi, 1)

            def unit_step(s, par, routed):
                t = s - 4
                if has(t, NALL) and is_routed(t, routed):
                    p = par
                    if isinstance(t, int) and t == NT:
                        act.wait_ge(slots_in, 16)
                    if isinstance(t, int) and t < NT + 2:
                        act.wait_ge(sum_row_out[p], before(NT))
                    wait(act, Y_ok, t + 1)
                    wait(act, y_out[p], before(t - NT))
                    act.activation(yrow[:, p, :], ps[:, 6 + p, 0:D], ACT.Copy,
                                   scale=slots[:, bass.ds(t - NT, 1), 1].bitcast(F32)).then_inc(y_ok, 1)
                t = s
                if has(t, NALL):
                    p = par
                    wait(act, X_ok, t + 1)
                    wait(act, UV_ok, t - 1)
                    act.activation(uxTh[:, p, :], ps[:, 0, 0:D], ACT.Copy).then_inc(uxTh_ok, 1)
                t = s - 3
                if has(t, NALL):
                    wait(act, H_ok, t + 1)
                    wait(act, Y_ok, t)
                    act.activation(hTh[:, :], ps[:, 5, 0:H3], ACT.Copy).then_inc(hTh_ok, 1)
                t = s - 2
                if has(t, NALL):
                    p = par
                    wait(act, z_ok, t + 1)
                    act.activation(hid[:, p, 0:H], hid[:, p, 0:H], ACT.Silu).then_inc(h_ok, 1)

            def weight(e, par, half):
                one = bass.ds(e, 1)
                wait(act, raw_in[par], 80 * half + 80)
                for k in range(KD):
                    act.activation(w13h[:, one, k, :], w13_raw[:, one, k, :], ACT.Copy).then_inc(w_hi, 1)
                high, raw = [a[:, one, :, :].rearrange("p e c d -> p (e c d)") for a in (w2h, w2_raw)]
                act.activation(high, raw, ACT.Copy).then_inc(w_hi, 1)

            act.wait_ge(lg_ok, NT)
            act.wait_ge(hid_one, 3)
            expert_steps(act, unit_step, weights=(4, E), weight=weight)

        @block.vector
        def _(dve):
            def heads(ap):
                return ap.rearrange("p (h k) -> p h k", k=NK)

            def tile_step(s, par):
                t = s - 2
                if has(t, NT):
                    p = par
                    wait(dve, exp_ok, t + 1)
                    dve.tensor_reduce(hsum[:, p, 0:HS], heads(prob[:, p, 0:HS * NK]), AX.X,
                                      ALU.add).then_inc(sum_ok, 1)
                    wait(dve, sum_ok, t + 1)
                    wait(dve, norm_ok, t - 1)
                    dve.reciprocal(hinv[:, p, :], hsum[:, p, :]).then_inc(inv_ok, 1)
                t = s - 5
                if has(t, NT):
                    p = (par + 1) % 2
                    wait(dve, rstd2_ok, t + 1)
                    wait(dve, xn2_ok, t - 1)
                    dve.scalar_tensor_tensor(out=nm2[:, p, :], in0=mv2[:, p, 0:1], scalar=-1.0, in1=rs2[:, p, 1:2],
                                             op0=ALU.mult, op1=ALU.mult).then_inc(nm2_ok, 1)
                t = s + 1
                if has(t, NT):
                    p = (par + 1) % 2
                    wait(dve, rstd1_ok, t + 1)
                    wait(dve, xn_ok, t - 1)
                    dve.scalar_tensor_tensor(out=nm1[:, p, :], in0=mv1[:, p, 0:1], scalar=-1.0, in1=rs1[:, p, 1:2],
                                             op0=ALU.mult, op1=ALU.mult).then_inc(nm1_ok, 1)
                t = s - 6
                if has(t, NT):
                    wait(dve, R_ok, t + 1)
                    dve.tensor_copy(logits[:, bass.ds(t, 1), :].rearrange("p a e -> p (a e)"),
                                    ps[:, 0, 0:E]).then_inc(lg_ok, 1)
                t = s + 2
                if has(t, NT):
                    p = par
                    wait(dve, x_in[p], before(t) + 16)
                    dve.bn_stats(st1[:, p, :], xin[:, p, :]).then_inc(st1_ok, 1)
                    wait(dve, st1_ok, t + 1)
                    wait(dve, rstd1_ok, t - 1)
                    dve.sem_inc(waited_dve, 1)
                    dve.bn_aggr(mv1[:, p, :], st1[:, p, :]).then_inc(mv1_ok, 1)
                t = s - 1
                if has(t, NT):
                    p = (par + 1) % 2
                    wait(dve, S_ok, t + 1)
                    scores = ps[:, s_bank(p):s_bank(p) + 2, :].rearrange("p a (h k) -> p (a h) k", k=NK)
                    dve.tensor_reduce(hmax[:, p, :], scores, AX.X, ALU.max).then_inc(max_ok, 1)
                    wait(dve, max_ok, t + 1)
                    wait(dve, exp_ok, t - 1)
                    dve.tensor_scalar(nmax[:, p, :], hmax[:, p, HS:HEADS], -SCALE, None,
                                      ALU.mult).then_inc(nmax_ok, 1)
                    wait(dve, PT_ok, 2 * t - 2)
                    dve.tensor_tensor(heads(prob[:, p, 0:HS * NK]), scores[:, 0:HS, :],
                                      hmax[:, p, 0:HS].unsqueeze(2).to_broadcast([P, HS, NK]),
                                      ALU.subtract).then_inc(sub_ok, 1)
                t = s
                if has(t, NT):
                    p = par
                    wait(dve, xTh_ok, t + 1)
                    wait(dve, S_ok, t - 1)
                    dve.tensor_tensor(xTl[:, p, :], ps[:, 0, 0:D], f32(xTh[:, p, :]),
                                      ALU.subtract).then_inc(xTl_ok, 1)
                t = s - 3
                if has(t, NT):
                    p = (par + 1) % 2
                    for h in range(2):
                        cols = slice(h * BANK, (h + 1) * BANK)
                        wait(dve, pTh_ok, 2 * t + h + 1)
                        dve.tensor_tensor(pTl[:, p, cols], ps[:, 3 + h, :], f32(pTh[:, p, cols]),
                                          ALU.subtract).then_inc(pTl_ok, 1)
                t = s - 4
                if has(t, NT):
                    p = par
                    wait(dve, O_ok, t + 1)
                    wait(dve, xb_ok, t + 1)
                    wait(dve, x2_out[p], before(t))
                    wait(dve, xn2_ok, t - 1)
                    dve.tensor_tensor(x2[:, p, :], ps[:, 5, 0:D], xres[:, p, :], ALU.add).then_inc(x2_ok, 1)
                    wait(dve, x2_ok, t + 1)
                    dve.bn_stats(st2[:, p, :], x2[:, p, :]).then_inc(st2_ok, 1)
                    wait(dve, st2_ok, t + 1)
                    wait(dve, rstd2_ok, t - 1)
                    dve.sem_inc(waited_dve, 1)
                    dve.bn_aggr(mv2[:, p, :], st2[:, p, :]).then_inc(mv2_ok, 1)

            for s in (-2, -1):
                tile_step(s, s % 2)
            dve.wait_ge(zeros_ok, 1)
            for k in (kTh, kTl):
                dve.tensor_copy(k[:, :, :, :].rearrange("p a r n -> p (a r n)"), zeros[:, :]).then_inc(kT_zero, 1)
            for v in (vTh, vTl):
                dve.tensor_copy(v[:, :, :, :, :].rearrange("p a b r n -> p (a b r n)"),
                                zeros[:, :]).then_inc(vT_zero, 1)
            dve.wait_ge(kT_zero, 2)
            dve.wait_ge(vT_zero, 2)
            for c, (kind, j, i) in enumerate(plan):
                bank = ps[:, c % 8, :]
                dve.wait_ge(pre_act, c + 1)
                if kind == "C":
                    n = KC[i][1]
                    last = dve.tensor_tensor(ctxTl[0:n, i, :], ps[0:n, c % 8, 0:BK], f32(ctxTh[0:n, i, :]),
                                             ALU.subtract)
                elif kind == "W":
                    last = dve.tensor_tensor(wqTl[:, j % 2, :], bank[:, 0:D], f32(wqTh[:, j % 2, :]), ALU.subtract)
                elif kind == "K":
                    for half, r in halves:
                        last = dve.tensor_tensor(kTl[half, j % 2, r, :], ps[half, c % 8, 0:BK],
                                                 f32(kTh[half, j % 2, r, :]), ALU.subtract)
                elif kind == "A":
                    for r in range(2):
                        cols = slice((2 * j + r) * NK, (2 * j + r + 1) * NK)
                        last = dve.tensor_tensor(Al[:, :, i, cols],
                                                 bank[:, r * BK:(r + 1) * BK].rearrange("p (b n) -> p b n", b=B),
                                                 f32(Ah[:, :, i, cols]), ALU.subtract)
                elif kind == "V":
                    for half, r in halves:
                        last = dve.tensor_tensor(vTl[half, j % 2, :, r, :],
                                                 ps[half, c % 8, 0:BK].rearrange("p (b n) -> p b n", b=B),
                                                 f32(vTh[half, j % 2, :, r, :]), ALU.subtract)
                else:
                    last = dve.tensor_tensor(Ul[:, 2 * i:2 * i + 2, j, :], bank.rearrange("p (b d) -> p b d", b=2),
                                             f32(Uh[:, 2 * i:2 * i + 2, j, :]), ALU.subtract)
                last.then_inc(pre_dve, 1)
            dve.wait_ge(pre_pe, NPRE)
            dve.wait_ge(pre_act, NPRE)
            steps(dve, NT, 2, 6, tile_step, begun=0, per=6)

            def unit_step(s, par, routed):
                t = s - 4
                if has(t, NALL) and not is_routed(t, routed):
                    p = par
                    wait(dve, Y_ok, t + 1)
                    wait(dve, x2row_in[p], before(t) + 16)
                    wait(dve, sum_row_out[p], before(t))
                    dve.tensor_tensor(yrow[:, p, :], ps[:, 6 + p, 0:D], x2row[:, p, :],
                                      ALU.add).then_inc(sum_row_ok, 1)
                t = s
                if has(t, NALL):
                    p = par
                    wait(dve, uxTh_ok, t + 1)
                    wait(dve, UV_ok, t - 1)
                    dve.tensor_tensor(uxTl[:, p, :], ps[:, 0, 0:D], f32(uxTh[:, p, :]),
                                      ALU.subtract).then_inc(uxTl_ok, 1)
                t = s - 3
                if has(t, NALL):
                    wait(dve, hTh_ok, t + 1)
                    wait(dve, Y_ok, t)
                    dve.tensor_tensor(hTl[:, :], ps[:, 5, 0:H3], f32(hTh[:, :]), ALU.subtract).then_inc(hTl_ok, 1)
                t = s - 1
                if has(t, NALL):
                    p = (par + 1) % 2
                    if is_routed(t, routed):
                        e = dve.value_load(expert_of[0:1, bass.ds(t - NT, 1)], min_val=0, max_val=E - 1)
                        if isinstance(t, int) and t == NT:
                            dve.wait_ge(b13_in, 32 * E)
                        bias = b13[:, bass.ds(e, 1), :].rearrange("p e (a h) -> p (e a) h", a=2)
                    else:
                        bias = bs13[:, :].rearrange("p (a h) -> p a h", a=2)
                    wait(dve, UV_ok, t + 1)
                    wait(dve, z_ok, t)
                    dve.tensor_tensor(uv[:, :, :], ps[:, 1 + 2 * p:3 + 2 * p, 0:H], bias,
                                      ALU.add).then_inc(bias_ok, 1)
                    wait(dve, bias_ok, t + 1)
                    wait(dve, H_ok, t - 1)
                    dve.tensor_tensor(hid[:, p, 0:H], uv[:, 0, :], uv[:, 1, :], ALU.mult).then_inc(z_ok, 1)

            def weight(e, *_):
                one = bass.ds(e, 1)
                for k in range(KD):
                    wait(dve, w_hi, 3 * e + k + 1)
                    dve.tensor_tensor(w13l[:, one, k, :], w13_raw[:, one, k, :], f32(w13h[:, one, k, :]),
                                      ALU.subtract).then_inc(w_lo, 1)
                wait(dve, w_hi, 3 * e + 3)
                low, raw, high = [a[:, one, :, :].rearrange("p e c d -> p (e c d)") for a in (w2l, w2_raw, w2h)]
                dve.tensor_tensor(low, raw, f32(high), ALU.subtract).then_inc(w_lo, 1)

            linked = [0]

            def link(ins):
                linked[0] += 1
                ins.then_inc(rt, 1)
                dve.wait_ge(rt, linked[0])

            def over_e(ap):
                return ap.unsqueeze(2).to_broadcast([P, NT, E])

            dve.wait_ge(lg_ok, NT)
            dve.wait_ge(O_ok, NT)
            dve.wait_ge(const_ok, 13)
            link(dve.tensor_reduce(v32[:, 0, :], logits[:, :, :], AX.X, ALU.max))
            dve.tensor_tensor(mA[:, :, :], logits[:, :, :], over_e(v32[:, 0, :]), ALU.subtract).then_inc(rt_sub, 1)
            dve.wait_ge(rt_exp, 1)
            link(dve.tensor_reduce(v32[:, 1, :], score[:, :, :], AX.X, ALU.add))
            link(dve.reciprocal(v32[:, 2, :], v32[:, 1, :]))
            link(dve.tensor_tensor(score[:, :, :], score[:, :, :], over_e(v32[:, 2, :]), ALU.mult))
            link(dve.tensor_tensor(biased[:, :, :], score[:, :, :],
                                   gateb_bc[:, :].unsqueeze(1).to_broadcast([P, NT, E]), ALU.add))
            for k, mark in enumerate((first, second)):
                link(dve.tensor_reduce(v32[:, 3, :], biased[:, :, :], AX.X, ALU.max))
                link(dve.tensor_tensor(mA[:, :, :], biased[:, :, :], over_e(v32[:, 3, :]), ALU.is_ge))
                link(dve.tensor_tensor(mA[:, :, :], mA[:, :, :],
                                       pref[:, :].unsqueeze(1).to_broadcast([P, NT, E]), ALU.mult))
                link(dve.tensor_reduce(v32[:, 3, :], mA[:, :, :], AX.X, ALU.max))
                link(dve.tensor_tensor(mark[:, :, :], mA[:, :, :], over_e(v32[:, 3, :]), ALU.is_equal))
                if k == 0:
                    link(dve.scalar_tensor_tensor(out=biased[:, :, :], in0=mark[:, :, :], scalar=LOWEST,
                                                  in1=biased[:, :, :], op0=ALU.mult, op1=ALU.add))
            dve.tensor_tensor(chosen[:, :, :], first[:, :, :], second[:, :, :], ALU.add).then_inc(chosen_ok, 1)
            for k, mark in enumerate((first, second)):
                link(dve.tensor_tensor(mA[:, :, :], mark[:, :, :], score[:, :, :], ALU.mult))
                link(dve.tensor_reduce(record[:, :, k, 1].bitcast(F32), mA[:, :, :], AX.X, ALU.add))
            dve.wait_ge(small_in, 96)
            unit_step(0, 0, None)
            dve.wait_ge(rank_ok, 1)
            rows = v32[:, 4, 0:E]
            tiles = v32[:, 4, E:2 * E]
            ends = v32[:, 4, 2 * E:3 * E]
            begin = v32[:, 4, 3 * E:4 * E]
            link(dve.tensor_reduce(rows, ps[:, 7, 0:NT * E].rearrange("p (t e) -> p e t", e=E), AX.X, ALU.add))
            link(dve.tensor_tensor(mA[:, :, :].rearrange("p t e -> p (t e)").rearrange("p (e t) -> p e t", e=E),
                                   rows.unsqueeze(2).to_broadcast([P, E, NT]),
                                   tile128[:, :].unsqueeze(1).to_broadcast([P, E, NT]), ALU.is_gt))
            link(dve.tensor_reduce(tiles, mA[:, :, :].rearrange("p t e -> p (t e)").rearrange("p (e t) -> p e t", e=E),
                                   AX.X, ALU.add))
            ee = mB[:, 0:E, :]
            link(dve.tensor_tensor(ee, upto[:, :, :], tiles.unsqueeze(1).to_broadcast([P, E, E]), ALU.mult))
            link(dve.tensor_reduce(ends, ee, AX.X, ALU.add))
            link(dve.tensor_tensor(begin, ends, tiles, ALU.subtract))
            dve.wait_ge(rank_ok, 2)
            link(dve.scalar_tensor_tensor(out=slot8[:, :, :], in0=begin.unsqueeze(1).to_broadcast([P, NT, E]),
                                          scalar=float(P), in1=ps[:, 6, 0:NT * E].rearrange("p (t e) -> p t e", e=E),
                                          op0=ALU.mult, op1=ALU.add))
            for k, mark in enumerate((first, second)):
                link(dve.tensor_tensor(mA[:, :, :], mark[:, :, :], slot8[:, :, :], ALU.mult))
                link(dve.tensor_reduce(v32[:, 5 + k, :], mA[:, :, :], AX.X, ALU.add))
            link(dve.tensor_copy(slot[:, :, :], v32[:, 5:5 + TOP, :]))
            link(dve.tensor_scalar(slot_col[:, :, :], slot[:, :, :], 7, None, ALU.logical_shift_right))
            link(dve.tensor_scalar(slot_row[:, :, :], slot[:, :, :], P - 1, None, ALU.bitwise_and))
            dve.scalar_tensor_tensor(out=slot[:, :, :], in0=slot_row[:, :, :], scalar=float(NU),
                                     in1=slot_col[:, :, :],
                                     op0=ALU.mult, op1=ALU.add).then_inc(slot_ok, 1)
            dve.wait_ge(hid_one, 3)
            unit_step(1, 1, None)
            link(dve.tensor_tensor(big[:, :, :], unit_no[:, :].unsqueeze(2).to_broadcast([P, NU, E]),
                                   ends.unsqueeze(1).to_broadcast([P, NU, E]), ALU.is_ge))
            passed = mB[:, :, :].rearrange("p t e -> p (t e)")[:, 0:NU]
            link(dve.tensor_reduce(passed, big[:, :, :], AX.X, ALU.add))
            link(dve.tensor_scalar(expert_of[:, :], passed, float(E - 1), None, ALU.min))
            link(dve.memset(step_experts[:, :], 0))
            link(dve.tensor_copy(step_experts[:, 1:1 + NU], expert_of[:, :]))
            dve.scalar_tensor_tensor(out=step_experts[:, 4:4 + NU], in0=expert_of[:, :], scalar=float(E),
                                     in1=step_experts[:, 4:4 + NU], op0=ALU.mult, op1=ALU.add).then_inc(eid_ok, 1)
            unit_step(2, 0, None)
            dve.wait_ge(pads_out, 32)
            expert_steps(dve, unit_step, begun=3, weights=(4, E_DVE), weight=weight)

        @block.tensor
        def _(pe):
            PARTS = ((0, 0), (1, 0), (0, 1))

            def product(out, stationary, moving, n):
                last = None
                for k in range(n):
                    for i, (a, b) in enumerate(PARTS):
                        last = pe.matmul(out, stationary(k, a), moving(k, b), start=(k == 0 and i == 0),
                                         stop=(k == n - 1 and i == len(PARTS) - 1))
                return last

            pe.wait_ge(id_ok, 2)
            for c, (kind, j, i) in enumerate(plan):
                cols = slice(j * P, (j + 1) * P)
                bank = ps[:, c % 8, :]
                if c >= 8:
                    pe.wait_ge(pre_dve, c - 7)
                if kind == "C":
                    pe.wait_ge(ctx_in, 16)
                    lo, n = KC[i]
                    for r in range(2):
                        last = pe.transpose(ps[0:n, c % 8, r * P:(r + 1) * P], ctx_sb[:, r, lo:lo + n], ident[:, :])
                elif kind == "W":
                    pe.wait_ge(wq_in, 16)
                    for k in range(KD):
                        last = pe.transpose(bank[:, k * P:(k + 1) * P], wq_sb[:, k, cols], ident[:, :])
                elif kind in "KV":
                    pe.wait_ge(pre_w_lo, w_number[kind, j] + 1)
                    pe.wait_ge(pre_dve, 2)
                    w = (wkh, wkl) if kind == "K" else (wvh, wvl)
                    last = product(bank[:, 0:BK], lambda k, part: w[part][0:KC[k][1], k, cols],
                                   lambda k, part: (ctxTh, ctxTl)[part][0:KC[k][1], k, :], len(KC))
                elif kind == "A":
                    pe.wait_ge(pre_dve, number["K", j, 0] + 1)
                    last = product(bank, lambda _, part: (wqTh, wqTl)[part][:, j % 2, i * P:(i + 1) * P],
                                   lambda _, part: (kTh, kTl)[part][:, j % 2, :, :].rearrange("p r n -> p (r n)"), 1)
                else:
                    pe.wait_ge(pre_w_lo, w_number["O", j] + 1)
                    pe.wait_ge(pre_dve, number["V", j, 0] + 1)
                    for b in range(2):
                        last = product(bank[:, b * D:(b + 1) * D],
                                       lambda _, part: (vTh, vTl)[part][:, j % 2, 2 * i + b, :,
                                                                        :].rearrange("p a n -> p (a n)"),
                                       lambda _, part: (woh, wol)[part][:, j, :], 1)
                last.then_inc(pre_pe, 1)
            pe.wait_ge(pre_act, NPRE)
            pe.wait_ge(pre_dve, NPRE)
            pe.wait_ge(small_in, 96)

            def tile_step(s, par):
                def scores(t, p, g):
                    b = t // TPB
                    return product(ps[:, s_bank(p) + g, :],
                                   lambda k, part: (xTh, xTl)[part][:, p, k * P:(k + 1) * P],
                                   lambda k, part: (Ah, Al)[part][:, bass.ds(b, 1), k, g * BANK:(g + 1) * BANK]
                                   .rearrange("p a n -> p (a n)"), KD)

                t = s - 1
                if has(t, NT):
                    wait(pe, xTl_ok, t + 1)
                    wait(pe, exp_ok, t - 1)
                    scores(t, (par + 1) % 2, 0)
                t = s - 6
                if has(t, NT):
                    p = par
                    wait(pe, xn2T_ok, t + 1)
                    for k in range(KD):
                        last = pe.matmul(ps[:, 0, 0:E], xn2T[:, p, k * P:(k + 1) * P], gateT[:, k, :],
                                         start=(k == 0), stop=(k == KD - 1))
                    last.then_inc(R_ok, 1)
                t = s - 1
                if has(t, NT):
                    scores(t, (par + 1) % 2, 1).then_inc(S_ok, 1)
                t = s
                if has(t, NT):
                    p = par
                    wait(pe, xn_ok, t + 1)
                    wait(pe, xTl_ok, t)
                    wait(pe, lg_ok, t - 5)
                    for k in range(KD):
                        last = pe.transpose(ps[:, 0, k * P:(k + 1) * P], xn[:, p, k * P:(k + 1) * P], ident[:, :])
                    last.then_inc(T_ok, 1)
                t = s - 3
                if has(t, NT):
                    p = (par + 1) % 2
                    wait(pe, norm_ok, t + 1)
                    for h in range(2):
                        wait(pe, pTl_ok, 2 * t + h - 1)
                        for i in range(NJ // 2):
                            j = h * (NJ // 2) + i
                            last = pe.transpose(ps[:, 3 + h, i * P:(i + 1) * P], prob[:, p, j * P:(j + 1) * P],
                                                ident[:, :])
                        last.then_inc(PT_ok, 1)
                t = s - 4
                if has(t, NT):
                    p = par
                    b = t // TPB
                    wait(pe, pTl_ok, 2 * t + 2)
                    wait(pe, x2_ok, t)
                    product(ps[:, 5, 0:D],
                            lambda k, part: (pTh, pTl)[part][:, p, k * P:(k + 1) * P],
                            lambda k, part: (Uh, Ul)[part][:, bass.ds(b, 1), k, :].rearrange("p a d -> p (a d)"),
                            NJ).then_inc(O_ok, 1)
                t = s - 5
                if has(t, NT):
                    p = (par + 1) % 2
                    wait(pe, xn2_ok, t + 1)
                    wait(pe, lg_ok, t)
                    wait(pe, xTl_ok, s + 1 if has(s, NT) else NT)
                    for k in range(KD):
                        last = pe.transpose(ps[:, 0, k * P:(k + 1) * P], xn2[:, p, k * P:(k + 1) * P], ident[:, :])
                    last.then_inc(T2_ok, 1)

            steps(pe, NT, 0, 6, tile_step, per=6)

            def unit_step(s, par, routed):
                def weights(parts, e, k, part, cols):
                    if e is None:
                        return parts[part][:, k, cols]
                    return parts[part][:, bass.ds(e, 1), k, cols].rearrange("p a n -> p (a n)")

                e_uv = e_y = None
                if is_routed(s - 1, routed):
                    if isinstance(s, int) and s - 1 == NT:
                        pe.wait_ge(eid_ok, 1)
                        pe.wait_ge(w_lo, 3 * E_DVE)
                        pe.wait_ge(w_lo_pool, 3 * (E - E_DVE))
                    both = pe.value_load(step_experts[0:1, bass.ds(s - NT, 1)], min_val=0, max_val=E * E - 1)
                    e_uv = both % E
                    if is_routed(s - 4, routed):
                        e_y = both // E

                t = s - 4
                if has(t, NALL):
                    p = par
                    wait(pe, hTl_ok, t + 1)
                    if is_routed(t - 2, routed):
                        wait(pe, y_ok, t - 1 - NT)
                    else:
                        wait(pe, sum_row_ok, t - 1)
                    w2s = (w2h, w2l) if is_routed(t, routed) else (ws2h, ws2l)
                    product(ps[:, 6 + p, 0:D],
                            lambda k, part: (hTh, hTl)[part][:, k * P:(k + 1) * P],
                            lambda k, part: weights(w2s, e_y, k, part, slice(0, D)), KH).then_inc(Y_ok, 1)
                t = s
                if has(t, NALL):
                    p = par
                    if is_routed(t, routed):
                        wait(pe, gather_in[p], before(t - NT) + 16)
                    else:
                        wait(pe, row_in[p], before(t) + 16)
                    wait(pe, uxTl_ok, t)
                    for k in range(KD):
                        last = pe.transpose(ps[:, 0, k * P:(k + 1) * P], xrow[:, p, k * P:(k + 1) * P], ident[:, :])
                    last.then_inc(X_ok, 1)
                t = s - 3
                if has(t, NALL):
                    p = (par + 1) % 2
                    wait(pe, h_ok, t + 1)
                    wait(pe, hTl_ok, t)
                    for k in range(KH):
                        last = pe.transpose(ps[:, 5, k * P:(k + 1) * P], hid[:, p, k * P:(k + 1) * P], ident[:, :])
                    last.then_inc(H_ok, 1)
                t = s - 1
                if has(t, NALL):
                    p = (par + 1) % 2
                    wait(pe, uxTl_ok, t + 1)
                    wait(pe, bias_ok, t - 1)
                    w13 = (w13h, w13l) if is_routed(t, routed) else (ws13h, ws13l)
                    for g in range(2):
                        last = product(ps[:, 1 + 2 * p + g, 0:H],
                                       lambda k, part: (uxTh, uxTl)[part][:, p, k * P:(k + 1) * P],
                                       lambda k, part: weights(w13, e_uv, k, part, slice(g * H, (g + 1) * H)), KD)
                    last.then_inc(UV_ok, 1)

            pe.wait_ge(x2_ok, NT)
            pe.wait_ge(lg_ok, NT)
            unit_step(0, 0, None)
            pe.wait_ge(chosen_ok, 1)
            flat = chosen[:, :, :].rearrange("p t e -> p (t e)")
            pe.matmul(ps[:, 7, 0:NT * E], ones[:, :], flat, start=True, stop=True).then_inc(rank_ok, 1)
            pe.matmul(ps[:, 6, 0:NT * E], tri[:, :], flat, start=True, stop=False, skip_group_check=True)
            for t in range(NT - 1):
                n = NT - 1 - t
                last = pe.matmul(ps[:, 6, (t + 1) * E:NT * E], ones[:, :],
                                 chosen[:, t:t + 1, :].to_broadcast([P, n, E]), start=False, stop=(t == NT - 2),
                                 skip_group_check=True)
            last.then_inc(rank_ok, 1)

            pe.wait_ge(sw_lo, 2)
            expert_steps(pe, unit_step, begun=1)


_INS = ['x', 'ctx_768', 'L0_xattn_Wq', 'L0_xattn_Wk', 'L0_xattn_Wv', 'L0_xattn_Wo', 'L0_xattn_bo',
        'L0_ffn_gate_w', 'L0_ffn_gate_b', 'L0_ffn_w1', 'L0_ffn_b1', 'L0_ffn_w3', 'L0_ffn_b3', 'L0_ffn_w2', 'L0_ffn_b2',
        'L0_ffn_sw1', 'L0_ffn_sb1', 'L0_ffn_sw3', 'L0_ffn_sb3', 'L0_ffn_sw2', 'L0_ffn_sb2']


def kernel(**inputs):
    import numpy as _np
    import concourse.bacc as _bacc
    from concourse import mybir as _mybir
    from concourse.bass_utils import run_bass_kernel_spmd as _run

    nc = _bacc.Bacc("TRN2", target_bir_lowering=False, num_devices=1)
    arrays, args = {}, []
    for name in _INS:
        a = _np.ascontiguousarray(inputs[name])
        arrays[f"in_{name}"] = a
        args.append(nc.dram_tensor(f"in_{name}", a.shape, _mybir.dt.from_np(a.dtype), kind="ExternalInput").ap())
    b, n, d = inputs['x'].shape
    out = nc.dram_tensor("out_x", (b * n + PADS, d), _mybir.dt.float32, kind="ExternalOutput")
    xattn_moe(nc, *args, out.ap())
    r = _run(nc, [arrays], core_ids=[0])
    return r.results[0]["out_x"][:b * n].reshape(b, n, d)
```
